# Optimizing a Trainium2 kernel written in Bass

```python
import numpy as np
import jax
import jax.numpy as jnp

def _softmax(x, axis=-1):
    return jax.nn.softmax(x, axis=axis)

def _gelu(x):
    return jax.nn.gelu(x, approximate=True)

def _silu(x):
    return jax.nn.silu(x)

def _sigmoid(x):
    return jax.nn.sigmoid(x)

def _layernorm(x, axis=-1, eps=1e-05):
    m = jnp.mean(x, axis=axis, keepdims=True)
    v = jnp.var(x, axis=axis, keepdims=True)
    return (x - m) / jnp.sqrt(v + eps)

def _scatter_add(tgt, idx, src, axis=0):
    return tgt.at[idx].add(src)

def _segment_sum(src, seg, n):
    return jax.ops.segment_sum(src, seg, n)
kernel_name = 'mk_flamingo_gated_d2_seqx_r8_3b70f5'

def setup_inputs(seed: int=0):
    np.random.seed(seed)
    _w = jnp.asarray

    def _rec_inputs():
        import jax
        import jax.numpy as jnp
        _rk = jax.random.key(seed)
        x = -0.0002928 + 1 * jax.random.normal(jax.random.fold_in(_rk, 1), (32, 128, 128), jnp.float32)
        _lenS = 128 - jax.random.randint(jax.random.fold_in(_rk, 7), (32,), 0, max(1, 128 // 4) + 1, jnp.int32)
        _lenS2 = 128 - jax.random.randint(jax.random.fold_in(_rk, 8), (32,), 0, max(1, 128 // 4) + 1, jnp.int32)
        _ctx_1024P = jax.random.normal(jax.random.fold_in(_rk, 11), (32, 16, 128), jnp.float32)
        _ctx_1024c = jax.random.dirichlet(jax.random.fold_in(_rk, 511), 0.3 * jnp.ones((16,), jnp.float32), (32, 128))
        _ctx_1024t = jnp.einsum('bsk,bkd->bsd', _ctx_1024c, _ctx_1024P)
        _ctx_1024t = _ctx_1024t * jax.lax.rsqrt(jnp.mean(jnp.square(_ctx_1024t)) + 1e-12) * 0.953939
        ctx_1024 = -1.39393e-06 + 0.999914 * (_ctx_1024t + 0.3 * jax.random.normal(jax.random.fold_in(_rk, 611), (32, 128, 128), jnp.float32))
        _g = jax.random.normal(jax.random.fold_in(_rk, 9001), (2, 2), jnp.float32)
        _g = jnp.sign(_g) * jnp.maximum(jnp.abs(_g), 1.0) + (_g == 0) * 1.0
        g_xattn = _g[0]
        g_ffn = _g[1]
        return (x, ctx_1024, g_xattn, g_ffn)
    x, ctx_1024, g_xattn, g_ffn = _rec_inputs()

    def _L0_xattn_setup():
        import jax, jax.numpy as jnp
        import numpy as np
        B, S, DIM, NH = (2, 256, 128, 8)
        DH = DIM // NH
        GATE_SOFT_CAP = 15.0
        BACKEND_EPS = 5e-05
        NORM_EPS = 1e-06

        def _mlstm_parallel(q, k, v, i_pre, f_pre):
            log_fg = jax.nn.log_sigmoid(f_pre)
            lf_cs = jnp.cumsum(log_fg, axis=-1)
            lf = jnp.concatenate([jnp.zeros_like(lf_cs[..., :1]), lf_cs], axis=-1)
            log_d = lf[..., 1:, None] - lf[..., None, 1:] + i_pre[..., None, :]
            t_idx = jnp.arange(q.shape[2])
            mask = t_idx[:, None] >= t_idx[None, :]
            log_d = jnp.where(mask, log_d, -jnp.inf)
            m = jnp.max(log_d, axis=-1, keepdims=True)
            d_mat = jnp.exp(log_d - m)
            scores = jnp.einsum('bhtd,bhsd->bhts', q, k) * (1.0 / np.sqrt(DH))
            s_mat = scores * d_mat
            denom = jnp.maximum(jnp.abs(jnp.sum(s_mat, axis=-1, keepdims=True)), jnp.exp(-m)) + BACKEND_EPS
            return jnp.einsum('bhts,bhsd->bhtd', s_mat, v) / denom
        key = jax.random.key(seed)
        kq, kk, kv, kw = jax.random.split(key, 4)
        q = jax.random.normal(kq, (B, S, DIM), dtype=jnp.float32)
        k = jax.random.normal(kk, (B, S, DIM), dtype=jnp.float32)
        v = jax.random.normal(kv, (B, S, DIM), dtype=jnp.float32)
        ifgate_w = 0.02 * jax.random.normal(kw, (2 * NH, 3 * DIM), dtype=jnp.float32)
        ifgate_b = jnp.concatenate([jnp.full((NH,), -10.0, dtype=jnp.float32), jnp.linspace(3.0, 6.0, NH, dtype=jnp.float32)])
        outnorm_w = jnp.zeros((DIM,), dtype=jnp.float32)
        return {'q': q, 'k': k, 'v': v, 'ifgate_w': ifgate_w, 'ifgate_b': ifgate_b, 'outnorm_w': outnorm_w}
    _L0_xattn_all = _L0_xattn_setup()
    _L0_xattn_in = {k: v for k, v in _L0_xattn_all.items() if k in ('ifgate_w', 'ifgate_b', 'outnorm_w')}
    del _L0_xattn_all

    def _L0_ffn_setup():
        import jax, jax.numpy as jnp
        import numpy as np
        QMIN, QMAX = (-128.0, 127.0)

        def _affine_quantize(x):
            amin, amax = (jnp.min(x), jnp.max(x))
            scale = jnp.maximum((amax - amin) / 255.0, 1e-08)
            zp = jnp.clip(jnp.round(-amin / scale) + QMIN, QMIN, QMAX)
            q = jnp.clip(jnp.round(x / scale) + zp, QMIN, QMAX)
            return (q, scale, zp)

        def _sym_quantize(w):
            scale = jnp.maximum(jnp.max(jnp.abs(w)) / 127.0, 1e-08)
            q = jnp.clip(jnp.round(w / scale), -127.0, 127.0)
            return (q, scale)

        def _qlinear(x, W, b):
            xq, sx, zx = _affine_quantize(x)
            wq, sw = _sym_quantize(W)
            acc = jnp.einsum('bsh,oh->bso', xq - zx, wq)
            return acc * (sx * sw) + b
        key = jax.random.key(seed)
        k1, k2, k3, k4, k5 = jax.random.split(key, 5)
        d, h = (128, 512)
        x = jax.random.normal(k1, (4, 512, d), dtype=jnp.float32)
        W1 = jax.random.normal(k2, (h, d), dtype=jnp.float32) * (1.0 / np.sqrt(d))
        b1 = jax.random.normal(k3, (h,), dtype=jnp.float32) * 0.02
        W2 = jax.random.normal(k4, (d, h), dtype=jnp.float32) * (1.0 / np.sqrt(h))
        b2 = jax.random.normal(k5, (d,), dtype=jnp.float32) * 0.02
        return {'x': x, 'W1': W1, 'b1': b1, 'W2': W2, 'b2': b2}
    _L0_ffn_all = _L0_ffn_setup()
    _L0_ffn_in = {k: v for k, v in _L0_ffn_all.items() if k in ('W1', 'b1', 'W2', 'b2')}
    del _L0_ffn_all

    def _L1_xattn_setup():
        import jax, jax.numpy as jnp
        import numpy as np
        from jax import lax
        BIG = jnp.float32(1e+30)

        def _pairwise_euclidean(a, b):
            aa = jnp.sum(a * a, axis=-1)[:, None]
            bb = jnp.sum(b * b, axis=-1)[None, :]
            ab = a @ b.T
            return jnp.sqrt(jnp.maximum(aa + bb - 2.0 * ab, 0.0))

        def _dtw_cost(D):
            row0 = jnp.cumsum(D[0])

            def row_step(prev_row, d_row):
                first = d_row[0] + prev_row[0]

                def col_step(left, inp):
                    d_ij, up, diag = inp
                    r = d_ij + jnp.minimum(jnp.minimum(up, left), diag)
                    return (r, r)
                _, rest = lax.scan(col_step, first, (d_row[1:], prev_row[1:], prev_row[:-1]))
                row = jnp.concatenate([first[None], rest])
                return (row, row)
            _, rows = lax.scan(row_step, row0, D[1:])
            return jnp.concatenate([row0[None], rows], axis=0)

        def _backtrack(R, T1, T2):
            L = T1 + T2 - 1

            def step(carry, _):
                i, j, done = carry
                valid = jnp.logical_not(done)
                cd = jnp.where((i > 0) & (j > 0), R[jnp.maximum(i - 1, 0), jnp.maximum(j - 1, 0)], BIG)
                cu = jnp.where(i > 0, R[jnp.maximum(i - 1, 0), j], BIG)
                cl = jnp.where(j > 0, R[i, jnp.maximum(j - 1, 0)], BIG)
                choice = jnp.argmin(jnp.stack([cd, cu, cl]))
                ni = jnp.where(choice <= 1, i - 1, i)
                nj = jnp.where((choice == 0) | (choice == 2), j - 1, j)
                at_origin = (i == 0) & (j == 0)
                ni = jnp.where(at_origin, 0, ni)
                nj = jnp.where(at_origin, 0, nj)
                return ((ni, nj, done | at_origin), (i, j, valid))
            init = (jnp.int32(T1 - 1), jnp.int32(T2 - 1), jnp.bool_(False))
            _, (i_idx, j_idx, valid) = lax.scan(step, init, None, length=L)
            return (i_idx, j_idx, valid)

        def _align_one(small, large):
            T_small, d = small.shape
            T_large = large.shape[0]
            D = _pairwise_euclidean(small, large)
            R = _dtw_cost(D)
            i_idx, j_idx, valid = _backtrack(R, T_small, T_large)
            contrib = small[i_idx] * valid[:, None].astype(small.dtype)
            expanded = jnp.zeros((T_large, d), dtype=small.dtype).at[j_idx].add(contrib)
            return expanded
        key = jax.random.key(seed)
        k1, k2 = jax.random.split(key)
        teacher = jax.random.normal(k1, (16, 50, 128), dtype=jnp.float32)
        student = jax.random.normal(k2, (16, 75, 128), dtype=jnp.float32)
        return {'teacher_features': teacher, 'student_features': student}
    _L1_xattn_all = _L1_xattn_setup()
    _L1_xattn_in = {k: v for k, v in _L1_xattn_all.items() if k in ()}
    del _L1_xattn_all

    def _L1_ffn_setup():
        import jax, jax.numpy as jnp
        import numpy as np
        B, L, D = (4, 128, 128)
        E, H = (8, 512)
        CAPACITY = 6
        key = jax.random.key(seed)
        ks = jax.random.split(key, 6)
        x = jax.random.normal(ks[0], (B, L, D), dtype=jnp.float32)
        gate_weight = jax.random.normal(ks[1], (E, D), dtype=jnp.float32) * 0.006
        w1 = jax.random.normal(ks[2], (E, H, D), dtype=jnp.float32) * 0.02
        b1 = jnp.zeros((E, H), dtype=jnp.float32)
        w2 = jax.random.normal(ks[3], (E, D, H), dtype=jnp.float32) * 0.02
        b2 = jnp.zeros((E, D), dtype=jnp.float32)
        return {'x': x, 'gate_weight': gate_weight, 'w1': w1, 'b1': b1, 'w2': w2, 'b2': b2}
    _L1_ffn_all = _L1_ffn_setup()
    _L1_ffn_in = {k: v for k, v in _L1_ffn_all.items() if k in ('gate_weight', 'w1', 'b1', 'w2', 'b2')}
    del _L1_ffn_all
    return {'x': x, 'ctx_1024': ctx_1024, 'g_xattn': g_xattn, 'g_ffn': g_ffn, 'L0_xattn_ifgate_w': _L0_xattn_in['ifgate_w'], 'L0_xattn_ifgate_b': _L0_xattn_in['ifgate_b'], 'L0_xattn_outnorm_w': _L0_xattn_in['outnorm_w'], 'L0_ffn_W1': _L0_ffn_in['W1'], 'L0_ffn_b1': _L0_ffn_in['b1'], 'L0_ffn_W2': _L0_ffn_in['W2'], 'L0_ffn_b2': _L0_ffn_in['b2'], 'L1_ffn_gate_weight': _L1_ffn_in['gate_weight'], 'L1_ffn_w1': _L1_ffn_in['w1'], 'L1_ffn_b1': _L1_ffn_in['b1'], 'L1_ffn_w2': _L1_ffn_in['w2'], 'L1_ffn_b2': _L1_ffn_in['b2']}

def reference(x, ctx_1024, g_xattn, g_ffn, L0_xattn_ifgate_w, L0_xattn_ifgate_b, L0_xattn_outnorm_w, L0_ffn_W1, L0_ffn_b1, L0_ffn_W2, L0_ffn_b2, L1_ffn_gate_weight, L1_ffn_w1, L1_ffn_b1, L1_ffn_w2, L1_ffn_b2):
    import jax
    import jax.numpy as jnp

    def _L0_xattn_ref(q, k, v, ifgate_w, ifgate_b, outnorm_w):
        import jax, jax.numpy as jnp
        import numpy as np
        B, S, DIM, NH = (2, 256, 128, 8)
        DH = DIM // NH
        GATE_SOFT_CAP = 15.0
        BACKEND_EPS = 5e-05
        NORM_EPS = 1e-06

        def _mlstm_parallel(q, k, v, i_pre, f_pre):
            log_fg = jax.nn.log_sigmoid(f_pre)
            lf_cs = jnp.cumsum(log_fg, axis=-1)
            lf = jnp.concatenate([jnp.zeros_like(lf_cs[..., :1]), lf_cs], axis=-1)
            log_d = lf[..., 1:, None] - lf[..., None, 1:] + i_pre[..., None, :]
            t_idx = jnp.arange(q.shape[2])
            mask = t_idx[:, None] >= t_idx[None, :]
            log_d = jnp.where(mask, log_d, -jnp.inf)
            m = jnp.max(log_d, axis=-1, keepdims=True)
            d_mat = jnp.exp(log_d - m)
            scores = jnp.einsum('bhtd,bhsd->bhts', q, k) * (1.0 / np.sqrt(DH))
            s_mat = scores * d_mat
            denom = jnp.maximum(jnp.abs(jnp.sum(s_mat, axis=-1, keepdims=True)), jnp.exp(-m)) + BACKEND_EPS
            return jnp.einsum('bhts,bhsd->bhtd', s_mat, v) / denom
        b, s, dim = q.shape
        gate_in = jnp.concatenate([q, k, v], axis=-1)
        pre = gate_in @ ifgate_w.T + ifgate_b
        pre = GATE_SOFT_CAP * jnp.tanh(pre / GATE_SOFT_CAP)
        i_pre = pre[..., :NH].transpose(0, 2, 1)
        f_pre = pre[..., NH:].transpose(0, 2, 1)
        qh = q.reshape(b, s, NH, DH).transpose(0, 2, 1, 3)
        kh = k.reshape(b, s, NH, DH).transpose(0, 2, 1, 3)
        vh = v.reshape(b, s, NH, DH).transpose(0, 2, 1, 3)
        h = _mlstm_parallel(qh, kh, vh, i_pre, f_pre)
        rrms = jax.lax.rsqrt(jnp.mean(h * h, axis=-1, keepdims=True) + NORM_EPS)
        gain = (1.0 + outnorm_w).reshape(1, NH, 1, DH)
        h = h * rrms * gain
        return h.transpose(0, 2, 1, 3).reshape(b, s, dim)

    def _L0_ffn_ref(x, W1, b1, W2, b2):
        import jax, jax.numpy as jnp
        import numpy as np
        QMIN, QMAX = (-128.0, 127.0)

        def _affine_quantize(x):
            amin, amax = (jnp.min(x), jnp.max(x))
            scale = jnp.maximum((amax - amin) / 255.0, 1e-08)
            zp = jnp.clip(jnp.round(-amin / scale) + QMIN, QMIN, QMAX)
            q = jnp.clip(jnp.round(x / scale) + zp, QMIN, QMAX)
            return (q, scale, zp)

        def _sym_quantize(w):
            scale = jnp.maximum(jnp.max(jnp.abs(w)) / 127.0, 1e-08)
            q = jnp.clip(jnp.round(w / scale), -127.0, 127.0)
            return (q, scale)

        def _qlinear(x, W, b):
            xq, sx, zx = _affine_quantize(x)
            wq, sw = _sym_quantize(W)
            acc = jnp.einsum('bsh,oh->bso', xq - zx, wq)
            return acc * (sx * sw) + b
        h = _qlinear(x, W1, b1)
        h = jax.nn.gelu(h, approximate=False)
        out = _qlinear(h, W2, b2)
        return out

    def _L1_xattn_ref(teacher_features, student_features):
        import jax, jax.numpy as jnp
        import numpy as np
        from jax import lax
        BIG = jnp.float32(1e+30)

        def _pairwise_euclidean(a, b):
            aa = jnp.sum(a * a, axis=-1)[:, None]
            bb = jnp.sum(b * b, axis=-1)[None, :]
            ab = a @ b.T
            return jnp.sqrt(jnp.maximum(aa + bb - 2.0 * ab, 0.0))

        def _dtw_cost(D):
            row0 = jnp.cumsum(D[0])

            def row_step(prev_row, d_row):
                first = d_row[0] + prev_row[0]

                def col_step(left, inp):
                    d_ij, up, diag = inp
                    r = d_ij + jnp.minimum(jnp.minimum(up, left), diag)
                    return (r, r)
                _, rest = lax.scan(col_step, first, (d_row[1:], prev_row[1:], prev_row[:-1]))
                row = jnp.concatenate([first[None], rest])
                return (row, row)
            _, rows = lax.scan(row_step, row0, D[1:])
            return jnp.concatenate([row0[None], rows], axis=0)

        def _backtrack(R, T1, T2):
            L = T1 + T2 - 1

            def step(carry, _):
                i, j, done = carry
                valid = jnp.logical_not(done)
                cd = jnp.where((i > 0) & (j > 0), R[jnp.maximum(i - 1, 0), jnp.maximum(j - 1, 0)], BIG)
                cu = jnp.where(i > 0, R[jnp.maximum(i - 1, 0), j], BIG)
                cl = jnp.where(j > 0, R[i, jnp.maximum(j - 1, 0)], BIG)
                choice = jnp.argmin(jnp.stack([cd, cu, cl]))
                ni = jnp.where(choice <= 1, i - 1, i)
                nj = jnp.where((choice == 0) | (choice == 2), j - 1, j)
                at_origin = (i == 0) & (j == 0)
                ni = jnp.where(at_origin, 0, ni)
                nj = jnp.where(at_origin, 0, nj)
                return ((ni, nj, done | at_origin), (i, j, valid))
            init = (jnp.int32(T1 - 1), jnp.int32(T2 - 1), jnp.bool_(False))
            _, (i_idx, j_idx, valid) = lax.scan(step, init, None, length=L)
            return (i_idx, j_idx, valid)

        def _align_one(small, large):
            T_small, d = small.shape
            T_large = large.shape[0]
            D = _pairwise_euclidean(small, large)
            R = _dtw_cost(D)
            i_idx, j_idx, valid = _backtrack(R, T_small, T_large)
            contrib = small[i_idx] * valid[:, None].astype(small.dtype)
            expanded = jnp.zeros((T_large, d), dtype=small.dtype).at[j_idx].add(contrib)
            return expanded
        return jax.vmap(_align_one)(teacher_features, student_features)

    def _L1_ffn_ref(x, gate_weight, w1, b1, w2, b2):
        import jax, jax.numpy as jnp
        import numpy as np
        B, L, D = (4, 128, 128)
        E, H = (8, 512)
        CAPACITY = 6
        logits = jnp.einsum('bld,ed->ble', x, gate_weight)
        expert_k = B * L * CAPACITY
        kth_val = jnp.sort(logits.reshape(-1))[expert_k - 1]
        mask = (logits >= kth_val).astype(x.dtype)
        gates = logits * mask
        h = jax.nn.gelu(jnp.einsum('bld,ehd->bleh', x, w1) + b1, approximate=True)
        y = jnp.einsum('bleh,edh->blde', h, w2) + b2.T[None, None]
        out = jnp.einsum('blde,ble->bld', y, gates)
        return out
    x = x + jnp.tanh(g_xattn[0]) * _L0_xattn_ref(_layernorm(x, axis=-1), ctx_1024, ctx_1024, L0_xattn_ifgate_w, L0_xattn_ifgate_b, L0_xattn_outnorm_w)
    x = x + jnp.tanh(g_ffn[0]) * _L0_ffn_ref(_layernorm(x, axis=-1), L0_ffn_W1, L0_ffn_b1, L0_ffn_W2, L0_ffn_b2)
    x = x + jnp.tanh(g_xattn[1]) * _L1_xattn_ref(ctx_1024, _layernorm(x, axis=-1))
    x = x + jnp.tanh(g_ffn[1]) * _L1_ffn_ref(_layernorm(x, axis=-1), L1_ffn_gate_weight, L1_ffn_w1, L1_ffn_b1, L1_ffn_w2, L1_ffn_b2)
    return x

_drawn_inputs = setup_inputs


def setup_inputs(seed=0):
    import zlib

    import numpy as np

    out = dict(_drawn_inputs(seed))
    spreads = {'g_ffn': (-1.0, 0.6),
     'L0_xattn_outnorm_w': (0.0, 0.1),
     'L1_ffn_b1': (0.0, 0.8),
     'L1_ffn_b2': (0.0, 0.8)}
    factors = {'L0_ffn_b1': 7.481,
     'L0_ffn_b2': 6.645,
     'L1_ffn_gate_weight': 6.335,
     'L1_ffn_w1': 8.0,
     'L1_ffn_w2': 8.0}
    for name, (base, spread) in spreads.items():
        noise = np.random.default_rng([zlib.crc32(name.encode()), seed]).standard_normal(out[name].shape)
        drawn = base * np.exp(spread * noise) if base else spread * noise
        out[name] = jnp.asarray(drawn.astype(out[name].dtype))
    for name, factor in factors.items():
        out[name] = (out[name] * factor).astype(out[name].dtype)
    return out
```

```python
from contextlib import ExitStack

import concourse.bass as bass
import concourse.mybir as mybir

F32 = mybir.dt.float32
BF16 = mybir.dt.bfloat16
I32 = mybir.dt.int32
ALU = mybir.AluOpType
ACT = mybir.ActivationFunctionType
AX = mybir.AxisListType.X

P = 128
B = 32
D = 128
NH, DH = 8, 16
HID = 512
NC = HID // P
E = 8
G4 = B // 4
TOK = B * P
KTH = 4 * 128 * 6
MAGIC = 12582912.0
BIG = 1e30
LN_EPS, NORM_EPS, BACKEND_EPS = 1e-5, 1e-6, 5e-5
GATE_CAP = 15.0
VW = DH + 1
RC = 32
NRC = P // RC
RW = P + 1


def program(nc, x, ctx_, g_x, g_f, if_w, if_b, on_w, a_w1, a_b1, a_w2, a_b2, gate_w, m_w1, m_b1, m_w2, m_b2, out):
    with ExitStack() as stack:
        def sb(name, shape, dt=F32):
            return stack.enter_context(nc.sbuf_tensor(name, shape, dt))

        def sem(name):
            return stack.enter_context(nc.semaphore(name))

        def dram(name, shape, dt):
            return nc.dram_tensor(name, shape, dt)

        xs = sb("xs", [P, B, D])
        cs = sb("cs", [P, B, D])
        xn_w1 = sb("xn_w1", [P, B * D])
        kT_w2 = sb("kT_w2", [P, B * D])
        A = sb("A", [P, 16384])
        Bm = sb("Bm", [P, 14848])
        slab = sb("slab", [P, 2048])
        slab2 = sb("slab2", [P, 512])
        PS = stack.enter_context(nc.psum_tensor("PS", [P, 8, 512], F32))

        xn = xn_w1[:].rearrange("p (b d) -> p b d", b=B)
        kT = kT_w2

        qT = A[:, 0:4096]
        bmask = A[:, 8192:10240].bitcast(BF16).rearrange("p (k h t) -> p k h t", k=4, h=NH)
        av = A[:, 10240:12288].rearrange("p (w g t) -> p w g t", w=2, g=G4)
        av_res = A[:, 12288:14336].rearrange("p (w g t) -> p w g t", w=2, g=G4)
        av_cut = A[:, 14336:15360].bitcast(BF16).rearrange("p (w g t) -> p w g t", w=2, g=G4)
        av_part = A[:, 15360:16384].bitcast(BF16).rearrange("p (w g t) -> p w g t", w=2, g=G4)
        vaug = Bm[:, 0:4352].rearrange("p (b w) -> p b w", b=B)
        oall = Bm[:, 4352:8704].rearrange("p (b w) -> p b w", b=B)
        decay = Bm[:, 8704:9728].rearrange("p (s c) -> p s c", s=2)
        smat = Bm[:, 9728:10752].rearrange("p (s c) -> p s c", s=2)
        mblk = Bm[:, 10752:14848].bitcast(BF16).rearrange("p (g h t) -> p g h t", g=G4, h=NH)
        osq = A[:, 0:4096]
        hid = A[:, 0:16384].rearrange("p (c t) -> p c t", c=NC)
        hq = Bm[:, 0:8192].bitcast(BF16).rearrange("p (c t) -> p c t", c=NC)
        xq = Bm[:, 8192:10240].bitcast(BF16)
        xqT = Bm[:, 10240:12288].bitcast(BF16)
        xT2 = Bm[:, 0:1024].rearrange("p (s t) -> p s t", s=2)
        xTsq = Bm[:, 1024:2048].rearrange("p (s t) -> p s t", s=2)
        dsq = Bm[:, 2048:6144].rearrange("p (b j) -> p b j", b=B)
        dist = Bm[:, 6144:10240].rearrange("p (b j) -> p b j", b=B)
        dring = A[:, 0:8192].rearrange("p (s r j) -> p s r j", s=2, r=RC)
        kb = A[:, 8192:16384].bitcast(BF16).rearrange("p (i j) -> p i j", i=P)
        rring = Bm[:, 0:2 * (RC + 1) * RW].rearrange("p (s r j) -> p s r j", s=2, r=RC + 1)
        o0 = 2 * (RC + 1) * RW
        r9 = Bm[:, o0:o0 + 9 * RW].rearrange("p (r j) -> p r j", r=9)
        o0 += 9 * RW
        ch_m = Bm[:, o0:o0 + 1024].rearrange("p (r j) -> p r j", r=8)
        ch_g = Bm[:, o0 + 1024:o0 + 2048].rearrange("p (r j) -> p r j", r=8)
        ch_k = Bm[:, o0 + 2048:o0 + 3072].rearrange("p (r j) -> p r j", r=8)
        ch_s = Bm[:, o0 + 3072:o0 + 4096].rearrange("p (r j) -> p r j", r=8)
        o0 += 4096
        ch_d = Bm[:, o0:o0 + 512].bitcast(BF16).rearrange("p (r j) -> p r j", r=8)
        scanmask = Bm[:, o0 + 512:o0 + 1024].bitcast(BF16).rearrange("p (r j) -> p r j", r=8)
        path = Bm[:, 0:4096].rearrange("p (b j) -> p b j", b=B)
        x4 = A[:, 0:4096].rearrange("p (b d) -> p b d", b=B)
        x4h = A[:, 4096:6144].bitcast(BF16)
        x4l = A[:, 6144:8192].bitcast(BF16)
        x4f = A[:, 8192:9216].rearrange("p (s t) -> p s t", s=2)
        hf = A[:, 9216:11264].rearrange("p (s t) -> p s t", s=4)
        hh = A[:, 11264:13312].bitcast(BF16).rearrange("p (s c t) -> p s c t", s=2, c=NC)
        hl = A[:, 13312:15360].bitcast(BF16).rearrange("p (s c t) -> p s c t", s=2, c=NC)
        w1h = xn_w1[:, 0:2048].bitcast(BF16).rearrange("p (e c t) -> p e c t", e=E, c=NC)
        w1l = xn_w1[:, 2048:4096].bitcast(BF16).rearrange("p (e c t) -> p e c t", e=E, c=NC)
        w2h = kT_w2[:, 0:2048].bitcast(BF16).rearrange("p (e c t) -> p e c t", e=E, c=NC)
        w2l = kT_w2[:, 2048:4096].bitcast(BF16).rearrange("p (e c t) -> p e c t", e=E, c=NC)

        identf = sb("identf", [P, P])
        identb = sb("identb", [P, P], BF16)
        tri = sb("tri", [P, P])
        neg = sb("neg", [P, P], BF16)
        iota2 = sb("iota2", [P, P])
        ones = sb("ones", [P, P])
        selb = slab2[:, 0:256].bitcast(BF16).rearrange("p (k t) -> p k t", k=4)
        pidx = sb("pidx", [P, 8], I32)
        hidx = sb("hidx", [P, 8], I32)
        hidf = sb("hidf", [P, 8])
        pm = sb("pm", [P, 16])
        hneg = sb("hneg", [P, 8])
        hpos = sb("hpos", [P, 8])
        cst = sb("cst", [P, 8])
        bns = sb("bns", [P, B, 6])
        lnt = sb("lnt", [P, 8, B])
        ifw_n = Bm[0:16, 8704:9088]
        ifb_b = sb("ifb_b", [P, 16])
        onw_b = sb("onw_b", [P, D])
        tgr = sb("tgr", [P, 4])
        tg = sb("tg", [P, 4])
        ab1_n = Bm[0:NC, 9088:9216]
        ab2_b = sb("ab2_b", [P, D])
        gw_n = Bm[0:E, 9216:9344]
        mb1_n = Bm[0:E * NC, 9344:9472]
        b2blk = sb("b2blk", [32, 4, D])
        small_t = sb("small_t", [P, 92])
        wkv = sb("wkv", [P, 16])
        pre = slab[:, 0:512].rearrange("p (b w) -> p b w", b=B)
        nlf = slab[:, 512:768].rearrange("p (b h) -> p b h", b=B)
        a_tok = slab[:, 768:1024].rearrange("p (b h) -> p b h", b=B)
        ncs = slab[:, 1024:1280].rearrange("p (b h) -> p b h", b=B)
        expnm = sb("expnm", [P, B, NH])
        fin = slab[:, 1280:2048].rearrange("p (k m) -> p k m", k=3)
        kslot = slab2[:, 256:512].rearrange("p (s t) -> p s t", s=2)
        qslot = slab[:, 0:512].rearrange("p (s r t) -> p s r t", s=2, r=2)
        mm = sb("mm", [P, 24])
        gq = sb("gq", [2, 8])
        qs = sb("qs", [P, 40])
        wtmp = Bm[:, 12288:13312]
        w1n = Bm[:, 13312:13824]
        w2n = Bm[:, 13824:14336]
        wqb = Bm[:, 14336:14848].bitcast(BF16)
        w1q = slab2[:, 0:256].bitcast(BF16)
        w2q = slab2[:, 256:512].bitcast(BF16).rearrange("p (c d) -> p c d", c=NC)
        aa = sb("aa", [P, B])
        ee = sb("ee", [B, P + 4])
        rowm = sb("rowm", [B, P])
        pathm = Bm[:, 4096:8192].rearrange("p (b j) -> p b j", b=B)
        hmm = sb("hmm", [P, 2, B])
        selw = A[:, 16128:16256].bitcast(BF16)
        eT = sb("eT", [P, 2, B])
        aa_tmp = Bm[:, 10752:14848].rearrange("p (b d) -> p b d", b=B)
        wraw = slab[:, 0:1024].rearrange("p (s c) -> p s c", s=2)
        wcp = slab[:, 1024:2048].rearrange("p (s c) -> p s c", s=2)
        lg = A[:, 15360:15616].rearrange("p (b e) -> p b e", b=B)
        gts = A[:, 15616:15872].rearrange("p (b e) -> p b e", b=B)
        gtT = A[0:32, 15872:16128].rearrange("p (s t) -> p s t", s=2)
        sel = sb("sel", [P, 16])
        seli = sb("seli", [P, 8], I32)

        d_dram = dram("d_scratch", (B, P, P), F32).ap()
        r_dram = dram("r_scratch", (B, RW, RW), F32).ap()
        k_dram = dram("k_scratch", (B, P, P), BF16).ap()


        S = {n: sem(n) for n in (
            "pool_step", "dve_step", "act_step",
            "consts_made", "small_in", "b2_in", "small_turned", "small_kept", "tg_in_ready", "tg_ready",
            "csq_done", "bn_done", "ln_sqrt", "ln_done", "q_turned", "c_turned", "q_kept", "k_kept",
            "gates_summed", "gates_biased", "gates_capped", "nlf_ready", "cumsum_done", "a_ready", "a_turned",
            "m_ready", "m_turned", "m_tok_ready", "expnm_ready", "parts_ready", "mblk_ready", "vaug_ready",
            "kslot_ready", "qslot_ready", "ld_ready", "sc_ready", "exp_done", "prod_done", "av_done", "o_kept",
            "osq_done", "osum_done", "osqrt_done",
            "mm_ready", "mm_turned", "mm_global", "mm_spread", "scale_ready", "x_scaled", "xq_ready",
            "xq_turned", "xqT_kept", "aw_in", "w_scaled", "wq_ready", "wq_turned", "wq_kept",
            "ffn1_done", "gelu_done", "h_scaled", "hq_ready", "b2_added", "ffn2_done", "ffn2_added",
            "x3T_turned", "x3T_kept", "dsum_done", "dsq_ready", "dist_ready", "d_out", "row_done",
            "r_out", "r9_in", "left_ready", "k_made", "k_cut", "k_out", "k_in",
            "track_done", "e_turned", "e_kept", "path_ready", "expanded", "expanded_added",
            "raw_turned", "raw_kept", "w_split",
            "x4_turned", "x4_kept", "x4_split", "logits_done", "count_ready", "count_all", "gates_ready",
            "gt_turned", "gt_kept", "gb_done", "gb_added", "h_ready", "h_gelu", "h_high", "h_low_even", "h_low_odd", "y_ready",
            "y_added", "stored")}
        x_in = [sem(f"x_in{c}") for c in range(4)]
        ctx_in = [sem(f"ctx_in{c}") for c in range(4)]
        d_in = [sem(f"d_in{c}") for c in range(2)]
        raw_in = [sem(f"raw_in{c}") for c in range(2)]

        def bank(n, a=0, b=512):
            return PS[:, n, a:b]

        def bankb(n):
            return PS[:, n, 0:256].bitcast(BF16)

        def g4(ap, g):
            return ap[:, 4 * g:4 * g + 4]

        def four(ap):
            return ap.rearrange("p (k t) -> p k t", k=4)

        def rep(ap, n):
            return ap.unsqueeze(1).to_broadcast([ap.shape[0], n, ap.shape[1]])

        def last(ap, n):
            return ap.unsqueeze(2).to_broadcast([ap.shape[0], ap.shape[1], n])

        def raw_load(pool, n):
            if n < E:
                dst, src = four(wraw[:, n % 2, :]), m_w1[n].rearrange("(c p) d -> p c d", c=NC)
            else:
                dst, src = wraw[:, n % 2, :], m_w2[n - E]
            pool.dma_start(dst, src).then_inc(raw_in[n % 2], 16)

        def steps_out(sp, c):
            sp.wait_ge(S["k_cut"], c + 1)
            for q in range(4):
                sp.dma_start(k_dram[:, RC * c + 8 * q:RC * c + 8 * q + 8], ch_d[32 * q:32 * q + 32]).then_inc(S["k_out"], 16)
            sp.wait_ge(S["k_out"], 64 * (c + 1))
            sp.dma_start(kb[0:B, RC * c:RC * c + RC], k_dram[:, RC * c:RC * c + RC]).then_inc(S["k_in"], 16)

        def back_steps(dve, link, c):
            dve.wait_ge(S["r9_in"], 64 * (c + 1))
            if c >= 1:
                dve.wait_ge(S["k_made"], c)
            link(dve.tensor_tensor(ch_m, r9[:, 0:8, 0:P], r9[:, 0:8, 1:RW], ALU.min))
            dve.tensor_tensor(ch_g, r9[:, 0:8, 0:P], r9[:, 0:8, 1:RW], ALU.is_le)
            dve.tensor_tensor(ch_m, r9[:, 1:9, 0:P], ch_m, ALU.is_ge).then_inc(S["left_ready"], 1)
            dve.wait_ge(S["k_made"], c + 1)
            fl = lambda v: v.rearrange("p r j -> p (r j)")
            link(dve.tensor_tensor_scan(fl(ch_s), fl(scanmask), fl(ch_k), 0.0, ALU.mult, ALU.max))
            if c >= 1:
                dve.wait_ge(S["k_out"], 64 * c)
            dve.tensor_copy(ch_d[:, :, 0:1], ch_s[:, :, 0:1])
            dve.tensor_tensor(ch_d[:, :, 1:P], ch_s[:, :, 1:P], ch_s[:, :, 0:P - 1], ALU.subtract).then_inc(S["k_cut"], 1)

        block = stack.enter_context(nc.Block())

        @block.sync
        def _(sp):
            small = [(ifw_n, if_w), (ifb_b[:], if_b.partition_broadcast(P)),
                     (onw_b[:], on_w.partition_broadcast(P)),
                     (tgr[:, 0:2], g_x.partition_broadcast(P)), (tgr[:, 2:4], g_f.partition_broadcast(P)),
                     (ab1_n, a_b1.rearrange("(c p) -> c p", c=NC)), (ab2_b[:], a_b2.partition_broadcast(P)),
                     (gw_n, gate_w), (mb1_n, m_b1.rearrange("e (c p) -> (e c) p", c=NC))]
            for c in range(4):
                sp.dma_start(xs[:, 8 * c:8 * c + 8], x[8 * c:8 * c + 8].rearrange("b t d -> t b d")).then_inc(x_in[c], 16)
                sp.dma_start(cs[:, 8 * c:8 * c + 8], ctx_[8 * c:8 * c + 8].rearrange("b t d -> t b d")).then_inc(ctx_in[c], 16)
                if c == 0:
                    for dst, src in small:
                        sp.dma_start(dst, src).then_inc(S["small_in"], 16)
            sp.wait_ge(S["consts_made"], 1)
            for k in range(4):
                sp.dma_start(b2blk[8 * k:8 * k + 8, k, :], m_b2).then_inc(S["b2_in"], 16)
            sp.wait_ge(S["av_done"], 2 * B + 2)
            sp.dma_start(w1n.rearrange("p (c d) -> p c d", c=NC), a_w1.rearrange("(c p) d -> p c d", c=NC)).then_inc(S["aw_in"], 16)
            sp.dma_start(w2n, a_w2).then_inc(S["aw_in"], 16)
            for g in range(G4):
                sp.wait_ge(S["dist_ready"], g + 1)
                sp.dma_start(d_dram[4 * g:4 * g + 4].rearrange("b i j -> i b j"), g4(dist, g)).then_inc(S["d_out"], 16)
            sp.wait_ge(S["d_out"], 16 * G4)
            for c in range(2):
                sp.dma_start(dring[0:B, c], d_dram[:, RC * c:RC * c + RC]).then_inc(d_in[c], 16)
            for c in range(NRC):
                sp.wait_ge(S["row_done"], RC * (c + 1))
                lo = 0 if c == 0 else 1
                sp.dma_start(r_dram[:, RC * c + lo:RC * c + RC + 1], rring[0:B, c % 2, lo:RC + 1]).then_inc(S["r_out"], 16)
                if c + 2 < NRC:
                    sp.dma_start(dring[0:B, c % 2], d_dram[:, RC * (c + 2):RC * (c + 3)]).then_inc(d_in[c % 2], 16)
                sp.wait_ge(S["r_out"], 16 * (c + 1))
                if c >= 1:
                    sp.wait_ge(S["left_ready"], c)
                for q in range(4):
                    rows = r_dram[:, RC * c + 8 * q:RC * c + 8 * q + 9]
                    sp.dma_start(r9[32 * q:32 * q + 32], rows).then_inc(S["r9_in"], 16)
                if c >= 1:
                    steps_out(sp, c - 1)
            steps_out(sp, NRC - 1)
            with sp.Fori(0, G4) as blk:
                sp.wait_ge(S["y_added"], blk * E + (E + 2))
                sp.dma_start(out[bass.ds(blk * 4, 4)].rearrange("b t d -> t b d"),
                             xs[:, bass.ds(blk * 4, 4)]).then_inc(S["stored"], 16)
            sp.wait_ge(S["stored"], 16 * G4)

        @block.gpsimd
        def _(pool):
            steps = [0]

            def link(ins):
                steps[0] += 1
                ins.then_inc(S["pool_step"], 1)
                pool.wait_ge(S["pool_step"], steps[0])

            pool.sem_inc(S["h_low_even"], 2)
            pool.memset(identf[:], 0.0)
            pool.memset(identb[:], 0.0)
            pool.memset(tri[:], 1.0)
            pool.memset(neg[:], 0.0)
            pool.memset(ones[:], 1.0)
            pool.iota(pidx[:, 0:1], [[0, 1]], base=0, channel_multiplier=1)
            pool.iota(hidx[:], [[1, 8]], base=0, channel_multiplier=0)
            pool.iota(iota2[:], [[2, P]], base=0, channel_multiplier=0, allow_small_or_imprecise_dtypes=True)
            link(pool.memset(b2blk[:], 0.0))
            line = [[1, P]]
            pool.affine_select(out=identf[:], in_=identf[:], compare_op=ALU.not_equal, fill=1.0, base=0, pattern=line, channel_multiplier=-1)
            pool.affine_select(out=identb[:], in_=identb[:], compare_op=ALU.not_equal, fill=1.0, base=0, pattern=line, channel_multiplier=-1)
            pool.affine_select(out=tri[:], in_=tri[:], compare_op=ALU.is_ge, fill=0.0, base=0, pattern=line, channel_multiplier=-1)
            pool.affine_select(out=neg[:], in_=neg[:], compare_op=ALU.is_ge, fill=-BIG, base=0, pattern=line, channel_multiplier=-1).then_inc(S["consts_made"], 1)
            for c in range(4):
                pool.wait_ge(ctx_in[c], 16)
            v4 = vaug.rearrange("p b (h w) -> p (b h) w", h=NH)
            pool.memset(v4[:, :, DH:VW], 1.0)
            pool.tensor_scalar(v4[:, :, 0:DH], cs[:].rearrange("p b (h w) -> p (b h) w", h=NH), 1.0, 0.0, ALU.mult, ALU.add).then_inc(S["vaug_ready"], 1)
            pool.wait_ge(S["k_kept"], G4)
            with pool.Fori(0, G4) as g:
                for k in range(4):
                    pool.wait_ge(S["sc_ready"], g * 8 + (2 * k + 2))
                    pool.tensor_copy(kslot[:, k % 2, :], kT[:, bass.ds(g * 512 + k * P, P)]).then_inc(S["kslot_ready"], 1)
            pool.wait_ge(S["scale_ready"], 2)
            pool.tensor_tensor(xs[:], xs[:], rep(ab2_b[:], B), ALU.add).then_inc(S["b2_added"], 1)
            raw_load(pool, 0)
            raw_load(pool, 1)
            pool.wait_ge(S["dsum_done"], G4)
            for n in range(2 * E):
                wh, wl = (w1h, w1l) if n < E else (w2h, w2l)
                pool.wait_ge(S["raw_kept"], n + 1)
                if n + 2 < 2 * E:
                    raw_load(pool, n + 2)
                src = four(wcp[:, n % 2, :])
                link(pool.tensor_scalar(wh[:, n % E], src, 1.0, 0.0, ALU.mult, ALU.add))
                pool.tensor_tensor(wl[:, n % E], src, wh[:, n % E], ALU.subtract).then_inc(S["w_split"], 1)
            link(pool.memset(scanmask, 1.0))
            link(pool.memset(scanmask[:, :, 0:1], 0.0))
            for c in range(NRC):
                pool.wait_ge(S["left_ready"], c + 1)
                link(pool.tensor_tensor(ch_k, rep(iota2[:], 8), ch_g, ALU.subtract))
                pool.tensor_tensor(ch_k, ch_k, ch_m, ALU.mult).then_inc(S["k_made"], 1)
            with pool.Fori(0, G4) as blk:
                for e in range(E):
                    for c in range(0, NC, 2):
                        pool.wait_ge(S["h_high"], blk * (E * NC) + (e * NC + c + 1))
                        pool.tensor_tensor(hl[:, e % 2, c, :], hf[:, c, :], hh[:, e % 2, c, :], ALU.subtract).then_inc(S["h_low_even"], 1)

        @block.scalar
        def _(act):
            steps = [0]

            def link(ins):
                steps[0] += 1
                ins.then_inc(S["act_step"], 1)
                act.wait_ge(S["act_step"], steps[0])

            def ln(n):
                for h in range(2):
                    act.wait_ge(S["bn_done"], 2 * n + h + 1)
                    act.activation(lnt[:, 5, 16 * h:16 * h + 16], lnt[:, 4, 16 * h:16 * h + 16], ACT.Sqrt, bias=cst[:, 0:1]).then_inc(S["ln_sqrt"], 1)

            act.sem_inc(S["exp_done"], 2)
            act.sem_inc(S["o_kept"], 2)
            act.sem_inc(S["h_gelu"], 4)
            act.wait_ge(S["tg_in_ready"], 1)
            act.activation(tg[:], tgr[:], ACT.Tanh).then_inc(S["tg_ready"], 1)
            for c in range(4):
                act.wait_ge(ctx_in[c], 16)
            act.activation(aa_tmp, cs[:], ACT.Square).then_inc(S["csq_done"], 1)
            ln(0)
            for g in range(G4):
                act.wait_ge(S["c_turned"], g + 1)
                act.activation(kT[:, 512 * g:512 * g + 512], bank(2 + g % 2), ACT.Copy).then_inc(S["k_kept"], 1)
            act.wait_ge(S["gates_biased"], 1)
            act.activation(pre, pre, ACT.Tanh, scale=1.0 / GATE_CAP).then_inc(S["gates_capped"], 1)
            act.wait_ge(S["gates_capped"], 1)
            link(act.activation(nlf, pre[:, :, NH:2 * NH], ACT.Exp, scale=-GATE_CAP))
            act.activation(nlf, nlf, ACT.Ln, bias=cst[:, 3:4]).then_inc(S["nlf_ready"], 1)
            act.wait_ge(S["m_tok_ready"], 1)
            act.activation(expnm[:], expnm[:], ACT.Exp).then_inc(S["expnm_ready"], 1)
            with act.Fori(0, G4) as g:
                def keep(m):
                    act.wait_ge(S["av_done"], g * 8 + (m + 3))
                    o = 2 * VW * (m % 2)
                    own = PS[:, 6 + m % 2, o:o + 4 * 7 * VW].rearrange("p (j w) -> p j w", j=4)[:, :, 0:VW]
                    act.activation(oall[:, bass.ds(g * 4 + m // 2, 1), 4 * VW * (m % 2):4 * VW * (m % 2) + 4 * VW]
                                   .rearrange("p b (j w) -> p (b j) w", j=4), own, ACT.Copy).then_inc(S["o_kept"], 1)

                for k in range(4):
                    for half in range(2):
                        u = g * 8 + (2 * k + half)
                        act.wait_ge(S["ld_ready"], u + 1)
                        act.wait_ge(S["prod_done"], u + 1)
                        act.activation(decay[:, half, :], bank(half), ACT.Exp).then_inc(S["exp_done"], 1)
                        if 2 * k + half:
                            keep(2 * k + half - 1)
                keep(7)
            act.wait_ge(S["o_kept"], 2 * B + 2)
            o3 = oall.rearrange("p b (h w) -> p (b h) w", h=NH)
            act.activation(osq.rearrange("p (m w) -> p m w", w=DH), o3[:, :, 0:DH], ACT.Square).then_inc(S["osq_done"], 1)
            act.wait_ge(S["osum_done"], 1)
            act.activation(fin[:, 1, :], fin[:, 1, :], ACT.Sqrt, bias=cst[:, 1:2], scale=1.0 / DH).then_inc(S["osqrt_done"], 1)
            ln(1)
            act.wait_ge(S["scale_ready"], 1)
            act.activation(wtmp[:, 0:HID], w1n, ACT.Identity, scale=qs[:, 2:3], bias=cst[:, 2:3])
            act.activation(wtmp[:, HID:2 * HID], w2n, ACT.Identity, scale=qs[:, 3:4], bias=cst[:, 2:3]).then_inc(S["w_scaled"], 1)
            act.wait_ge(S["scale_ready"], 2)
            for c in range(4):
                v = xn[:, 8 * c:8 * c + 8]
                act.activation(v, v, ACT.Identity, scale=qs[:, 8:9], bias=cst[:, 2:3]).then_inc(S["x_scaled"], 1)
            for n in range(2):
                act.wait_ge(S["wq_turned"], n + 1)
                dst = w1q if n == 0 else w2q.rearrange("p c d -> p (c d)")
                act.activation(dst, bankb(6 + n), ACT.Copy).then_inc(S["wq_kept"], 1)
            for nb in range(G4):
                act.wait_ge(S["xq_turned"], nb + 1)
                act.activation(xqT[:, 512 * nb:512 * nb + 512], bankb(nb % 2), ACT.Copy).then_inc(S["xqT_kept"], 1)
                for c in range(NC):
                    act.wait_ge(S["ffn1_done"], NC * nb + c + 1)
                    act.activation(hid[:, c, 512 * nb:512 * nb + 512], bank(2 + c), ACT.Gelu, scale=qs[:, 12:13],
                                   bias=small_t[:, 80 + c:81 + c]).then_inc(S["gelu_done"], 1)
            act.wait_ge(S["scale_ready"], 3)
            for nb in range(G4):
                v = hid[:, :, 512 * nb:512 * nb + 512]
                act.activation(v, v, ACT.Identity, scale=qs[:, 16:17], bias=cst[:, 2:3]).then_inc(S["h_scaled"], 1)
            ln(2)
            for g in range(G4 + 1):
                if g < G4:
                    act.wait_ge(S["x3T_turned"], g + 1)
                    if g >= 2:
                        act.wait_ge(S["dsum_done"], g - 1)
                    act.activation(xT2[:, g % 2, :], bank(g % 2), ACT.Copy, scale=-2.0)
                    act.activation(xTsq[:, g % 2, :], bank(g % 2), ACT.Square).then_inc(S["x3T_kept"], 1)
                if g >= 1:
                    act.wait_ge(S["dsq_ready"], g)
                    act.activation(g4(dist, g - 1), g4(dsq, g - 1), ACT.Sqrt).then_inc(S["dist_ready"], 1)
            for n in range(2 * E):
                if n >= 2:
                    act.wait_ge(S["w_split"], n - 1)
                act.wait_ge(S["raw_turned"], n + 1)
                act.activation(wcp[:, n % 2, :], bank(4 + n % 2), ACT.Copy).then_inc(S["raw_kept"], 1)
            ln(3)
            for g in range(G4):
                act.wait_ge(S["x4_turned"], g + 1)
                if g >= 2:
                    act.wait_ge(S["logits_done"], g - 1)
                    act.wait_ge(S["x4_split"], g - 1)
                act.activation(x4f[:, g % 2, :], bank(g % 2), ACT.Copy).then_inc(S["x4_kept"], 1)
            with act.Fori(0, G4) as blk:
                for e in range(E):
                    for c in range(NC):
                        n = blk * (E * NC) + (e * NC + c)
                        act.wait_ge(S["h_ready"], n + 1)
                        act.wait_ge(S["h_low_even" if c % 2 == 0 else "h_low_odd"], blk * (2 * E) + (2 * e + c // 2 + 1))
                        b1 = small_t[:, 48 + e * NC + c:49 + e * NC + c]
                        act.activation(hf[:, c, :], bank(c), ACT.Gelu_apprx_tanh, bias=b1).then_inc(S["h_gelu"], 1)

        @block.vector
        def _(dve):
            steps = [0]

            def link(ins):
                steps[0] += 1
                ins.then_inc(S["dve_step"], 1)
                dve.wait_ge(S["dve_step"], steps[0])

            def ts(out, a, s1, s2, op0, op1=ALU.bypass):
                return dve.tensor_scalar(out, a, s1, s2, op0, op1)

            def ln(n, src, dst, stats_ready=None):
                for h in range(2):
                    w = slice(16 * h, 16 * h + 16)
                    for b in range(16 * h, 16 * h + 16):
                        if stats_ready is not None:
                            stats_ready(b)
                        ins = dve.bn_stats(bns[:, b, :], src[:, b, :])
                    link(ins)
                    t = lambda k: lnt[:, k, w]
                    dve.tensor_tensor(t(0), bns[:, w, 1], bns[:, w, 4], ALU.add)
                    dve.tensor_tensor(t(1), bns[:, w, 1], bns[:, w, 4], ALU.subtract)
                    link(dve.tensor_tensor(t(2), bns[:, w, 2], bns[:, w, 5], ALU.add))
                    ts(t(3), t(0), 0.5, None, ALU.mult)
                    link(dve.tensor_tensor(t(6), t(1), t(1), ALU.mult))
                    link(ts(t(6), t(6), 0.25, None, ALU.mult))
                    dve.scalar_tensor_tensor(out=t(4), in0=t(2), scalar=1.0 / D, in1=t(6), op0=ALU.mult, op1=ALU.add).then_inc(S["bn_done"], 1)
                for h in range(2):
                    w = slice(16 * h, 16 * h + 16)
                    dve.wait_ge(S["ln_sqrt"], 2 * n + h + 1)
                    link(dve.reciprocal(lnt[:, 7, w], lnt[:, 5, w]))
                    for b in range(16 * h, 16 * h + 16):
                        ins = ts(dst[:, b, :], src[:, b, :], lnt[:, 3, b:b + 1], lnt[:, 7, b:b + 1], ALU.subtract, ALU.mult)
                        if b % 4 == 3:
                            ins.then_inc(S["ln_done"], 1)

            def spread(n):
                dve.wait_ge(S["mm_turned"], n + 1)
                link(dve.tensor_reduce(gq[0:2, 0:1], PS[0:2, 7, 0:P], AX, ALU.max))
                ts(gq[0:2, 2:4], identf[0:2, 0:2], gq[0:2, 0:1], None, ALU.mult).then_inc(S["mm_global"], 1)
                dve.wait_ge(S["mm_spread"], n + 1)
                link(dve.tensor_copy(mm[:, 2:4], bank(7, P, P + 2)))

            def affine(o):
                q = lambda k: qs[:, o + k:o + k + 1]
                link(dve.tensor_tensor(q(0), mm[:, 2:3], mm[:, 3:4], ALU.add))
                link(ts(q(1), q(0), 1.0 / 255.0, 1e-8, ALU.mult, ALU.max))
                link(dve.reciprocal(q(0), q(1)))
                link(ts(q(2), q(0), mm[:, 3:4], MAGIC, ALU.mult, ALU.add))
                link(ts(q(2), q(2), MAGIC, -128.0, ALU.subtract, ALU.add))
                link(ts(q(2), q(2), -128.0, 127.0, ALU.max, ALU.min))
                ts(q(3), q(2), -1.0, MAGIC + 127.0, ALU.mult, ALU.add)
                link(ts(q(2), q(2), -1.0, MAGIC - 128.0, ALU.mult, ALU.add))

            dve.sem_inc(S["prod_done"], 2)
            dve.sem_inc(S["y_added"], 2)
            dve.sem_inc(S["h_low_odd"], 2)
            dve.memset(cst[:, 0:1], LN_EPS)
            dve.memset(cst[:, 1:2], NORM_EPS)
            dve.memset(cst[:, 2:3], MAGIC)
            dve.memset(cst[:, 3:4], 1.0)
            dve.wait_ge(S["consts_made"], 1)
            ts(pidx[:, 1:2], pidx[:, 0:1], 3, 3, ALU.logical_shift_right, ALU.bitwise_and)
            ts(pidx[:, 2:3], pidx[:, 0:1], 4, 1, ALU.logical_shift_right, ALU.bitwise_and)
            ts(pidx[:, 3:4], pidx[:, 0:1], 7, None, ALU.bitwise_and)
            link(ts(pidx[:, 4:5], pidx[:, 0:1], 5, None, ALU.logical_shift_right))
            ts(pm[:, 0:1], pidx[:, 2:3], 0.0, None, ALU.is_equal)
            ts(pm[:, 1:2], pidx[:, 2:3], 1.0, None, ALU.is_equal)
            ts(pm[:, 2:3], pidx[:, 1:2], 1.0, -1.0, ALU.is_ge, ALU.mult)
            ts(pm[:, 3:4], pidx[:, 1:2], 2.0, -1.0, ALU.is_ge, ALU.mult)
            ts(pm[:, 4:5], pidx[:, 1:2], 3.0, None, ALU.is_lt)
            dve.tensor_copy(pm[:, 5:6], pidx[:, 3:4])
            for k in range(4):
                ts(pm[:, 6 + k:7 + k], pidx[:, 4:5], float(k), None, ALU.is_equal)
            link(dve.tensor_copy(hidf[:], hidx[:]))
            link(ts(hpos[:], hidf[:], pm[:, 5:6], None, ALU.is_equal))
            ts(hneg[:], hpos[:], -1.0, None, ALU.mult)
            for k in range(4):
                ts(selb[:, k, :], ones[:], pm[:, 6 + k:7 + k], None, ALU.mult)
                ins = ts(bmask[:, k], last(hpos[:], P), pm[:, 6 + k:7 + k], None, ALU.mult)
            link(ins)
            dve.wait_ge(S["small_in"], 16 * 9)
            dve.tensor_copy(tgr[:, 0:1], tgr[:, 0:1]).then_inc(S["tg_in_ready"], 1)

            def x_here(b):
                if b % 8 == 0:
                    dve.wait_ge(x_in[b // 8], 16)
            ln(0, xs, xn, x_here)
            dve.wait_ge(S["small_turned"], 1)
            link(dve.tensor_copy(small_t[:, 0:92], bank(6, 0, 92)))
            dve.tensor_tensor(wkv[:], small_t[:, 16:32], small_t[:, 32:48], ALU.add).then_inc(S["small_kept"], 1)
            for g in range(G4):
                dve.wait_ge(S["q_turned"], g + 1)
                dve.tensor_copy(qT[:, 512 * g:512 * g + 512], bank(g % 2)).then_inc(S["q_kept"], 1)
            dve.wait_ge(S["csq_done"], 1)
            dve.tensor_reduce(aa[:], aa_tmp, AX, ALU.add)
            dve.wait_ge(S["gates_summed"], 1)
            dve.tensor_tensor(pre, bank(4).rearrange("p (b w) -> p b w", b=B), rep(ifb_b[:], B), ALU.add).then_inc(S["gates_biased"], 1)
            dve.wait_ge(S["cumsum_done"], 1)
            csum = bank(5, 0, B * NH).rearrange("p (b h) -> p b h", b=B)
            dve.tensor_copy(ncs, csum)
            link(dve.scalar_tensor_tensor(out=a_tok, in0=pre[:, :, 0:NH], scalar=GATE_CAP, in1=csum, op0=ALU.mult, op1=ALU.add))
            arep = A[:, 12288:13312].rearrange("p (b r h) -> p b r h", b=B, r=4)
            dve.tensor_copy(arep, a_tok.unsqueeze(2).to_broadcast([P, B, 4, NH])).then_inc(S["a_ready"], 1)
            for j in range(2):
                dve.wait_ge(S["a_turned"], j + 1)
                dve.tensor_copy(av[:, 0, 4 * j:4 * j + 4, :].rearrange("p g t -> p (g t)"), bank(j)).then_inc(S["dve_step"], 1)
            steps[0] += 2
            dve.wait_ge(S["dve_step"], steps[0])
            for g in range(G4):
                dve.tensor_tensor_scan(av[:, 1, g, :], av[:, 0, g, :], av[:, 0, g, :], -3e38, ALU.max, ALU.max).then_inc(S["m_ready"], 1)
            for j in range(2):
                dve.wait_ge(S["m_turned"], j + 1)
                mtok = bank(2 + j).rearrange("p (b r h) -> p b r h", b=16, r=4)[:, :, 0, :]
                ins = dve.tensor_tensor(expnm[:, 16 * j:16 * j + 16, :], ncs[:, 16 * j:16 * j + 16, :], mtok, ALU.subtract)
            ins.then_inc(S["m_tok_ready"], 1)
            dve.wait_ge(S["m_ready"], G4)
            dve.wait_ge(S["a_turned"], 2)
            fl = lambda v: v.rearrange("p w g t -> p (w g t)")
            link(dve.tensor_copy(fl(av_cut), fl(av)))
            link(dve.scalar_tensor_tensor(out=fl(av_res), in0=fl(av_cut), scalar=pm[:, 2:3], in1=fl(av), op0=ALU.mult, op1=ALU.add))
            link(dve.tensor_copy(fl(av_cut), fl(av_res)))
            link(dve.scalar_tensor_tensor(out=fl(av_res), in0=fl(av_cut), scalar=pm[:, 3:4], in1=fl(av_res), op0=ALU.mult, op1=ALU.add))
            link(ts(fl(av_part), fl(av_res), pm[:, 4:5], None, ALU.mult))
            for h in range(NH):
                ins = ts(mblk[:, :, h, :], av_part[:, 1], hneg[:, h:h + 1], None, ALU.mult)
            ins.then_inc(S["mblk_ready"], 1)
            with dve.Fori(0, G4) as g:
                for k in range(4):
                    dve.wait_ge(S["sc_ready"], g * 8 + (2 * k + 2))
                    for r in range(2):
                        ins = ts(qslot[:, k % 2, r], qT[:, bass.ds(g * 512 + k * P, P)], pm[:, r:r + 1], None, ALU.mult)
                    ins.then_inc(S["qslot_ready"], 1)
                    for half in range(2):
                        u = g * 8 + (2 * k + half)
                        dve.wait_ge(S["exp_done"], u + 3)
                        dve.wait_ge(S["sc_ready"], u + 5)
                        dve.wait_ge(S["av_done"], u + 1)
                        dve.tensor_tensor(smat[:, half, :].rearrange("p (j c) -> p j c", j=2),
                                          decay[:, half, :].rearrange("p (j c) -> p j c", j=2),
                                          PS[:, 2 + 2 * half:4 + 2 * half, 0:256], ALU.mult).then_inc(S["prod_done"], 1)
            dve.wait_ge(S["o_kept"], 2 * B + 2)
            o3 = oall.rearrange("p b (h w) -> p (b h) w", h=NH)
            f = lambda k: fin[:, k, :]
            fr = f(0).unsqueeze(2)
            link(ts(fr, o3[:, :, DH:VW], 0.25, None, ALU.mult))
            link(dve.scalar_tensor_tensor(out=f(0), in0=f(0), scalar=-1.0, in1=f(0), op0=ALU.mult, op1=ALU.max))
            dve.wait_ge(S["expnm_ready"], 1)
            link(dve.tensor_tensor(f(0), f(0), expnm[:].rearrange("p b h -> p (b h)"), ALU.max))
            link(ts(f(0), f(0), BACKEND_EPS, None, ALU.add))
            link(dve.reciprocal(f(2), f(0)))
            link(ts(f(0), f(2), 0.25, None, ALU.mult))
            dve.wait_ge(S["osq_done"], 1)
            dve.tensor_reduce(f(1), osq.rearrange("p (m w) -> p m w", w=DH), AX, ALU.add)
            link(dve.tensor_tensor(f(2), f(0), f(0), ALU.mult))
            dve.tensor_tensor(f(1), f(1), f(2), ALU.mult).then_inc(S["osum_done"], 1)
            dve.wait_ge(S["tg_ready"], 1)
            ts(onw_b[:], onw_b[:], 1.0, tg[:, 0:1], ALU.add, ALU.mult)
            dve.wait_ge(S["osqrt_done"], 1)
            link(dve.reciprocal(f(2), f(1)))
            link(dve.tensor_tensor(f(0), f(0), f(2), ALU.mult))
            link(dve.tensor_tensor(osq.rearrange("p (m w) -> p m w", w=DH), o3[:, :, 0:DH], last(f(0), DH), ALU.mult))
            o4 = osq.rearrange("p (b d) -> p b d", b=B)
            link(dve.tensor_tensor(o4, o4, rep(onw_b[:], B), ALU.mult))
            link(dve.tensor_tensor(xs[:], xs[:], o4, ALU.add))
            ln(1, xs, xn)
            dve.wait_ge(S["aw_in"], 32)
            dve.scalar_tensor_tensor(out=wtmp[:, 0:HID], in0=w1n, scalar=-1.0, in1=w1n, op0=ALU.mult, op1=ALU.max)
            link(dve.scalar_tensor_tensor(out=wtmp[:, HID:2 * HID], in0=w2n, scalar=-1.0, in1=w2n, op0=ALU.mult, op1=ALU.max))
            dve.tensor_reduce(mm[:, 0:2], wtmp.rearrange("p (w c) -> p w c", w=2), AX, ALU.max).then_inc(S["mm_ready"], 1)
            spread(0)
            link(ts(qs[:, 0:2], mm[:, 2:4], 1.0 / 127.0, 1e-8, ALU.mult, ALU.max))
            dve.reciprocal(qs[:, 2:4], qs[:, 0:2]).then_inc(S["scale_ready"], 1)
            dve.wait_ge(S["ln_done"], 2 * G4)
            dve.tensor_reduce(mm[:, 0:1], xn_w1[:], AX, ALU.max)
            link(dve.tensor_reduce(mm[:, 4:5], xn_w1[:], AX, ALU.min))
            ts(mm[:, 1:2], mm[:, 4:5], -1.0, None, ALU.mult).then_inc(S["mm_ready"], 1)
            dve.wait_ge(S["w_scaled"], 1)
            link(ts(wtmp, wtmp, MAGIC - 127.0, MAGIC + 127.0, ALU.max, ALU.min))
            ts(wqb, wtmp, MAGIC, None, ALU.subtract).then_inc(S["wq_ready"], 1)
            spread(1)
            affine_x = 20
            affine(affine_x)
            dve.tensor_copy(qs[:, 8:9], qs[:, affine_x:affine_x + 1])
            link(dve.tensor_tensor(qs[:, 12:13], qs[:, affine_x + 1:affine_x + 2], qs[:, 0:1], ALU.mult))
            dve.tensor_tensor(ab2_b[:], ab2_b[:], tg[:, 2:3].to_broadcast([P, D]), ALU.mult).then_inc(S["scale_ready"], 1)
            for c in range(4):
                v = xn_w1[:, 1024 * c:1024 * c + 1024]
                dve.wait_ge(S["x_scaled"], c + 1)
                link(ts(v, v, qs[:, affine_x + 2:affine_x + 3], qs[:, affine_x + 3:affine_x + 4], ALU.max, ALU.min))
                ts(xq[:, 1024 * c:1024 * c + 1024], v, MAGIC, None, ALU.subtract).then_inc(S["xq_ready"], 1)
            for nb in range(G4):
                dve.wait_ge(S["gelu_done"], NC * (nb + 1))
                v = hid[:, :, 512 * nb:512 * nb + 512]
                dve.tensor_reduce(hmm[:, 0, NC * nb:NC * nb + NC], v, AX, ALU.max)
                ins = dve.tensor_reduce(hmm[:, 1, NC * nb:NC * nb + NC], v, AX, ALU.min)
            link(ins)
            dve.tensor_reduce(mm[:, 0:1], hmm[:, 0, :], AX, ALU.max)
            link(dve.tensor_reduce(mm[:, 4:5], hmm[:, 1, :], AX, ALU.min))
            ts(mm[:, 1:2], mm[:, 4:5], -1.0, None, ALU.mult).then_inc(S["mm_ready"], 1)
            spread(2)
            affine_h = 24
            affine(affine_h)
            link(dve.tensor_tensor(qs[:, 13:14], qs[:, affine_h + 1:affine_h + 2], qs[:, 1:2], ALU.mult))
            link(dve.tensor_tensor(qs[:, 13:14], qs[:, 13:14], tg[:, 2:3], ALU.mult))
            dve.tensor_copy(qs[:, 16:17], qs[:, affine_h:affine_h + 1]).then_inc(S["scale_ready"], 1)

            def add2(nb):
                dve.wait_ge(S["ffn2_done"], nb + 1)
                dve.scalar_tensor_tensor(out=g4(xs, nb), in0=four(bank(nb % 2)), scalar=qs[:, 13:14], in1=g4(xs, nb),
                                         op0=ALU.mult, op1=ALU.add).then_inc(S["ffn2_added"], 1)
            dve.wait_ge(S["b2_added"], 1)
            for nb in range(G4):
                v = hid[:, :, 512 * nb:512 * nb + 512]
                dve.wait_ge(S["h_scaled"], nb + 1)
                link(ts(v, v, qs[:, affine_h + 2:affine_h + 3], qs[:, affine_h + 3:affine_h + 4], ALU.max, ALU.min))
                ts(hq[:, :, 512 * nb:512 * nb + 512], v, MAGIC, None, ALU.subtract).then_inc(S["hq_ready"], 1)
                if nb >= 1:
                    add2(nb - 1)
            add2(G4 - 1)
            dve.wait_ge(S["ffn2_added"], G4)
            ln(2, xs, xn)
            for g in range(G4):
                dve.wait_ge(S["dsum_done"], g + 1)
                for k in range(4):
                    ins = ts(dsq[:, 4 * g + k, :], bank(2 + g % 2, P * k, P * k + P), aa[:, 4 * g + k:4 * g + k + 1], 0.0, ALU.add, ALU.max)
                ins.then_inc(S["dsq_ready"], 1)
            dve.wait_ge(S["d_out"], 16 * G4)
            rr = Bm[0:B, 0:2 * (RC + 1) * RW]
            link(dve.memset(rr, BIG))
            link(dve.memset(rring[0:B, 0, 0, 0:1], 0.0))
            dve.memset(ee[:], 2.0 * (P - 1))
            for c in range(NRC):
                dve.wait_ge(d_in[c % 2], 16 * (c // 2 + 1))
                if c >= 2:
                    dve.wait_ge(S["r_out"], 16 * (c - 1))
                for r in range(RC):
                    above = rring[0:B, c % 2, r] if r or not c else rring[0:B, (c - 1) % 2, RC]
                    link(dve.tensor_tensor(rowm[:], above[:, 1:RW], above[:, 0:P], ALU.min))
                    dve.tensor_tensor_scan(rring[0:B, c % 2, r + 1, 1:RW], rowm[:], dring[0:B, c % 2, r], BIG, ALU.min, ALU.add)\
                        .then_inc(S["row_done"], 1)
                    dve.wait_ge(S["row_done"], RC * c + r + 1)
                if c >= 1:
                    back_steps(dve, link, c - 1)
            back_steps(dve, link, NRC - 1)
            for i in reversed(range(P)):
                if i % RC == RC - 1:
                    dve.wait_ge(S["k_in"], 16 * NRC)
                dve.scalar_tensor_tensor(out=rowm[:], in0=iota2[0:B], scalar=ee[:, i + 1:i + 2], in1=kb[0:B, i, :],
                                         op0=ALU.is_le, op1=ALU.mult, accum_out=ee[:, i:i + 1]).then_inc(S["track_done"], 1)
                dve.wait_ge(S["track_done"], P - i)
            dve.wait_ge(S["e_turned"], 1)
            link(dve.tensor_copy(eT[:], bank(0, 0, 2 * B).rearrange("p (w b) -> p w b", w=2)))
            for g in range(G4):
                for b in range(4 * g, 4 * g + 4):
                    ins = ts(pathm[:, b, :], iota2[:], eT[:, 1, b:b + 1], None, ALU.is_le)
                link(ins)
                for b in range(4 * g, 4 * g + 4):
                    ins = dve.scalar_tensor_tensor(out=path[:, b, :], in0=iota2[:], scalar=eT[:, 0, b:b + 1], in1=pathm[:, b, :],
                                                   op0=ALU.is_ge, op1=ALU.mult)
                ins.then_inc(S["path_ready"], 1)
            for g in range(G4):
                dve.wait_ge(S["expanded"], g + 1)
                dve.scalar_tensor_tensor(out=g4(xs, g), in0=four(bank(1 + g % 2)), scalar=tg[:, 1:2], in1=g4(xs, g),
                                         op0=ALU.mult, op1=ALU.add).then_inc(S["expanded_added"], 1)
            dve.wait_ge(S["expanded_added"], G4)
            ln(3, xs, x4)
            for g in range(G4):
                dve.wait_ge(S["x4_kept"], g + 1)
                w = slice(512 * g, 512 * g + 512)
                link(dve.tensor_copy(x4h[:, w], x4f[:, g % 2, :]))
                dve.tensor_tensor(x4l[:, w], x4f[:, g % 2, :], x4h[:, w], ALU.subtract).then_inc(S["x4_split"], 1)
            dve.wait_ge(S["logits_done"], G4)
            lgf = lg.rearrange("p b e -> p (b e)")
            link(dve.tensor_copy(lgf, bank(2, 0, B * E)))
            key, cand, flip, fbits, fl32 = (seli[:, k:k + 1] for k in range(5))
            MIN32 = -(1 << 31)
            dve.memset(key, 0)
            dve.memset(flip, -1)
            dve.memset(fl32, MIN32)
            link(dve.memset(fbits, 0))
            for n in range(32):
                if n:
                    link(ts(cand, key, 1 << (31 - n), None, ALU.bitwise_or))
                    link(dve.tensor_tensor(fbits, cand, flip, ALU.bitwise_xor))
                dve.tensor_scalar(selw, lgf, fbits.bitcast(F32), None, ALU.is_lt, ALU.add, accum_out=sel[:, 0:1]).then_inc(S["count_ready"], 1)
                dve.wait_ge(S["count_all"], n + 1)
                link(ts(sel[:, 1:2], bank(3, 0, 1), KTH - 1.0, None, ALU.is_le))
                link(dve.copy_predicated(key, sel[:, 1:2].bitcast(I32), fl32 if n == 0 else cand))
                if n == 0:
                    link(dve.copy_predicated(flip, sel[:, 1:2].bitcast(I32), fl32))
            link(dve.tensor_tensor(fbits, key, flip, ALU.bitwise_xor))
            link(dve.scalar_tensor_tensor(out=gts, in0=lg, scalar=fbits.bitcast(F32), in1=lg, op0=ALU.is_ge, op1=ALU.mult))
            ts(gts, gts, tg[:, 3:4], None, ALU.mult).then_inc(S["gates_ready"], 1)
            for g in range(G4 + 1):
                if g < G4:
                    dve.wait_ge(S["gt_turned"], g + 1)
                    dve.tensor_copy(gtT[:, g % 2, :], PS[0:32, 4 + g % 2, 0:P]).then_inc(S["gt_kept"], 1)
                if g >= 1:
                    dve.wait_ge(S["gb_done"], g)
                    dve.tensor_tensor(g4(xs, g - 1), g4(xs, g - 1), four(bank(6 + (g - 1) % 2)), ALU.add).then_inc(S["gb_added"], 1)
            dve.wait_ge(S["gb_added"], G4)
            dve.wait_ge(S["gates_ready"], 1)
            def parts(blk, e):
                for c in range(NC):
                    dve.wait_ge(S["h_gelu"], blk * (E * NC) + (e * NC + c + 5))
                    if c == 0:
                        dve.wait_ge(S["y_ready"], blk * E + (e + 1))
                    dve.tensor_copy(hh[:, e % 2, c, :], hf[:, c, :]).then_inc(S["h_high"], 1)
                    if c % 2:
                        dve.wait_ge(S["h_high"], blk * (E * NC) + (e * NC + c + 1))
                        dve.tensor_tensor(hl[:, e % 2, c, :], hf[:, c, :], hh[:, e % 2, c, :], ALU.subtract).then_inc(S["h_low_odd"], 1)

            def gated_sum(blk, e):
                dve.wait_ge(S["y_ready"], blk * E + (e + 3))
                dve.wait_ge(S["y_added"], blk * E + (e + 2))
                for k in range(4):
                    row = xs[:].rearrange("p b d -> p (b d)")[:, bass.ds(blk * 512 + k * P, P)]
                    gate = gts.rearrange("p b e -> p (b e)")[:, bass.ds(blk * (4 * E) + (k * E + e), 1)]
                    ins = dve.scalar_tensor_tensor(out=row, in0=bank(4 + e % 2, P * k, P * k + P), scalar=gate, in1=row,
                                                   op0=ALU.mult, op1=ALU.add)
                ins.then_inc(S["y_added"], 1)

            parts(0, 0)
            with dve.Fori(0, G4 - 1) as blk:
                for e in range(1, E):
                    parts(blk, e)
                    gated_sum(blk, e - 1)
                parts(blk + 1, 0)
                gated_sum(blk, E - 1)
            for e in range(1, E):
                parts(G4 - 1, e)
                gated_sum(G4 - 1, e - 1)
            gated_sum(G4 - 1, E - 1)

        @block.tensor
        def _(pe):
            def spread(n):
                pe.wait_ge(S["mm_ready"], n + 1)
                pe.transpose(PS[0:2, 7, 0:P], mm[:, 0:2], identf[:]).then_inc(S["mm_turned"], 1)
                pe.wait_ge(S["mm_global"], n + 1)
                pe.matmul(bank(7, P, P + 2), ones[0:2, :], gq[0:2, 2:4], start=True, stop=True).then_inc(S["mm_spread"], 1)

            pe.sem_inc(S["sc_ready"], 4)
            pe.sem_inc(S["av_done"], 2)
            pe.sem_inc(S["y_ready"], 2)
            pe.wait_ge(S["consts_made"], 1)
            pe.wait_ge(S["small_in"], 16 * 9)
            for k in range(3):
                pe.transpose(bank(6, 16 * k, 16 * k + 16), ifw_n[:, P * k:P * k + P], identf[0:16, 0:16])
            pe.transpose(bank(6, 48, 80), mb1_n, identf[0:32, 0:32])
            pe.transpose(bank(6, 80, 84), ab1_n, identf[0:4, 0:4])
            pe.transpose(bank(6, 84, 92), gw_n, identf[0:8, 0:8]).then_inc(S["small_turned"], 1)
            for g in range(G4):
                if g % 2 == 0:
                    pe.wait_ge(ctx_in[g // 2], 16)
                if g >= 2:
                    pe.wait_ge(S["k_kept"], g - 1)
                for k in range(4):
                    ins = pe.transpose(bank(2 + g % 2, P * k, P * k + P), cs[:, 4 * g + k, :], identf[:])
                ins.then_inc(S["c_turned"], 1)
                pe.wait_ge(S["ln_done"], g + 1)
                if g >= 2:
                    pe.wait_ge(S["q_kept"], g - 1)
                for k in range(4):
                    ins = pe.transpose(bank(g % 2, P * k, P * k + P), xn[:, 4 * g + k, :], identf[:])
                ins.then_inc(S["q_turned"], 1)
            pe.wait_ge(S["small_kept"], 1)
            for g in range(G4):
                pe.wait_ge(S["q_kept"], g + 1)
                pe.wait_ge(S["k_kept"], g + 1)
                for b in range(4 * g, 4 * g + 4):
                    o = bank(4, 16 * b, 16 * b + 16)
                    w = slice(P * b, P * b + P)
                    pe.matmul(o, qT[:, w], small_t[:, 0:16], start=True, stop=False)
                    ins = pe.matmul(o, kT[:, w], wkv[:], start=False, stop=True)
            ins.then_inc(S["gates_summed"], 1)
            pe.wait_ge(S["nlf_ready"], 1)
            pe.matmul(bank(5, 0, B * NH), tri[:], nlf.rearrange("p b h -> p (b h)"), start=True, stop=True).then_inc(S["cumsum_done"], 1)
            pe.wait_ge(S["a_ready"], 1)
            for j in range(2):
                for g in range(4):
                    ins = pe.transpose(bank(j, P * g, P * g + P), A[:, 12288 + P * (4 * j + g):12288 + P * (4 * j + g + 1)], identf[:])
                ins.then_inc(S["a_turned"], 1)
            for j in range(2):
                pe.wait_ge(S["m_ready"], 4 * (j + 1))
                for g in range(4):
                    ins = pe.transpose(bank(2 + j, P * g, P * g + P), av[:, 1, 4 * j + g, :], identf[:])
                ins.then_inc(S["m_turned"], 1)
            pe.wait_ge(S["m_tok_ready"], 1)
            pe.wait_ge(S["mblk_ready"], 1)
            pe.wait_ge(S["vaug_ready"], 1)
            with pe.Fori(0, G4) as g:
                def weigh(k, half):
                    u = g * 8 + (2 * k + half)
                    pe.wait_ge(S["prod_done"], u + 3)
                    pe.wait_ge(S["o_kept"], u + 1)
                    for j in range(4):
                        v6 = vaug[:, bass.ds(g * 4 + k, 1), 2 * VW * half:2 * VW * half + 6 * VW].rearrange("p b w -> p (b w)")
                        ins = pe.matmul(bank(6 + half, 6 * VW * j, 6 * VW * (j + 1)), smat[:, half, P * j:P * j + P], v6, start=True, stop=True)
                    ins.then_inc(S["av_done"], 1)

                for k in range(4):
                    for half in range(2):
                        u = g * 8 + (2 * k + half)
                        pe.wait_ge(S["exp_done"], u + 1)
                        mb = mblk.rearrange("p g h t -> p (g h t)")[:, bass.ds(g * 1024 + 512 * half, 512)]
                        pe.matmul(bank(half), selb[:, k, :], mb, start=True, stop=False)
                        pe.matmul(bank(half), av_part[:, 0].rearrange("p g t -> p (g t)")[:, bass.ds(g * P, P)],
                                  bmask[:, k, 4 * half:4 * half + 4, :].rearrange("p h t -> p (h t)"), start=False, stop=False)
                        pe.matmul(bank(half), identb[:], rep(neg[:], 4), start=False, stop=True).then_inc(S["ld_ready"], 1)
                        pe.wait_ge(S["prod_done"], u + 1)
                        if half == 0:
                            pe.wait_ge(S["kslot_ready"], g * 4 + (k + 1))
                            pe.wait_ge(S["qslot_ready"], g * 4 + (k + 1))
                        for jj in range(2):
                            r = slice(64 * half + 32 * jj, 64 * half + 32 * jj + 32)
                            ins = pe.matmul(PS[:, 2 + 2 * half + jj, 0:256], kslot[r, k % 2, :], qslot[r, k % 2],
                                            start=True, stop=True)
                        ins.then_inc(S["sc_ready"], 1)
                        if half == 1:
                            weigh(k, 0)
                        elif k:
                            weigh(k - 1, 1)
                weigh(3, 1)
            spread(0)
            pe.wait_ge(S["wq_ready"], 1)
            spread(1)
            for n in range(2):
                if n == 1:
                    pe.wait_ge(S["scale_ready"], 2)
                for c in range(NC):
                    w = slice(HID * n + P * c, HID * n + P * c + P)
                    ins = pe.transpose(bankb(6 + n)[:, P * c:P * c + P], wqb[:, w], identb[:])
                ins.then_inc(S["wq_turned"], 1)
            for nb in range(G4):
                pe.wait_ge(S["xq_ready"], nb // 2 + 1)
                if nb >= 2:
                    pe.wait_ge(S["xqT_kept"], nb - 1)
                for k in range(4):
                    b = 4 * nb + k
                    ins = pe.transpose(bankb(nb % 2)[:, P * k:P * k + P], xq[:, P * b:P * b + P], identb[:])
                ins.then_inc(S["xq_turned"], 1)
                pe.wait_ge(S["xqT_kept"], nb + 1)
                pe.wait_ge(S["wq_kept"], 2)
                for c in range(NC):
                    if nb >= 1:
                        pe.wait_ge(S["gelu_done"], NC * (nb - 1) + c + 1)
                    pe.matmul(bank(2 + c), w1q[:, P * c:P * c + P], xqT[:, 512 * nb:512 * nb + 512], start=True, stop=True).then_inc(S["ffn1_done"], 1)
            spread(2)
            for nb in range(G4):
                pe.wait_ge(S["hq_ready"], nb + 1)
                if nb >= 2:
                    pe.wait_ge(S["ffn2_added"], nb - 1)
                for k in range(4):
                    for c in range(NC):
                        t0 = 512 * nb + P * k
                        ins = pe.matmul(bank(nb % 2, P * k, P * k + P), hq[:, c, t0:t0 + P], w2q[:, c, :], start=(c == 0), stop=(c == NC - 1))
                ins.then_inc(S["ffn2_done"], 1)
            pe.wait_ge(S["ffn2_added"], G4)
            for g in range(G4 + 1):
                if g < G4:
                    pe.wait_ge(S["ln_done"], 2 * G4 + g + 1)
                    if g >= 2:
                        pe.wait_ge(S["x3T_kept"], g - 1)
                    for k in range(4):
                        ins = pe.transpose(bank(g % 2, P * k, P * k + P), xn[:, 4 * g + k, :], identf[:])
                    ins.then_inc(S["x3T_turned"], 1)
                if g >= 1:
                    m = g - 1
                    pe.wait_ge(S["x3T_kept"], m + 1)
                    if m >= 2:
                        pe.wait_ge(S["dsq_ready"], m - 1)
                    pe.matmul(bank(2 + m % 2), ones[:], xTsq[:, m % 2, :], start=True, stop=False)
                    for k in range(4):
                        b = 4 * m + k
                        ins = pe.matmul(bank(2 + m % 2, P * k, P * k + P), kT[:, P * b:P * b + P], xT2[:, m % 2, P * k:P * k + P],
                                        start=False, stop=(k == 3))
                    ins.then_inc(S["dsum_done"], 1)
            for n in range(2 * E):
                pe.wait_ge(raw_in[n % 2], 16 * (n // 2 + 1))
                if n >= 2:
                    pe.wait_ge(S["raw_kept"], n - 1)
                for c in range(NC):
                    ins = pe.transpose(bank(4 + n % 2, P * c, P * c + P), wraw[:, n % 2, P * c:P * c + P], identf[:])
                ins.then_inc(S["raw_turned"], 1)
            pe.wait_ge(S["track_done"], P)
            pe.transpose(bank(0, 0, B), ee[:, 0:P], identf[0:B, 0:B])
            pe.transpose(bank(0, B, 2 * B), ee[:, 1:P + 1], identf[0:B, 0:B]).then_inc(S["e_turned"], 1)
            for g in range(G4):
                pe.wait_ge(S["path_ready"], g + 1)
                if g >= 2:
                    pe.wait_ge(S["expanded_added"], g - 1)
                for k in range(4):
                    b = 4 * g + k
                    ins = pe.matmul(bank(1 + g % 2, P * k, P * k + P), path[:, b, :], cs[:, b, :], start=True, stop=True)
                ins.then_inc(S["expanded"], 1)
            pe.wait_ge(S["expanded_added"], G4)
            for g in range(G4 + 1):
                if g < G4:
                    pe.wait_ge(S["ln_done"], 3 * G4 + g + 1)
                    if g >= 2:
                        pe.wait_ge(S["x4_kept"], g - 1)
                    for k in range(4):
                        ins = pe.transpose(bank(g % 2, P * k, P * k + P), x4[:, 4 * g + k, :], identf[:])
                    ins.then_inc(S["x4_turned"], 1)
                if g >= 1:
                    pe.wait_ge(S["x4_kept"], g)
                    for k in range(4):
                        b = 4 * (g - 1) + k
                        ins = pe.matmul(bank(2, E * b, E * b + E), x4f[:, (g - 1) % 2, P * k:P * k + P], small_t[:, 84:92], start=True, stop=True)
                    ins.then_inc(S["logits_done"], 1)
            for n in range(32):
                pe.wait_ge(S["count_ready"], n + 1)
                pe.matmul(bank(3, 0, 1), ones[:], sel[:, 0:1], start=True, stop=True).then_inc(S["count_all"], 1)
            pe.wait_ge(S["gates_ready"], 1)
            pe.wait_ge(S["b2_in"], 64)
            for g in range(G4 + 1):
                if g < G4:
                    if g >= 2:
                        pe.wait_ge(S["gt_kept"], g - 1)
                    pe.transpose(PS[0:32, 4 + g % 2, 0:P], gts[:, 4 * g:4 * g + 4, :].rearrange("p b e -> p (b e)"), identf[:]).then_inc(S["gt_turned"], 1)
                if g >= 1:
                    m = g - 1
                    pe.wait_ge(S["gt_kept"], m + 1)
                    if m >= 2:
                        pe.wait_ge(S["gb_added"], m - 1)
                    pe.matmul(bank(6 + m % 2), gtT[:, m % 2, :], b2blk[:].rearrange("p k d -> p (k d)"), start=True, stop=True).then_inc(S["gb_done"], 1)
            pe.wait_ge(S["x4_split"], G4)
            pe.wait_ge(S["w_split"], 2 * E)

            def hidden(blk, e):
                xw = slice(512 * blk, 512 * blk + 512) if isinstance(blk, int) else bass.ds(blk * 512, 512)
                for c in range(NC):
                    pe.wait_ge(S["h_gelu"], blk * (E * NC) + (e * NC + c + 1))
                    pe.matmul(bank(c), w1h[:, e, c, :], x4h[:, xw], start=True, stop=False)
                    pe.matmul(bank(c), w1h[:, e, c, :], x4l[:, xw], start=False, stop=False)
                    pe.matmul(bank(c), w1l[:, e, c, :], x4h[:, xw], start=False, stop=True).then_inc(S["h_ready"], 1)

            def outputs(blk, e):
                pe.wait_ge(S["y_added"], blk * E + (e + 1))
                for c in range(NC):
                    pe.wait_ge(S["h_low_even" if c % 2 == 0 else "h_low_odd"], blk * (2 * E) + (2 * e + c // 2 + 3))
                    for k in range(4):
                        o = bank(4 + e % 2, P * k, P * k + P)
                        t = slice(P * k, P * k + P)
                        pe.matmul(o, hh[:, e % 2, c, t], w2h[:, e, c, :], start=(c == 0 and k == 0), stop=False, skip_group_check=True)
                        pe.matmul(o, hh[:, e % 2, c, t], w2l[:, e, c, :], start=False, stop=False, skip_group_check=True)
                        ins = pe.matmul(o, hl[:, e % 2, c, t], w2h[:, e, c, :], start=False, stop=(c == NC - 1), skip_group_check=True)
                ins.then_inc(S["y_ready"], 1)

            hidden(0, 0)
            with pe.Fori(0, G4 - 1) as blk:
                for e in range(1, E):
                    hidden(blk, e)
                    outputs(blk, e - 1)
                hidden(blk + 1, 0)
                outputs(blk, E - 1)
            for e in range(1, E):
                hidden(G4 - 1, e)
                outputs(G4 - 1, e - 1)
            outputs(G4 - 1, E - 1)


_INS = ['x', 'ctx_1024', 'g_xattn', 'g_ffn', 'L0_xattn_ifgate_w', 'L0_xattn_ifgate_b', 'L0_xattn_outnorm_w', 'L0_ffn_W1',
        'L0_ffn_b1', 'L0_ffn_W2', 'L0_ffn_b2', 'L1_ffn_gate_weight', 'L1_ffn_w1', 'L1_ffn_b1', 'L1_ffn_w2', 'L1_ffn_b2']
_OUTS = [((32, 128, 128), 'float32')]


def kernel(**inputs):
    import numpy as _np
    import concourse.bacc as _bacc
    from concourse import mybir as _mybir
    from concourse.bass_utils import run_bass_kernel_spmd as _run

    nc = _bacc.Bacc("TRN2", target_bir_lowering=False, num_devices=1)
    arrays, args = {}, []
    for name in _INS:
        a = _np.ascontiguousarray(inputs[name])
        arrays[f"in_{name}_dram"] = a
        args.append(nc.dram_tensor(f"in_{name}_dram", a.shape, _mybir.dt.from_np(a.dtype), kind="ExternalInput").ap())
    for i, (shape, dtype) in enumerate(_OUTS):
        dt = _mybir.dt.from_np(_np.dtype(dtype))
        args.append(nc.dram_tensor(f"out_{i}_dram", shape, dt, kind="ExternalOutput").ap())
    program(nc, *args)
    r = _run(nc, [arrays], core_ids=[0])
    got = tuple(r.results[0][f"out_{i}_dram"] for i in range(len(_OUTS)))
    return got[0]
```

```python
from contextlib import ExitStack

import concourse.bass as bass
import concourse.mybir as mybir

F32 = mybir.dt.float32
BF16 = mybir.dt.bfloat16
I32 = mybir.dt.int32
U32 = mybir.dt.uint32
ALU = mybir.AluOpType
ACT = mybir.ActivationFunctionType
AX = mybir.AxisListType.X

P = 128
B = 32
D = 128
NH, DH = 8, 16
HID = 512
NC = HID // P
E = 8
G4 = B // 4
TOK = B * P
KTH = 4 * 128 * 6
MAGIC = 12582912.0
BIG = 1e30
LN_EPS, NORM_EPS, BACKEND_EPS = 1e-5, 1e-6, 5e-5
GATE_CAP = 15.0
VW = DH + 1
RC = 32
NRC = P // RC
SHIFT = [31] + [29 - 2 * n for n in range(15)] + [0]
ROUNDS = len(SHIFT)
RW = P + 1


def program(nc, x, ctx_, g_x, g_f, if_w, if_b, on_w, a_w1, a_b1, a_w2, a_b2, gate_w, m_w1, m_b1, m_w2, m_b2, out):
    with ExitStack() as stack:
        def sb(name, shape, dt=F32):
            return stack.enter_context(nc.sbuf_tensor(name, shape, dt))

        def sem(name):
            return stack.enter_context(nc.semaphore(name))

        def dram(name, shape, dt):
            return nc.dram_tensor(name, shape, dt)

        xs = sb("xs", [P, B, D])
        cs = sb("cs", [P, B, D])
        xn_w1 = sb("xn_w1", [P, B * D])
        kT_w2 = sb("kT_w2", [P, B * D])
        A = sb("A", [P, 16384])
        Bm = sb("Bm", [P, 14848])
        slab = sb("slab", [P, 2048])
        slab2 = sb("slab2", [P, 512])
        PS = stack.enter_context(nc.psum_tensor("PS", [P, 8, 512], F32))

        xn = xn_w1[:].rearrange("p (b d) -> p b d", b=B)
        kT = kT_w2

        qT = A[:, 0:4096]
        bmask = A[:, 8192:10240].bitcast(BF16).rearrange("p (k h t) -> p k h t", k=4, h=NH)
        av = A[:, 10240:12288].rearrange("p (w g t) -> p w g t", w=2, g=G4)
        av_res = A[:, 12288:14336].rearrange("p (w g t) -> p w g t", w=2, g=G4)
        av_cut = A[:, 14336:15360].bitcast(BF16).rearrange("p (w g t) -> p w g t", w=2, g=G4)
        av_part = A[:, 15360:16384].bitcast(BF16).rearrange("p (w g t) -> p w g t", w=2, g=G4)
        vaug = Bm[:, 0:4352].rearrange("p (b w) -> p b w", b=B)
        oall = Bm[:, 4352:8704].rearrange("p (b w) -> p b w", b=B)
        decay = Bm[:, 8704:9728].rearrange("p (s c) -> p s c", s=2)
        smat = Bm[:, 9728:10752].rearrange("p (s c) -> p s c", s=2)
        mblk = Bm[:, 10752:14848].bitcast(BF16).rearrange("p (g h t) -> p g h t", g=G4, h=NH)
        osq = A[:, 4096:8192]
        hid = A[:, 0:16384].rearrange("p (c t) -> p c t", c=NC)
        hq = Bm[:, 0:8192].bitcast(BF16).rearrange("p (c t) -> p c t", c=NC)
        xq = Bm[:, 8192:10240].bitcast(BF16)
        xqT = Bm[:, 10240:12288].bitcast(BF16)
        xT2 = Bm[:, 0:1024].rearrange("p (s t) -> p s t", s=2)
        xTsq = Bm[:, 1024:2048].rearrange("p (s t) -> p s t", s=2)
        dsq = Bm[:, 2048:6144].rearrange("p (b j) -> p b j", b=B)
        dist = Bm[:, 6144:10240].rearrange("p (b j) -> p b j", b=B)
        dring = A[:, 0:8192].rearrange("p (s r j) -> p s r j", s=2, r=RC)
        kb = A[:, 8192:16384].bitcast(BF16).rearrange("p (i j) -> p i j", i=P)
        rring = Bm[:, 0:2 * (RC + 1) * RW].rearrange("p (s r j) -> p s r j", s=2, r=RC + 1)
        o0 = 2 * (RC + 1) * RW
        r9 = Bm[:, o0:o0 + 9 * RW].rearrange("p (r j) -> p r j", r=9)
        o0 += 9 * RW
        ch_m = Bm[:, o0:o0 + 1024].rearrange("p (r j) -> p r j", r=8)
        ch_g = Bm[:, o0 + 1024:o0 + 2048].rearrange("p (r j) -> p r j", r=8)
        ch_k = Bm[:, o0 + 2048:o0 + 3072].rearrange("p (r j) -> p r j", r=8)
        ch_s = Bm[:, o0 + 3072:o0 + 4096].rearrange("p (r j) -> p r j", r=8)
        o0 += 4096
        ch_d = Bm[:, o0:o0 + 512].bitcast(BF16).rearrange("p (r j) -> p r j", r=8)
        scanmask = Bm[:, o0 + 512:o0 + 1024].bitcast(BF16).rearrange("p (r j) -> p r j", r=8)
        path = Bm[:, 0:4096].rearrange("p (b j) -> p b j", b=B)
        x4 = A[:, 0:4096].rearrange("p (b d) -> p b d", b=B)
        x4h = A[:, 4096:6144].bitcast(BF16)
        x4l = A[:, 6144:8192].bitcast(BF16)
        x4f = A[:, 8192:9216].rearrange("p (s t) -> p s t", s=2)
        hf = A[:, 9216:11264].rearrange("p (s t) -> p s t", s=4)
        hh = A[:, 11264:13312].bitcast(BF16).rearrange("p (s c t) -> p s c t", s=2, c=NC)
        hl = A[:, 13312:15360].bitcast(BF16).rearrange("p (s c t) -> p s c t", s=2, c=NC)
        w1h = xn_w1[:, 0:2048].bitcast(BF16).rearrange("p (e c t) -> p e c t", e=E, c=NC)
        w1l = xn_w1[:, 2048:4096].bitcast(BF16).rearrange("p (e c t) -> p e c t", e=E, c=NC)
        w2h = kT_w2[:, 0:2048].bitcast(BF16).rearrange("p (e c t) -> p e c t", e=E, c=NC)
        w2l = kT_w2[:, 2048:4096].bitcast(BF16).rearrange("p (e c t) -> p e c t", e=E, c=NC)

        identf = sb("identf", [P, P])
        identb = sb("identb", [P, P], BF16)
        tri = sb("tri", [P, P])
        neg = sb("neg", [P, P], BF16)
        iota2 = sb("iota2", [P, P])
        ones = sb("ones", [P, P])
        selb = slab2[:, 0:256].bitcast(BF16).rearrange("p (k t) -> p k t", k=4)
        pidx = sb("pidx", [P, 8], I32)
        hidx = sb("hidx", [P, 8], I32)
        hidf = sb("hidf", [P, 8])
        pm = sb("pm", [P, 16])
        hneg = sb("hneg", [P, 8])
        hpos = sb("hpos", [P, 8])
        cst = sb("cst", [P, 8])
        mhalf = sb("mhalf", [P, 32])
        bns = sb("bns", [P, B, 6])
        lnt = sb("lnt", [P, 8, B])
        ifw_n = Bm[0:16, 8704:9088]
        ifb_b = sb("ifb_b", [P, 16])
        onw_b = sb("onw_b", [P, D])
        tgr = sb("tgr", [P, 4])
        tg = sb("tg", [P, 4])
        ab1_n = Bm[0:NC, 9088:9216]
        ab2_b = sb("ab2_b", [P, D])
        gw_n = Bm[0:E, 9216:9344]
        mb1_n = Bm[0:E * NC, 9344:9472]
        b2blk = sb("b2blk", [32, 4, D])
        small_t = sb("small_t", [P, 92])
        wkv = sb("wkv", [P, 16])
        pre = slab[:, 0:512].rearrange("p (b w) -> p b w", b=B)
        nlf = slab[:, 512:768].rearrange("p (b h) -> p b h", b=B)
        a_tok = slab[:, 768:1024].rearrange("p (b h) -> p b h", b=B)
        ncs = slab[:, 1024:1280].rearrange("p (b h) -> p b h", b=B)
        expnm = sb("expnm", [P, B, NH])
        fin = slab[:, 1280:2048].rearrange("p (k m) -> p k m", k=3)
        kslot = slab2[:, 256:512].rearrange("p (s t) -> p s t", s=2)
        qslot = slab[:, 0:512].rearrange("p (s r t) -> p s r t", s=2, r=2)
        mm = sb("mm", [P, 24])
        gq = sb("gq", [2, 8])
        qs = sb("qs", [P, 40])
        w1n = xn_w1[:, 0:512]
        w2n = xn_w1[:, 512:1024]
        wtmp = xn_w1[:, 1024:2048]
        wqb = xn_w1[:, 3584:4096].bitcast(BF16)
        w1q = slab2[:, 0:256].bitcast(BF16)
        w2q = slab2[:, 256:512].bitcast(BF16).rearrange("p (c d) -> p c d", c=NC)
        aa = sb("aa", [P, B])
        ee = sb("ee", [B, P + 4])
        rowm = sb("rowm", [B, P])
        pathm = Bm[:, 4096:8192].rearrange("p (b j) -> p b j", b=B)
        hmm = sb("hmm", [P, 2, B])
        selw = A[:, 16000:16384].bitcast(BF16).rearrange("p (k n) -> p k n", k=3)
        eT = sb("eT", [P, 2, B])
        aa_tmp = Bm[:, 10752:14848].rearrange("p (b d) -> p b d", b=B)
        wraw = slab[:, 0:1024].rearrange("p (s c) -> p s c", s=2)
        wcp = slab[:, 1024:2048].rearrange("p (s c) -> p s c", s=2)
        lg = A[:, 15360:15616].rearrange("p (b e) -> p b e", b=B)
        gts = A[:, 15616:15872].rearrange("p (b e) -> p b e", b=B)
        gtT = A[0:32, 15872:16128].rearrange("p (s t) -> p s t", s=2)
        sel = sb("sel", [P, 16])
        seli = sb("seli", [P, 16], U32)
        key, flip, top, step = (seli[:, k:k + 1] for k in range(4))
        cand, digit = seli[:, 4:7], seli[:, 8:11]
        ykept = Bm[:, 0:4096].rearrange("p (e c) -> p e c", e=E)
        gbias = Bm[:, 4096:8192]

        d_dram = dram("d_scratch", (B, P, P), F32).ap()
        r_dram = dram("r_scratch", (B, RW, RW), F32).ap()
        k_dram = dram("k_scratch", (B, P, P), BF16).ap()


        S = {n: sem(n) for n in (
            "pool_step", "dve_step", "act_step",
            "consts_made", "small_in", "b2_in", "small_turned", "small_kept", "tg_in_ready", "tg_ready",
            "csq_done", "bn_done", "ln_sqrt", "ln_done", "q_turned", "c_turned", "q_kept", "k_kept",
            "gates_summed", "gates_biased", "gates_capped", "nlf_ready", "cumsum_done", "a_ready", "a_turned",
            "m_ready", "m_turned", "m_tok_ready", "expnm_ready", "parts_ready", "mblk_ready", "vaug_ready",
            "kslot_ready", "qslot_ready", "ld_ready", "sc_ready", "exp_done", "prod_done", "av_done", "o_kept",
            "gain_ready", "norm_step", "onto_step", "osq_done", "osum_done", "osqrt_done", "x2_ready",
            "mm_ready", "mm_turned", "mm_global", "mm_spread", "scale_ready", "x_scaled", "xq_ready",
            "xq_turned", "xqT_kept", "aw_in", "w_scaled", "wq_ready", "wq_turned", "wq_kept",
            "ffn1_done", "gelu_done", "h_scaled", "hq_ready", "b2_added", "ffn2_done", "ffn2_added",
            "x3T_turned", "x3T_kept", "dsum_done", "dsq_ready", "dist_ready", "d_out", "row_done",
            "r_out", "r9_in", "left_ready", "k_made", "k_cut", "k_out", "k_in",
            "track_done", "e_turned", "e_kept", "path_ready", "expanded", "expanded_added",
            "raw_turned", "raw_kept", "w_split",
            "x4_turned", "x4_kept", "x4_split", "logits_done", "count_ready", "count_all", "gates_ready", "late_added", "bias_added", "gb_kept",
            "gt_turned", "gt_kept", "gb_done", "gb_added", "h_ready", "h_gelu", "h_high", "h_low_even", "h_low_odd", "y_ready",
            "y_added", "stored")}
        x_in = [sem(f"x_in{c}") for c in range(4)]
        ctx_in = [sem(f"ctx_in{c}") for c in range(4)]
        d_in = [sem(f"d_in{c}") for c in range(2)]
        raw_in = [sem(f"raw_in{c}") for c in range(2)]

        def bank(n, a=0, b=512):
            return PS[:, n, a:b]

        def bankb(n):
            return PS[:, n, 0:256].bitcast(BF16)

        def g4(ap, g):
            return ap[:, 4 * g:4 * g + 4]

        def four(ap):
            return ap.rearrange("p (k t) -> p k t", k=4)

        def rep(ap, n):
            return ap.unsqueeze(1).to_broadcast([ap.shape[0], n, ap.shape[1]])

        def heads(m):
            return oall[:, bass.ds(m * 4, 4), :].rearrange("p b (h w) -> p (b h) w", h=NH)

        def last(ap, n):
            return ap.unsqueeze(2).to_broadcast([ap.shape[0], ap.shape[1], n])

        def raw_load(pool, n):
            if n < E:
                dst, src = four(wraw[:, n % 2, :]), m_w1[n].rearrange("(c p) d -> p c d", c=NC)
            else:
                dst, src = wraw[:, n % 2, :], m_w2[n - E]
            pool.dma_start(dst, src).then_inc(raw_in[n % 2], 16)

        def steps_out(sp, c):
            sp.wait_ge(S["k_cut"], c + 1)
            for q in range(4):
                sp.dma_start(k_dram[:, RC * c + 8 * q:RC * c + 8 * q + 8], ch_d[32 * q:32 * q + 32]).then_inc(S["k_out"], 16)
            sp.wait_ge(S["k_out"], 64 * (c + 1))
            sp.dma_start(kb[0:B, RC * c:RC * c + RC], k_dram[:, RC * c:RC * c + RC]).then_inc(S["k_in"], 16)

        def back_steps(dve, link, c):
            dve.wait_ge(S["r9_in"], 64 * (c + 1))
            if c >= 1:
                dve.wait_ge(S["k_made"], c)
            link(dve.tensor_tensor(ch_m, r9[:, 0:8, 0:P], r9[:, 0:8, 1:RW], ALU.min))
            dve.tensor_tensor(ch_g, r9[:, 0:8, 0:P], r9[:, 0:8, 1:RW], ALU.is_le)
            dve.tensor_tensor(ch_m, r9[:, 1:9, 0:P], ch_m, ALU.is_ge).then_inc(S["left_ready"], 1)
            dve.wait_ge(S["k_made"], c + 1)
            fl = lambda v: v.rearrange("p r j -> p (r j)")
            link(dve.tensor_tensor_scan(fl(ch_s), fl(scanmask), fl(ch_k), 0.0, ALU.mult, ALU.max))
            if c >= 1:
                dve.wait_ge(S["k_out"], 64 * c)
            dve.tensor_copy(ch_d[:, :, 0:1], ch_s[:, :, 0:1])
            dve.tensor_tensor(ch_d[:, :, 1:P], ch_s[:, :, 1:P], ch_s[:, :, 0:P - 1], ALU.subtract).then_inc(S["k_cut"], 1)

        block = stack.enter_context(nc.Block())

        @block.sync
        def _(sp):
            small = [(ifw_n, if_w), (ifb_b[:], if_b.partition_broadcast(P)),
                     (onw_b[:], on_w.partition_broadcast(P)),
                     (tgr[:, 0:2], g_x.partition_broadcast(P)), (tgr[:, 2:4], g_f.partition_broadcast(P)),
                     (ab1_n, a_b1.rearrange("(c p) -> c p", c=NC)), (ab2_b[:], a_b2.partition_broadcast(P)),
                     (gw_n, gate_w), (mb1_n, m_b1.rearrange("e (c p) -> (e c) p", c=NC))]
            for c in range(4):
                sp.dma_start(xs[:, 8 * c:8 * c + 8], x[8 * c:8 * c + 8].rearrange("b t d -> t b d")).then_inc(x_in[c], 16)
                sp.dma_start(cs[:, 8 * c:8 * c + 8], ctx_[8 * c:8 * c + 8].rearrange("b t d -> t b d")).then_inc(ctx_in[c], 16)
                if c == 0:
                    for dst, src in small:
                        sp.dma_start(dst, src).then_inc(S["small_in"], 16)
            sp.wait_ge(S["consts_made"], 1)
            for k in range(4):
                sp.dma_start(b2blk[8 * k:8 * k + 8, k, :], m_b2).then_inc(S["b2_in"], 16)
            sp.wait_ge(S["q_turned"], G4)
            sp.dma_start(w1n.rearrange("p (c d) -> p c d", c=NC), a_w1.rearrange("(c p) d -> p c d", c=NC)).then_inc(S["aw_in"], 16)
            sp.dma_start(w2n, a_w2).then_inc(S["aw_in"], 16)
            for g in range(G4):
                sp.wait_ge(S["dist_ready"], g + 1)
                sp.dma_start(d_dram[4 * g:4 * g + 4].rearrange("b i j -> i b j"), g4(dist, g)).then_inc(S["d_out"], 16)
            sp.wait_ge(S["d_out"], 16 * G4)
            for c in range(2):
                sp.dma_start(dring[0:B, c], d_dram[:, RC * c:RC * c + RC]).then_inc(d_in[c], 16)
            for c in range(NRC):
                sp.wait_ge(S["row_done"], RC * (c + 1))
                lo = 0 if c == 0 else 1
                sp.dma_start(r_dram[:, RC * c + lo:RC * c + RC + 1], rring[0:B, c % 2, lo:RC + 1]).then_inc(S["r_out"], 16)
                if c + 2 < NRC:
                    sp.dma_start(dring[0:B, c % 2], d_dram[:, RC * (c + 2):RC * (c + 3)]).then_inc(d_in[c % 2], 16)
                sp.wait_ge(S["r_out"], 16 * (c + 1))
                if c >= 1:
                    sp.wait_ge(S["left_ready"], c)
                for q in range(4):
                    rows = r_dram[:, RC * c + 8 * q:RC * c + 8 * q + 9]
                    sp.dma_start(r9[32 * q:32 * q + 32], rows).then_inc(S["r9_in"], 16)
                if c >= 1:
                    steps_out(sp, c - 1)
            steps_out(sp, NRC - 1)
            for blk in range(2):
                sp.wait_ge(S["bias_added"], blk + 1)
                sp.dma_start(out[4 * blk:4 * blk + 4].rearrange("b t d -> t b d"), g4(xs, blk)).then_inc(S["stored"], 16)
            with sp.Fori(2, G4) as blk:
                sp.wait_ge(S["y_added"], blk * E + (E + 2))
                sp.dma_start(out[bass.ds(blk * 4, 4)].rearrange("b t d -> t b d"),
                             xs[:, bass.ds(blk * 4, 4)]).then_inc(S["stored"], 16)
            sp.wait_ge(S["stored"], 16 * G4)

        @block.gpsimd
        def _(pool):
            steps = [0]

            def link(ins):
                steps[0] += 1
                ins.then_inc(S["pool_step"], 1)
                pool.wait_ge(S["pool_step"], steps[0])

            pool.sem_inc(S["h_low_even"], 2)
            pool.memset(identf[:], 0.0)
            pool.memset(identb[:], 0.0)
            pool.memset(tri[:], 1.0)
            pool.memset(neg[:], 0.0)
            pool.memset(ones[:], 1.0)
            pool.iota(pidx[:, 0:1], [[0, 1]], base=0, channel_multiplier=1)
            pool.iota(hidx[:], [[1, 8]], base=0, channel_multiplier=0)
            pool.iota(iota2[:], [[2, P]], base=0, channel_multiplier=0, allow_small_or_imprecise_dtypes=True)
            pool.memset(mhalf[:], -0.5)
            link(pool.memset(b2blk[:], 0.0))
            line = [[1, P]]
            pool.affine_select(out=identf[:], in_=identf[:], compare_op=ALU.not_equal, fill=1.0, base=0, pattern=line, channel_multiplier=-1)
            pool.affine_select(out=identb[:], in_=identb[:], compare_op=ALU.not_equal, fill=1.0, base=0, pattern=line, channel_multiplier=-1)
            pool.affine_select(out=tri[:], in_=tri[:], compare_op=ALU.is_ge, fill=0.0, base=0, pattern=line, channel_multiplier=-1)
            pool.affine_select(out=neg[:], in_=neg[:], compare_op=ALU.is_ge, fill=-BIG, base=0, pattern=line, channel_multiplier=-1).then_inc(S["consts_made"], 1)
            for c in range(4):
                pool.wait_ge(ctx_in[c], 16)
            v4 = vaug.rearrange("p b (h w) -> p (b h) w", h=NH)
            pool.memset(v4[:, :, DH:VW], 1.0)
            pool.tensor_scalar(v4[:, :, 0:DH], cs[:].rearrange("p b (h w) -> p (b h) w", h=NH), 1.0, 0.0, ALU.mult, ALU.add).then_inc(S["vaug_ready"], 1)
            pool.wait_ge(S["k_kept"], G4)
            pool.wait_ge(S["gain_ready"], 1)

            def slot_keys(g, k):
                pool.wait_ge(S["sc_ready"], g * 8 + (2 * k + 2))
                pool.tensor_copy(kslot[:, k % 2, :], kT[:, bass.ds(g * 512 + k * P, P)]).then_inc(S["kslot_ready"], 1)

            def squares(m):
                pool.wait_ge(S["o_kept"], m * 8 + 10)
                o3 = heads(m)[:, :, 0:DH]
                pool.tensor_tensor(osq[:, bass.ds(m * 512, 512)].rearrange("p (m w) -> p m w", w=DH), o3, o3, ALU.mult).then_inc(S["osq_done"], 1)

            def chain(ins, m, i):
                ins.then_inc(S["onto_step"], 1)
                pool.wait_ge(S["onto_step"], m * 3 + i)

            def normed(m):
                pool.wait_ge(S["osum_done"], m + 1)
                t = osq[:, bass.ds(m * 512, 512)]
                f = fin[:, 1, bass.ds(m * 32, 32)]
                chain(pool.tensor_tensor(f, f, mhalf[:], ALU.pow), m, 1)
                chain(pool.tensor_tensor(t.rearrange("p (m w) -> p m w", w=DH), heads(m)[:, :, 0:DH], last(f, DH), ALU.mult), m, 2)

            def onto(m):
                t4 = four(osq[:, bass.ds(m * 512, 512)])
                chain(pool.tensor_tensor(t4, t4, rep(onw_b[:], 4), ALU.mult), m, 3)
                row = xs[:, bass.ds(m * 4, 4), :]
                pool.tensor_tensor(row, row, t4, ALU.add).then_inc(S["x2_ready"], 1)

            for g in range(G4):
                slot_keys(g, 0)
                slot_keys(g, 1)
                if g:
                    squares(g - 1)
                slot_keys(g, 2)
                if g:
                    normed(g - 1)
                slot_keys(g, 3)
                if g:
                    onto(g - 1)
            pool.wait_ge(S["scale_ready"], 2)
            pool.wait_ge(S["ln_done"], 2 * G4)
            pool.tensor_tensor(xs[:], xs[:], rep(ab2_b[:], B), ALU.add).then_inc(S["b2_added"], 1)
            raw_load(pool, 0)
            raw_load(pool, 1)
            pool.wait_ge(S["dsum_done"], G4)
            for n in range(2 * E):
                wh, wl = (w1h, w1l) if n < E else (w2h, w2l)
                pool.wait_ge(S["raw_kept"], n + 1)
                if n + 2 < 2 * E:
                    raw_load(pool, n + 2)
                src = four(wcp[:, n % 2, :])
                link(pool.tensor_scalar(wh[:, n % E], src, 1.0, 0.0, ALU.mult, ALU.add))
                pool.tensor_tensor(wl[:, n % E], src, wh[:, n % E], ALU.subtract).then_inc(S["w_split"], 1)
            link(pool.memset(scanmask, 1.0))
            link(pool.memset(scanmask[:, :, 0:1], 0.0))
            for c in range(NRC):
                pool.wait_ge(S["left_ready"], c + 1)
                link(pool.tensor_tensor(ch_k, rep(iota2[:], 8), ch_g, ALU.subtract))
                pool.tensor_tensor(ch_k, ch_k, ch_m, ALU.mult).then_inc(S["k_made"], 1)
            def low(blk, e, c):
                pool.wait_ge(S["h_high"], blk * (E * NC) + (e * NC + c + 1))
                pool.tensor_tensor(hl[:, e % 2, c, :], hf[:, c, :], hh[:, e % 2, c, :], ALU.subtract)\
                    .then_inc(S["h_low_even" if c % 2 == 0 else "h_low_odd"], 1)

            for e in range(E):
                for c in range(NC):
                    low(0, e, c)
            with pool.Fori(1, G4) as blk:
                for e in range(E):
                    for c in range(0, NC, 2):
                        low(blk, e, c)

        @block.scalar
        def _(act):
            steps = [0]

            def link(ins):
                steps[0] += 1
                ins.then_inc(S["act_step"], 1)
                act.wait_ge(S["act_step"], steps[0])

            def ln(n):
                for h in range(2):
                    act.wait_ge(S["bn_done"], 2 * n + h + 1)
                    act.activation(lnt[:, 5, 16 * h:16 * h + 16], lnt[:, 4, 16 * h:16 * h + 16], ACT.Sqrt, bias=cst[:, 0:1]).then_inc(S["ln_sqrt"], 1)

            act.sem_inc(S["exp_done"], 2)
            act.sem_inc(S["o_kept"], 2)
            act.sem_inc(S["h_gelu"], 4)
            act.wait_ge(S["tg_in_ready"], 1)
            act.activation(tg[:], tgr[:], ACT.Tanh).then_inc(S["tg_ready"], 1)
            for c in range(4):
                act.wait_ge(ctx_in[c], 16)
            act.activation(aa_tmp, cs[:], ACT.Square).then_inc(S["csq_done"], 1)
            ln(0)
            for g in range(G4):
                act.wait_ge(S["c_turned"], g + 1)
                act.activation(kT[:, 512 * g:512 * g + 512], bank(2 + g % 2), ACT.Copy).then_inc(S["k_kept"], 1)
            act.wait_ge(S["gates_biased"], 1)
            act.activation(pre, pre, ACT.Tanh, scale=1.0 / GATE_CAP).then_inc(S["gates_capped"], 1)
            act.wait_ge(S["gates_capped"], 1)
            link(act.activation(nlf, pre[:, :, NH:2 * NH], ACT.Exp, scale=-GATE_CAP))
            act.activation(nlf, nlf, ACT.Ln, bias=cst[:, 3:4]).then_inc(S["nlf_ready"], 1)
            act.wait_ge(S["m_tok_ready"], 1)
            act.activation(expnm[:], expnm[:], ACT.Exp).then_inc(S["expnm_ready"], 1)
            act.wait_ge(S["scale_ready"], 1)
            act.activation(wtmp[:, 0:HID], w1n, ACT.Identity, scale=qs[:, 2:3], bias=cst[:, 2:3])
            act.activation(wtmp[:, HID:2 * HID], w2n, ACT.Identity, scale=qs[:, 3:4], bias=cst[:, 2:3]).then_inc(S["w_scaled"], 1)
            with act.Fori(0, G4) as g:
                def keep(m):
                    act.wait_ge(S["av_done"], g * 8 + (m + 3))
                    o = 2 * VW * (m % 2)
                    own = PS[:, 6 + m % 2, o:o + 4 * 7 * VW].rearrange("p (j w) -> p j w", j=4)[:, :, 0:VW]
                    act.activation(oall[:, bass.ds(g * 4 + m // 2, 1), 4 * VW * (m % 2):4 * VW * (m % 2) + 4 * VW]
                                   .rearrange("p b (j w) -> p (b j) w", j=4), own, ACT.Copy).then_inc(S["o_kept"], 1)

                for k in range(4):
                    for half in range(2):
                        u = g * 8 + (2 * k + half)
                        act.wait_ge(S["ld_ready"], u + 1)
                        act.wait_ge(S["prod_done"], u + 1)
                        act.activation(decay[:, half, :], bank(half), ACT.Exp).then_inc(S["exp_done"], 1)
                        if 2 * k + half:
                            keep(2 * k + half - 1)
                keep(7)
            act.wait_ge(S["osum_done"], G4)
            f = fin[:, 1, 32 * (G4 - 1):32 * G4]
            act.activation(f, f, ACT.Sqrt).then_inc(S["osqrt_done"], 1)
            ln(1)
            act.wait_ge(S["scale_ready"], 2)
            for c in range(4):
                act.wait_ge(S["ln_done"], G4 + 2 * c + 2)
                v = xn[:, 8 * c:8 * c + 8]
                act.activation(v, v, ACT.Identity, scale=qs[:, 8:9], bias=cst[:, 2:3]).then_inc(S["x_scaled"], 1)
            for n in range(2):
                act.wait_ge(S["wq_turned"], n + 1)
                dst = w1q if n == 0 else w2q.rearrange("p c d -> p (c d)")
                act.activation(dst, bankb(5 + n), ACT.Copy).then_inc(S["wq_kept"], 1)
            for nb in range(G4):
                act.wait_ge(S["xq_turned"], nb + 1)
                act.activation(xqT[:, 512 * nb:512 * nb + 512], bankb(nb % 2), ACT.Copy).then_inc(S["xqT_kept"], 1)
                for c in range(NC):
                    act.wait_ge(S["ffn1_done"], NC * nb + c + 1)
                    act.activation(hid[:, c, 512 * nb:512 * nb + 512], bank(2 + c), ACT.Gelu, scale=qs[:, 12:13],
                                   bias=small_t[:, 80 + c:81 + c]).then_inc(S["gelu_done"], 1)
            act.wait_ge(S["scale_ready"], 3)
            for nb in range(G4):
                v = hid[:, :, 512 * nb:512 * nb + 512]
                act.activation(v, v, ACT.Identity, scale=qs[:, 16:17], bias=cst[:, 2:3]).then_inc(S["h_scaled"], 1)
            ln(2)
            for g in range(G4 + 1):
                if g < G4:
                    act.wait_ge(S["x3T_turned"], g + 1)
                    if g >= 2:
                        act.wait_ge(S["dsum_done"], g - 1)
                    act.activation(xT2[:, g % 2, :], bank(g % 2), ACT.Copy, scale=-2.0)
                    act.activation(xTsq[:, g % 2, :], bank(g % 2), ACT.Square).then_inc(S["x3T_kept"], 1)
                if g >= 1:
                    act.wait_ge(S["dsq_ready"], g)
                    act.activation(g4(dist, g - 1), g4(dsq, g - 1), ACT.Sqrt).then_inc(S["dist_ready"], 1)
            for n in range(2 * E):
                if n >= 2:
                    act.wait_ge(S["w_split"], n - 1)
                act.wait_ge(S["raw_turned"], n + 1)
                act.activation(wcp[:, n % 2, :], bank(4 + n % 2), ACT.Copy).then_inc(S["raw_kept"], 1)
            ln(3)
            for g in range(G4):
                act.wait_ge(S["x4_turned"], g + 1)
                if g >= 2:
                    act.wait_ge(S["logits_done"], g - 1)
                    act.wait_ge(S["x4_split"], g - 1)
                act.activation(x4f[:, g % 2, :], bank(g % 2), ACT.Copy).then_inc(S["x4_kept"], 1)
            def gelu(blk, e):
                for c in range(NC):
                    act.wait_ge(S["h_ready"], blk * (E * NC) + (e * NC + c + 1))
                    act.wait_ge(S["h_low_even" if c % 2 == 0 else "h_low_odd"], blk * (2 * E) + (2 * e + c // 2 + 1))
                    b1 = small_t[:, 48 + e * NC + c:49 + e * NC + c]
                    act.activation(hf[:, c, :], bank(c), ACT.Gelu_apprx_tanh, bias=b1).then_inc(S["h_gelu"], 1)

            def keep_y(e):
                act.wait_ge(S["y_ready"], e + 3)
                act.activation(ykept[:, e, :], bank(4 + e % 2), ACT.Copy).then_inc(S["y_added"], 1)

            gelu(0, 0)
            for e in range(1, E):
                gelu(0, e)
                keep_y(e - 1)
            gelu(1, 0)
            keep_y(E - 1)
            for e in range(1, E + 2):
                if e - 1 < G4:
                    act.wait_ge(S["gt_turned"], e)
                    act.activation(gtT[:, (e - 1) % 2, :], PS[0:32, 6, 0:P], ACT.Copy).then_inc(S["gt_kept"], 1)
                if e >= 2:
                    act.wait_ge(S["gb_done"], e - 1)
                    act.activation(gbias[:, 512 * (e - 2):512 * (e - 1)], bank(7), ACT.Copy).then_inc(S["gb_kept"], 1)
                if e < E:
                    gelu(1, e)
            with act.Fori(2, G4) as blk:
                for e in range(E):
                    gelu(blk, e)

        @block.vector
        def _(dve):
            steps = [0]

            def link(ins):
                steps[0] += 1
                ins.then_inc(S["dve_step"], 1)
                dve.wait_ge(S["dve_step"], steps[0])

            def ts(out, a, s1, s2, op0, op1=ALU.bypass):
                return dve.tensor_scalar(out, a, s1, s2, op0, op1)

            def ln_stats(n, h):
                w = slice(16 * h, 16 * h + 16)
                t = lambda k: lnt[:, k, w]
                dve.tensor_tensor(t(0), bns[:, w, 1], bns[:, w, 4], ALU.add)
                dve.tensor_tensor(t(1), bns[:, w, 1], bns[:, w, 4], ALU.subtract)
                link(dve.tensor_tensor(t(2), bns[:, w, 2], bns[:, w, 5], ALU.add))
                ts(t(3), t(0), 0.5, None, ALU.mult)
                link(dve.tensor_tensor(t(6), t(1), t(1), ALU.mult))
                link(ts(t(6), t(6), 0.25, None, ALU.mult))
                dve.scalar_tensor_tensor(out=t(4), in0=t(2), scalar=1.0 / D, in1=t(6), op0=ALU.mult, op1=ALU.add).then_inc(S["bn_done"], 1)

            def ln_scales(n, h):
                w = slice(16 * h, 16 * h + 16)
                dve.wait_ge(S["ln_sqrt"], 2 * n + h + 1)
                link(dve.reciprocal(lnt[:, 7, w], lnt[:, 5, w]))

            def ln_apply(h, src, dst):
                for b in range(16 * h, 16 * h + 16):
                    ins = ts(dst[:, b, :], src[:, b, :], lnt[:, 3, b:b + 1], lnt[:, 7, b:b + 1], ALU.subtract, ALU.mult)
                    if b % 4 == 3:
                        ins.then_inc(S["ln_done"], 1)

            def ln(n, src, dst, src_ready=None):
                for h in range(2):
                    for b in range(16 * h, 16 * h + 16):
                        if src_ready is not None:
                            src_ready(b)
                        ins = dve.bn_stats(bns[:, b, :], src[:, b, :])
                    link(ins)
                    ln_stats(n, h)
                for h in range(2):
                    ln_scales(n, h)
                    ln_apply(h, src, dst)

            def spread(n):
                dve.wait_ge(S["mm_turned"], n + 1)
                link(dve.tensor_reduce(gq[0:2, 0:1], PS[0:2, 7, 0:P], AX, ALU.max))
                ts(gq[0:2, 2:4], identf[0:2, 0:2], gq[0:2, 0:1], None, ALU.mult).then_inc(S["mm_global"], 1)
                dve.wait_ge(S["mm_spread"], n + 1)
                link(dve.tensor_copy(mm[:, 2:4], bank(7, P, P + 2)))

            def affine(o):
                q = lambda k: qs[:, o + k:o + k + 1]
                link(dve.tensor_tensor(q(0), mm[:, 2:3], mm[:, 3:4], ALU.add))
                link(ts(q(1), q(0), 1.0 / 255.0, 1e-8, ALU.mult, ALU.max))
                link(dve.reciprocal(q(0), q(1)))
                link(ts(q(2), q(0), mm[:, 3:4], MAGIC, ALU.mult, ALU.add))
                link(ts(q(2), q(2), MAGIC, -128.0, ALU.subtract, ALU.add))
                link(ts(q(2), q(2), -128.0, 127.0, ALU.max, ALU.min))
                ts(q(3), q(2), -1.0, MAGIC + 127.0, ALU.mult, ALU.add)
                link(ts(q(2), q(2), -1.0, MAGIC - 128.0, ALU.mult, ALU.add))

            dve.sem_inc(S["prod_done"], 2)
            dve.sem_inc(S["y_added"], 2)
            dve.sem_inc(S["h_low_odd"], 2)
            dve.memset(cst[:, 0:1], LN_EPS)
            dve.memset(cst[:, 2:3], MAGIC)
            dve.memset(cst[:, 3:4], 1.0)
            dve.wait_ge(S["consts_made"], 1)
            ts(pidx[:, 1:2], pidx[:, 0:1], 3, 3, ALU.logical_shift_right, ALU.bitwise_and)
            ts(pidx[:, 2:3], pidx[:, 0:1], 4, 1, ALU.logical_shift_right, ALU.bitwise_and)
            ts(pidx[:, 3:4], pidx[:, 0:1], 7, None, ALU.bitwise_and)
            link(ts(pidx[:, 4:5], pidx[:, 0:1], 5, None, ALU.logical_shift_right))
            ts(pm[:, 0:1], pidx[:, 2:3], 0.0, None, ALU.is_equal)
            ts(pm[:, 1:2], pidx[:, 2:3], 1.0, None, ALU.is_equal)
            ts(pm[:, 2:3], pidx[:, 1:2], 1.0, -1.0, ALU.is_ge, ALU.mult)
            ts(pm[:, 3:4], pidx[:, 1:2], 2.0, -1.0, ALU.is_ge, ALU.mult)
            ts(pm[:, 4:5], pidx[:, 1:2], 3.0, None, ALU.is_lt)
            dve.tensor_copy(pm[:, 5:6], pidx[:, 3:4])
            for k in range(4):
                ts(pm[:, 6 + k:7 + k], pidx[:, 4:5], float(k), None, ALU.is_equal)
            link(dve.tensor_copy(hidf[:], hidx[:]))
            link(ts(hpos[:], hidf[:], pm[:, 5:6], None, ALU.is_equal))
            ts(hneg[:], hpos[:], -1.0, None, ALU.mult)
            for k in range(4):
                ts(selb[:, k, :], ones[:], pm[:, 6 + k:7 + k], None, ALU.mult)
                ins = ts(bmask[:, k], last(hpos[:], P), pm[:, 6 + k:7 + k], None, ALU.mult)
            link(ins)
            dve.wait_ge(S["small_in"], 16 * 9)
            dve.tensor_copy(tgr[:, 0:1], tgr[:, 0:1]).then_inc(S["tg_in_ready"], 1)

            def x_here(b):
                if b % 8 == 0:
                    dve.wait_ge(x_in[b // 8], 16)
            ln(0, xs, xn, x_here)
            dve.wait_ge(S["small_turned"], 1)
            link(dve.tensor_copy(small_t[:, 0:92], bank(6, 0, 92)))
            dve.tensor_tensor(wkv[:], small_t[:, 16:32], small_t[:, 32:48], ALU.add).then_inc(S["small_kept"], 1)
            for g in range(G4):
                dve.wait_ge(S["q_turned"], g + 1)
                dve.tensor_copy(qT[:, 512 * g:512 * g + 512], bank(g % 2)).then_inc(S["q_kept"], 1)
            dve.wait_ge(S["csq_done"], 1)
            dve.tensor_reduce(aa[:], aa_tmp, AX, ALU.add)
            dve.wait_ge(S["aw_in"], 32)
            dve.scalar_tensor_tensor(out=wtmp[:, 0:HID], in0=w1n, scalar=-1.0, in1=w1n, op0=ALU.mult, op1=ALU.max)
            link(dve.scalar_tensor_tensor(out=wtmp[:, HID:2 * HID], in0=w2n, scalar=-1.0, in1=w2n, op0=ALU.mult, op1=ALU.max))
            dve.tensor_reduce(mm[:, 0:2], wtmp.rearrange("p (w c) -> p w c", w=2), AX, ALU.max).then_inc(S["mm_ready"], 1)
            dve.wait_ge(S["gates_summed"], 1)
            dve.tensor_tensor(pre, bank(4).rearrange("p (b w) -> p b w", b=B), rep(ifb_b[:], B), ALU.add).then_inc(S["gates_biased"], 1)
            spread(0)
            link(ts(qs[:, 0:2], mm[:, 2:4], 1.0 / 127.0, 1e-8, ALU.mult, ALU.max))
            dve.reciprocal(qs[:, 2:4], qs[:, 0:2]).then_inc(S["scale_ready"], 1)
            dve.wait_ge(S["cumsum_done"], 1)
            csum = bank(5, 0, B * NH).rearrange("p (b h) -> p b h", b=B)
            dve.tensor_copy(ncs, csum)
            link(dve.scalar_tensor_tensor(out=a_tok, in0=pre[:, :, 0:NH], scalar=GATE_CAP, in1=csum, op0=ALU.mult, op1=ALU.add))
            arep = A[:, 12288:13312].rearrange("p (b r h) -> p b r h", b=B, r=4)
            dve.tensor_copy(arep, a_tok.unsqueeze(2).to_broadcast([P, B, 4, NH])).then_inc(S["a_ready"], 1)
            for j in range(2):
                dve.wait_ge(S["a_turned"], j + 1)
                dve.tensor_copy(av[:, 0, 4 * j:4 * j + 4, :].rearrange("p g t -> p (g t)"), bank(j)).then_inc(S["dve_step"], 1)
            steps[0] += 2
            dve.wait_ge(S["dve_step"], steps[0])
            for g in range(G4):
                dve.tensor_tensor_scan(av[:, 1, g, :], av[:, 0, g, :], av[:, 0, g, :], -3e38, ALU.max, ALU.max).then_inc(S["m_ready"], 1)
            for j in range(2):
                dve.wait_ge(S["m_turned"], j + 1)
                mtok = bank(2 + j).rearrange("p (b r h) -> p b r h", b=16, r=4)[:, :, 0, :]
                ins = dve.tensor_tensor(expnm[:, 16 * j:16 * j + 16, :], ncs[:, 16 * j:16 * j + 16, :], mtok, ALU.subtract)
            ins.then_inc(S["m_tok_ready"], 1)
            dve.wait_ge(S["m_ready"], G4)
            dve.wait_ge(S["a_turned"], 2)
            fl = lambda v: v.rearrange("p w g t -> p (w g t)")
            link(dve.tensor_copy(fl(av_cut), fl(av)))
            link(dve.scalar_tensor_tensor(out=fl(av_res), in0=fl(av_cut), scalar=pm[:, 2:3], in1=fl(av), op0=ALU.mult, op1=ALU.add))
            link(dve.tensor_copy(fl(av_cut), fl(av_res)))
            link(dve.scalar_tensor_tensor(out=fl(av_res), in0=fl(av_cut), scalar=pm[:, 3:4], in1=fl(av_res), op0=ALU.mult, op1=ALU.add))
            link(ts(fl(av_part), fl(av_res), pm[:, 4:5], None, ALU.mult))
            for h in range(NH):
                ins = ts(mblk[:, :, h, :], av_part[:, 1], hneg[:, h:h + 1], None, ALU.mult)
            ins.then_inc(S["mblk_ready"], 1)
            def weights_of(g, k, half):
                u = g * 8 + (2 * k + half)
                dve.wait_ge(S["exp_done"], u + 3)
                dve.wait_ge(S["sc_ready"], u + 5)
                dve.wait_ge(S["av_done"], u + 1)
                dve.tensor_tensor(smat[:, half, :].rearrange("p (j c) -> p j c", j=2),
                                  decay[:, half, :].rearrange("p (j c) -> p j c", j=2),
                                  PS[:, 2 + 2 * half:4 + 2 * half, 0:256], ALU.mult).then_inc(S["prod_done"], 1)

            def slot_queries(g, k):
                dve.wait_ge(S["sc_ready"], g * 8 + (2 * k + 2))
                for r in range(2):
                    ins = ts(qslot[:, k % 2, r], qT[:, bass.ds(g * 512 + k * P, P)], pm[:, r:r + 1], None, ALU.mult)
                ins.then_inc(S["qslot_ready"], 1)

            def divisors(m):
                f = lambda k: fin[:, k, bass.ds(m * 32, 32)]
                dve.wait_ge(S["o_kept"], m * 8 + 10)
                s3 = heads(m)[:, :, DH:VW]
                chain(dve.scalar_tensor_tensor(out=f(0).unsqueeze(2), in0=s3, scalar=-1.0, in1=s3, op0=ALU.mult, op1=ALU.max), m, 1)
                chain(dve.scalar_tensor_tensor(out=f(0), in0=f(0), scalar=4 * BACKEND_EPS,
                                              in1=expnm[:].rearrange("p b h -> p (b h)")[:, bass.ds(m * 32, 32)],
                                              op0=ALU.add, op1=ALU.max), m, 2)
                dve.scalar_tensor_tensor(out=f(2), in0=f(0), scalar=NORM_EPS, in1=f(0), op0=ALU.mult, op1=ALU.mult)

            def mean_squares(m):
                f = lambda k: fin[:, k, bass.ds(m * 32, 32)]
                dve.wait_ge(S["osq_done"], m + 1)
                chain(dve.tensor_reduce(f(1), osq[:, bass.ds(m * 512, 512)].rearrange("p (m w) -> p m w", w=DH), AX, ALU.add), m, 3)
                dve.scalar_tensor_tensor(out=f(1), in0=f(1), scalar=1.0 / DH, in1=f(2), op0=ALU.mult, op1=ALU.add).then_inc(S["osum_done"], 1)

            def x_stats(m):
                dve.wait_ge(S["x2_ready"], m + 1)
                for k in range(4):
                    dve.bn_stats(bns[:].rearrange("p b s -> p (b s)")[:, bass.ds(m * 24 + 6 * k, 6)],
                                 xs[:].rearrange("p b d -> p (b d)")[:, bass.ds(m * 512 + P * k, P)])

            def x_range(m, w):
                op = ALU.max if w == 0 else ALU.min
                return dve.tensor_reduce(hmm[:, w, bass.ds(m * 4, 4)], xs[:, bass.ds(m * 4, 4), :], AX, op)

            def chain(ins, m, i):
                ins.then_inc(S["norm_step"], 1)
                dve.wait_ge(S["norm_step"], m * 3 + i)

            dve.wait_ge(S["tg_ready"], 1)
            ts(onw_b[:], onw_b[:], 1.0, tg[:, 0:1], ALU.add, ALU.mult)
            dve.wait_ge(S["expnm_ready"], 1)
            ts(expnm[:], expnm[:], 4.0, 4 * BACKEND_EPS, ALU.mult, ALU.add).then_inc(S["gain_ready"], 1)
            dve.wait_ge(S["gain_ready"], 1)
            def group(g, norm=True, stats=True, more=True):
                weights_of(g, 0, 0)
                slot_queries(g, 1)
                if norm:
                    divisors(g - 1)
                weights_of(g, 0, 1)
                if norm:
                    mean_squares(g - 1)
                weights_of(g, 1, 0)
                slot_queries(g, 2)
                if stats:
                    x_stats(g - 2)
                weights_of(g, 1, 1)
                if not norm:
                    dve.wait_ge(S["w_scaled"], 1)
                    link(ts(wtmp, wtmp, MAGIC - 127.0, MAGIC + 127.0, ALU.max, ALU.min))
                    ts(wqb, wtmp, MAGIC, None, ALU.subtract).then_inc(S["wq_ready"], 1)
                weights_of(g, 2, 0)
                slot_queries(g, 3)
                if stats:
                    x_range(g - 2, 0)
                weights_of(g, 2, 1)
                if stats:
                    x_range(g - 2, 1)
                weights_of(g, 3, 0)
                if more:
                    slot_queries(g + 1, 0)
                weights_of(g, 3, 1)

            slot_queries(0, 0)
            group(0, norm=False, stats=False)
            group(1, stats=False)
            with dve.Fori(2, G4 - 1) as g:
                group(g)
            group(G4 - 1, more=False)
            m = G4 - 1
            divisors(m)
            o3 = heads(m)[:, :, 0:DH]
            t = osq[:, 512 * m:512 * m + 512]
            th = t.rearrange("p (m w) -> p m w", w=DH)
            f = fin[:, 1, 32 * m:32 * m + 32]
            dve.tensor_tensor(th, o3, o3, ALU.mult).then_inc(S["osq_done"], 1)
            mean_squares(m)
            x_stats(m - 1)
            x_range(m - 1, 0)
            x_range(m - 1, 1)
            dve.wait_ge(S["osqrt_done"], 1)
            link(dve.reciprocal(f, f))
            link(dve.tensor_tensor(th, o3, last(f, DH), ALU.mult))
            link(dve.tensor_tensor(four(t), four(t), rep(onw_b[:], 4), ALU.mult))
            dve.tensor_tensor(g4(xs, m), g4(xs, m), four(t), ALU.add).then_inc(S["x2_ready"], 1)
            ln_stats(1, 0)
            x_stats(m)
            x_range(m, 0)
            link(x_range(m, 1))
            ln_stats(1, 1)
            ln_scales(1, 0)
            ln_scales(1, 1)
            link(dve.tensor_tensor(hmm[:], hmm[:], rep(lnt[:, 3, :], 2), ALU.subtract))
            link(dve.tensor_tensor(hmm[:], hmm[:], rep(lnt[:, 7, :], 2), ALU.mult))
            link(ts(hmm[:, 1, :], hmm[:, 1, :], -1.0, None, ALU.mult))
            dve.tensor_reduce(mm[:, 0:2], hmm[:], AX, ALU.max).then_inc(S["mm_ready"], 1)
            ln_apply(0, xs, xn)
            spread(1)
            affine_x = 20
            affine(affine_x)
            dve.tensor_copy(qs[:, 8:9], qs[:, affine_x:affine_x + 1])
            link(dve.tensor_tensor(qs[:, 12:13], qs[:, affine_x + 1:affine_x + 2], qs[:, 0:1], ALU.mult))
            dve.tensor_tensor(ab2_b[:], ab2_b[:], tg[:, 2:3].to_broadcast([P, D]), ALU.mult).then_inc(S["scale_ready"], 1)
            dve.wait_ge(S["wq_turned"], 2)
            ln_apply(1, xs, xn)
            for c in range(4):
                v = xn_w1[:, 1024 * c:1024 * c + 1024]
                dve.wait_ge(S["x_scaled"], c + 1)
                link(ts(v, v, qs[:, affine_x + 2:affine_x + 3], qs[:, affine_x + 3:affine_x + 4], ALU.max, ALU.min))
                ts(xq[:, 1024 * c:1024 * c + 1024], v, MAGIC, None, ALU.subtract).then_inc(S["xq_ready"], 1)
            for nb in range(G4):
                dve.wait_ge(S["gelu_done"], NC * (nb + 1))
                v = hid[:, :, 512 * nb:512 * nb + 512]
                dve.tensor_reduce(hmm[:, 0, NC * nb:NC * nb + NC], v, AX, ALU.max)
                ins = dve.tensor_reduce(hmm[:, 1, NC * nb:NC * nb + NC], v, AX, ALU.min)
            link(ins)
            dve.tensor_reduce(mm[:, 0:1], hmm[:, 0, :], AX, ALU.max)
            link(dve.tensor_reduce(mm[:, 4:5], hmm[:, 1, :], AX, ALU.min))
            ts(mm[:, 1:2], mm[:, 4:5], -1.0, None, ALU.mult).then_inc(S["mm_ready"], 1)
            spread(2)
            affine_h = 24
            affine(affine_h)
            link(dve.tensor_tensor(qs[:, 13:14], qs[:, affine_h + 1:affine_h + 2], qs[:, 1:2], ALU.mult))
            link(dve.tensor_tensor(qs[:, 13:14], qs[:, 13:14], tg[:, 2:3], ALU.mult))
            dve.tensor_copy(qs[:, 16:17], qs[:, affine_h:affine_h + 1]).then_inc(S["scale_ready"], 1)

            def add2(nb):
                dve.wait_ge(S["ffn2_done"], nb + 1)
                dve.scalar_tensor_tensor(out=g4(xs, nb), in0=four(bank(nb % 2)), scalar=qs[:, 13:14], in1=g4(xs, nb),
                                         op0=ALU.mult, op1=ALU.add).then_inc(S["ffn2_added"], 1)
            dve.wait_ge(S["b2_added"], 1)
            for nb in range(G4):
                v = hid[:, :, 512 * nb:512 * nb + 512]
                dve.wait_ge(S["h_scaled"], nb + 1)
                link(ts(v, v, qs[:, affine_h + 2:affine_h + 3], qs[:, affine_h + 3:affine_h + 4], ALU.max, ALU.min))
                ts(hq[:, :, 512 * nb:512 * nb + 512], v, MAGIC, None, ALU.subtract).then_inc(S["hq_ready"], 1)
                if nb >= 1:
                    add2(nb - 1)
            add2(G4 - 1)
            dve.wait_ge(S["ffn2_added"], G4)
            ln(2, xs, xn)
            for g in range(G4):
                dve.wait_ge(S["dsum_done"], g + 1)
                for k in range(4):
                    ins = ts(dsq[:, 4 * g + k, :], bank(2 + g % 2, P * k, P * k + P), aa[:, 4 * g + k:4 * g + k + 1], 0.0, ALU.add, ALU.max)
                ins.then_inc(S["dsq_ready"], 1)
            dve.wait_ge(S["d_out"], 16 * G4)
            rr = Bm[0:B, 0:2 * (RC + 1) * RW]
            link(dve.memset(rr, BIG))
            link(dve.memset(rring[0:B, 0, 0, 0:1], 0.0))
            dve.memset(ee[:], 2.0 * (P - 1))
            for c in range(NRC):
                dve.wait_ge(d_in[c % 2], 16 * (c // 2 + 1))
                if c >= 2:
                    dve.wait_ge(S["r_out"], 16 * (c - 1))
                for r in range(RC):
                    above = rring[0:B, c % 2, r] if r or not c else rring[0:B, (c - 1) % 2, RC]
                    link(dve.tensor_tensor(rowm[:], above[:, 1:RW], above[:, 0:P], ALU.min))
                    dve.tensor_tensor_scan(rring[0:B, c % 2, r + 1, 1:RW], rowm[:], dring[0:B, c % 2, r], BIG, ALU.min, ALU.add)\
                        .then_inc(S["row_done"], 1)
                    dve.wait_ge(S["row_done"], RC * c + r + 1)
                if c >= 1:
                    back_steps(dve, link, c - 1)
            back_steps(dve, link, NRC - 1)
            for i in reversed(range(P)):
                if i % RC == RC - 1:
                    dve.wait_ge(S["k_in"], 16 * NRC)
                dve.scalar_tensor_tensor(out=rowm[:], in0=iota2[0:B], scalar=ee[:, i + 1:i + 2], in1=kb[0:B, i, :],
                                         op0=ALU.is_le, op1=ALU.mult, accum_out=ee[:, i:i + 1]).then_inc(S["track_done"], 1)
                dve.wait_ge(S["track_done"], P - i)
            dve.wait_ge(S["e_turned"], 1)
            link(dve.tensor_copy(eT[:], bank(0, 0, 2 * B).rearrange("p (w b) -> p w b", w=2)))
            for g in range(G4):
                for b in range(4 * g, 4 * g + 4):
                    ins = ts(pathm[:, b, :], iota2[:], eT[:, 1, b:b + 1], None, ALU.is_le)
                link(ins)
                for b in range(4 * g, 4 * g + 4):
                    ins = dve.scalar_tensor_tensor(out=path[:, b, :], in0=iota2[:], scalar=eT[:, 0, b:b + 1], in1=pathm[:, b, :],
                                                   op0=ALU.is_ge, op1=ALU.mult)
                ins.then_inc(S["path_ready"], 1)
            for g in range(G4):
                dve.wait_ge(S["expanded"], g + 1)
                dve.scalar_tensor_tensor(out=g4(xs, g), in0=four(bank(1 + g % 2)), scalar=tg[:, 1:2], in1=g4(xs, g),
                                         op0=ALU.mult, op1=ALU.add).then_inc(S["expanded_added"], 1)
            dve.wait_ge(S["expanded_added"], G4)
            ln(3, xs, x4)
            for g in range(G4):
                dve.wait_ge(S["x4_kept"], g + 1)
                w = slice(512 * g, 512 * g + 512)
                link(dve.tensor_copy(x4h[:, w], x4f[:, g % 2, :]))
                dve.tensor_tensor(x4l[:, w], x4f[:, g % 2, :], x4h[:, w], ALU.subtract).then_inc(S["x4_split"], 1)
            dve.wait_ge(S["logits_done"], G4)
            lgf = lg.rearrange("p b e -> p (b e)")
            link(dve.tensor_copy(lgf, bank(2, 0, B * E)))
            dve.memset(key, 0)
            dve.memset(flip, 0xFFFFFFFF)
            dve.memset(top, 1 << 31)
            for k in range(3):
                dve.memset(digit[:, k:k + 1], k + 1)
            link(dve.memset(cand, 0))

            def count(k):
                return dve.tensor_scalar(selw[:, k, :], lgf, cand[:, k:k + 1].bitcast(F32), None, ALU.is_lt, ALU.add, accum_out=sel[:, k:k + 1])

            def round_start(n):
                if n == 0:
                    count(0).then_inc(S["count_ready"], 1)
                    return
                w = 1 if n == ROUNDS - 1 else 3
                link(dve.scalar_tensor_tensor(out=cand[:, 0:w], in0=digit[:, 0:w], scalar=SHIFT[n], in1=key.to_broadcast([P, w]),
                                              op0=ALU.logical_shift_left, op1=ALU.bitwise_or))
                link(dve.tensor_tensor(cand[:, 0:w], cand[:, 0:w], flip.to_broadcast([P, w]), ALU.bitwise_xor))
                for k in range(w):
                    ins = count(k)
                ins.then_inc(S["count_ready"], 1)

            def round_end(n):
                dve.wait_ge(S["count_all"], n + 1)
                if n == 0:
                    link(ts(sel[:, 4:5], bank(7, 0, 1), KTH - 1.0, None, ALU.is_le))
                    dve.copy_predicated(key, sel[:, 4:5].bitcast(U32), top)
                    link(dve.copy_predicated(flip, sel[:, 4:5].bitcast(U32), top))
                    return
                w = 1 if n == ROUNDS - 1 else 3
                link(dve.tensor_scalar(sel[:, 8:8 + w], bank(7, 0, w), KTH - 1.0, None, ALU.is_le, ALU.add, accum_out=sel[:, 4:5]))
                link(ts(step, sel[:, 4:5], float(1 << SHIFT[n]), None, ALU.mult))
                link(dve.tensor_tensor(key, key, step, ALU.bitwise_or))

            def gates():
                link(dve.tensor_tensor(cand[:, 0:1], key, flip, ALU.bitwise_xor))
                link(dve.scalar_tensor_tensor(out=gts, in0=lg, scalar=cand[:, 0:1].bitcast(F32), in1=lg, op0=ALU.is_ge, op1=ALU.mult))
                ts(gts, gts, tg[:, 3:4], None, ALU.mult).then_inc(S["gates_ready"], 1)

            def parts(blk, e):
                for c in range(NC):
                    dve.wait_ge(S["h_gelu"], blk * (E * NC) + (e * NC + c + 5))
                    if c == 0:
                        dve.wait_ge(S["y_ready"], blk * E + (e + 1))
                    dve.tensor_copy(hh[:, e % 2, c, :], hf[:, c, :]).then_inc(S["h_high"], 1)
                    if isinstance(blk, int) and blk == 0:
                        m = e * NC + c
                        if m % 2:
                            round_end(m // 2)
                            round_start(m // 2 + 1)
                    if not (isinstance(blk, int) and blk == 0) and c % 2:
                        dve.wait_ge(S["h_high"], blk * (E * NC) + (e * NC + c + 1))
                        dve.tensor_tensor(hl[:, e % 2, c, :], hf[:, c, :], hh[:, e % 2, c, :], ALU.subtract).then_inc(S["h_low_odd"], 1)

            def gated_sum(blk, e):
                dve.wait_ge(S["y_ready"], blk * E + (e + 3))
                dve.wait_ge(S["y_added"], blk * E + (e + 2))
                for k in range(4):
                    row = xs[:].rearrange("p b d -> p (b d)")[:, bass.ds(blk * 512 + k * P, P)]
                    gate = gts.rearrange("p b e -> p (b e)")[:, bass.ds(blk * (4 * E) + (k * E + e), 1)]
                    ins = dve.scalar_tensor_tensor(out=row, in0=bank(4 + e % 2, P * k, P * k + P), scalar=gate, in1=row,
                                                   op0=ALU.mult, op1=ALU.add)
                ins.then_inc(S["y_added"], 1)

            def late_sum(e):
                for k in range(4):
                    if e:
                        dve.wait_ge(S["late_added"], 4 * (e - 1) + k + 1)
                    dve.scalar_tensor_tensor(out=xs[:, k, :], in0=ykept[:, e, P * k:P * k + P], scalar=gts[:, k, e:e + 1], in1=xs[:, k, :],
                                             op0=ALU.mult, op1=ALU.add).then_inc(S["late_added"], 1)

            def bias_sum(blk):
                rows = slice(512 * blk, 512 * blk + 512) if isinstance(blk, int) else bass.ds(blk * 512, 512)
                row = xs[:].rearrange("p b d -> p (b d)")[:, rows]
                return dve.tensor_tensor(row, row, gbias[:, rows], ALU.add)

            round_start(0)
            for e in range(E):
                parts(0, e)
            round_end(ROUNDS - 1)
            gates()
            dve.wait_ge(S["gates_ready"], 1)
            dve.wait_ge(S["y_added"], E + 2)
            parts(1, 0)
            for e in range(1, E):
                late_sum(e - 1)
                parts(1, e)
                gated_sum(1, e - 1)
            late_sum(E - 1)
            parts(2, 0)
            gated_sum(1, E - 1)
            dve.wait_ge(S["gb_kept"], G4)
            dve.wait_ge(S["late_added"], 4 * E)
            dve.wait_ge(S["y_added"], 2 * E + 2)
            bias_sum(0).then_inc(S["bias_added"], 1)
            bias_sum(1).then_inc(S["bias_added"], 1)
            with dve.Fori(2, G4 - 1) as blk:
                bias_sum(blk).then_inc(S["bias_added"], 1)
                dve.wait_ge(S["bias_added"], blk + 1)
                for e in range(1, E):
                    parts(blk, e)
                    gated_sum(blk, e - 1)
                parts(blk + 1, 0)
                gated_sum(blk, E - 1)
            bias_sum(G4 - 1).then_inc(S["bias_added"], 1)
            dve.wait_ge(S["bias_added"], G4)
            for e in range(1, E):
                parts(G4 - 1, e)
                gated_sum(G4 - 1, e - 1)
            gated_sum(G4 - 1, E - 1)

        @block.tensor
        def _(pe):
            def spread(n):
                pe.wait_ge(S["mm_ready"], n + 1)
                pe.transpose(PS[0:2, 7, 0:P], mm[:, 0:2], identf[:]).then_inc(S["mm_turned"], 1)
                pe.wait_ge(S["mm_global"], n + 1)
                pe.matmul(bank(7, P, P + 2), ones[0:2, :], gq[0:2, 2:4], start=True, stop=True).then_inc(S["mm_spread"], 1)

            pe.sem_inc(S["sc_ready"], 4)
            pe.sem_inc(S["av_done"], 2)
            pe.sem_inc(S["y_ready"], 2)
            pe.wait_ge(S["consts_made"], 1)
            pe.wait_ge(S["small_in"], 16 * 9)
            for k in range(3):
                pe.transpose(bank(6, 16 * k, 16 * k + 16), ifw_n[:, P * k:P * k + P], identf[0:16, 0:16])
            pe.transpose(bank(6, 48, 80), mb1_n, identf[0:32, 0:32])
            pe.transpose(bank(6, 80, 84), ab1_n, identf[0:4, 0:4])
            pe.transpose(bank(6, 84, 92), gw_n, identf[0:8, 0:8]).then_inc(S["small_turned"], 1)
            for g in range(G4):
                if g % 2 == 0:
                    pe.wait_ge(ctx_in[g // 2], 16)
                if g >= 2:
                    pe.wait_ge(S["k_kept"], g - 1)
                for k in range(4):
                    ins = pe.transpose(bank(2 + g % 2, P * k, P * k + P), cs[:, 4 * g + k, :], identf[:])
                ins.then_inc(S["c_turned"], 1)
                pe.wait_ge(S["ln_done"], g + 1)
                if g >= 2:
                    pe.wait_ge(S["q_kept"], g - 1)
                for k in range(4):
                    ins = pe.transpose(bank(g % 2, P * k, P * k + P), xn[:, 4 * g + k, :], identf[:])
                ins.then_inc(S["q_turned"], 1)
            pe.wait_ge(S["small_kept"], 1)
            for g in range(G4):
                pe.wait_ge(S["q_kept"], g + 1)
                pe.wait_ge(S["k_kept"], g + 1)
                for b in range(4 * g, 4 * g + 4):
                    o = bank(4, 16 * b, 16 * b + 16)
                    w = slice(P * b, P * b + P)
                    pe.matmul(o, qT[:, w], small_t[:, 0:16], start=True, stop=False)
                    ins = pe.matmul(o, kT[:, w], wkv[:], start=False, stop=True)
            ins.then_inc(S["gates_summed"], 1)
            spread(0)
            pe.wait_ge(S["nlf_ready"], 1)
            pe.matmul(bank(5, 0, B * NH), tri[:], nlf.rearrange("p b h -> p (b h)"), start=True, stop=True).then_inc(S["cumsum_done"], 1)
            pe.wait_ge(S["a_ready"], 1)
            for j in range(2):
                for g in range(4):
                    ins = pe.transpose(bank(j, P * g, P * g + P), A[:, 12288 + P * (4 * j + g):12288 + P * (4 * j + g + 1)], identf[:])
                ins.then_inc(S["a_turned"], 1)
            for j in range(2):
                pe.wait_ge(S["m_ready"], 4 * (j + 1))
                for g in range(4):
                    ins = pe.transpose(bank(2 + j, P * g, P * g + P), av[:, 1, 4 * j + g, :], identf[:])
                ins.then_inc(S["m_turned"], 1)
            pe.wait_ge(S["m_tok_ready"], 1)
            pe.wait_ge(S["mblk_ready"], 1)
            pe.wait_ge(S["vaug_ready"], 1)
            with pe.Fori(0, G4) as g:
                def weigh(k, half):
                    u = g * 8 + (2 * k + half)
                    pe.wait_ge(S["prod_done"], u + 3)
                    pe.wait_ge(S["o_kept"], u + 1)
                    for j in range(4):
                        v6 = vaug[:, bass.ds(g * 4 + k, 1), 2 * VW * half:2 * VW * half + 6 * VW].rearrange("p b w -> p (b w)")
                        ins = pe.matmul(bank(6 + half, 6 * VW * j, 6 * VW * (j + 1)), smat[:, half, P * j:P * j + P], v6, start=True, stop=True)
                    ins.then_inc(S["av_done"], 1)

                for k in range(4):
                    for half in range(2):
                        u = g * 8 + (2 * k + half)
                        pe.wait_ge(S["exp_done"], u + 1)
                        mb = mblk.rearrange("p g h t -> p (g h t)")[:, bass.ds(g * 1024 + 512 * half, 512)]
                        pe.matmul(bank(half), selb[:, k, :], mb, start=True, stop=False)
                        pe.matmul(bank(half), av_part[:, 0].rearrange("p g t -> p (g t)")[:, bass.ds(g * P, P)],
                                  bmask[:, k, 4 * half:4 * half + 4, :].rearrange("p h t -> p (h t)"), start=False, stop=False)
                        pe.matmul(bank(half), identb[:], rep(neg[:], 4), start=False, stop=True).then_inc(S["ld_ready"], 1)
                        pe.wait_ge(S["prod_done"], u + 1)
                        if half == 0:
                            pe.wait_ge(S["kslot_ready"], g * 4 + (k + 1))
                            pe.wait_ge(S["qslot_ready"], g * 4 + (k + 1))
                        for jj in range(2):
                            r = slice(64 * half + 32 * jj, 64 * half + 32 * jj + 32)
                            ins = pe.matmul(PS[:, 2 + 2 * half + jj, 0:256], kslot[r, k % 2, :], qslot[r, k % 2],
                                            start=True, stop=True)
                        ins.then_inc(S["sc_ready"], 1)
                        if half == 1:
                            weigh(k, 0)
                        elif k:
                            weigh(k - 1, 1)
                weigh(3, 1)
            pe.wait_ge(S["wq_ready"], 1)
            pe.wait_ge(S["o_kept"], 2 * B + 2)
            for n in range(2):
                for c in range(NC):
                    w = slice(HID * n + P * c, HID * n + P * c + P)
                    ins = pe.transpose(bankb(5 + n)[:, P * c:P * c + P], wqb[:, w], identb[:])
                ins.then_inc(S["wq_turned"], 1)
            spread(1)
            for nb in range(G4):
                pe.wait_ge(S["xq_ready"], nb // 2 + 1)
                if nb >= 2:
                    pe.wait_ge(S["xqT_kept"], nb - 1)
                for k in range(4):
                    b = 4 * nb + k
                    ins = pe.transpose(bankb(nb % 2)[:, P * k:P * k + P], xq[:, P * b:P * b + P], identb[:])
                ins.then_inc(S["xq_turned"], 1)
                pe.wait_ge(S["xqT_kept"], nb + 1)
                pe.wait_ge(S["wq_kept"], 2)
                for c in range(NC):
                    if nb >= 1:
                        pe.wait_ge(S["gelu_done"], NC * (nb - 1) + c + 1)
                    pe.matmul(bank(2 + c), w1q[:, P * c:P * c + P], xqT[:, 512 * nb:512 * nb + 512], start=True, stop=True).then_inc(S["ffn1_done"], 1)
            spread(2)
            for nb in range(G4):
                pe.wait_ge(S["hq_ready"], nb + 1)
                if nb >= 2:
                    pe.wait_ge(S["ffn2_added"], nb - 1)
                for k in range(4):
                    for c in range(NC):
                        t0 = 512 * nb + P * k
                        ins = pe.matmul(bank(nb % 2, P * k, P * k + P), hq[:, c, t0:t0 + P], w2q[:, c, :], start=(c == 0), stop=(c == NC - 1))
                ins.then_inc(S["ffn2_done"], 1)
            pe.wait_ge(S["ffn2_added"], G4)
            for g in range(G4 + 1):
                if g < G4:
                    pe.wait_ge(S["ln_done"], 2 * G4 + g + 1)
                    if g >= 2:
                        pe.wait_ge(S["x3T_kept"], g - 1)
                    for k in range(4):
                        ins = pe.transpose(bank(g % 2, P * k, P * k + P), xn[:, 4 * g + k, :], identf[:])
                    ins.then_inc(S["x3T_turned"], 1)
                if g >= 1:
                    m = g - 1
                    pe.wait_ge(S["x3T_kept"], m + 1)
                    if m >= 2:
                        pe.wait_ge(S["dsq_ready"], m - 1)
                    pe.matmul(bank(2 + m % 2), ones[:], xTsq[:, m % 2, :], start=True, stop=False)
                    for k in range(4):
                        b = 4 * m + k
                        ins = pe.matmul(bank(2 + m % 2, P * k, P * k + P), kT[:, P * b:P * b + P], xT2[:, m % 2, P * k:P * k + P],
                                        start=False, stop=(k == 3))
                    ins.then_inc(S["dsum_done"], 1)
            for n in range(2 * E):
                pe.wait_ge(raw_in[n % 2], 16 * (n // 2 + 1))
                if n >= 2:
                    pe.wait_ge(S["raw_kept"], n - 1)
                for c in range(NC):
                    ins = pe.transpose(bank(4 + n % 2, P * c, P * c + P), wraw[:, n % 2, P * c:P * c + P], identf[:])
                ins.then_inc(S["raw_turned"], 1)
            pe.wait_ge(S["track_done"], P)
            pe.transpose(bank(0, 0, B), ee[:, 0:P], identf[0:B, 0:B])
            pe.transpose(bank(0, B, 2 * B), ee[:, 1:P + 1], identf[0:B, 0:B]).then_inc(S["e_turned"], 1)
            for g in range(G4):
                pe.wait_ge(S["path_ready"], g + 1)
                if g >= 2:
                    pe.wait_ge(S["expanded_added"], g - 1)
                for k in range(4):
                    b = 4 * g + k
                    ins = pe.matmul(bank(1 + g % 2, P * k, P * k + P), path[:, b, :], cs[:, b, :], start=True, stop=True)
                ins.then_inc(S["expanded"], 1)
            pe.wait_ge(S["expanded_added"], G4)
            for g in range(G4 + 1):
                if g < G4:
                    pe.wait_ge(S["ln_done"], 3 * G4 + g + 1)
                    if g >= 2:
                        pe.wait_ge(S["x4_kept"], g - 1)
                    for k in range(4):
                        ins = pe.transpose(bank(g % 2, P * k, P * k + P), x4[:, 4 * g + k, :], identf[:])
                    ins.then_inc(S["x4_turned"], 1)
                if g >= 1:
                    pe.wait_ge(S["x4_kept"], g)
                    for k in range(4):
                        b = 4 * (g - 1) + k
                        ins = pe.matmul(bank(2, E * b, E * b + E), x4f[:, (g - 1) % 2, P * k:P * k + P], small_t[:, 84:92], start=True, stop=True)
                    ins.then_inc(S["logits_done"], 1)
            pe.wait_ge(S["x4_split"], G4)
            pe.wait_ge(S["w_split"], 2 * E)

            def hidden(blk, e):
                xw = slice(512 * blk, 512 * blk + 512) if isinstance(blk, int) else bass.ds(blk * 512, 512)
                for c in range(NC):
                    pe.wait_ge(S["h_gelu"], blk * (E * NC) + (e * NC + c + 1))
                    pe.matmul(bank(c), w1h[:, e, c, :], x4h[:, xw], start=True, stop=False)
                    pe.matmul(bank(c), w1h[:, e, c, :], x4l[:, xw], start=False, stop=False)
                    pe.matmul(bank(c), w1l[:, e, c, :], x4h[:, xw], start=False, stop=True).then_inc(S["h_ready"], 1)
                    if isinstance(blk, int) and blk == 0 and c % 2 == 1:
                        counts(2 * e + c // 2)

            def outputs(blk, e):
                pe.wait_ge(S["y_added"], blk * E + (e + 1))
                for c in range(NC):
                    pe.wait_ge(S["h_low_even" if c % 2 == 0 else "h_low_odd"], blk * (2 * E) + (2 * e + c // 2 + 3))
                    for k in range(4):
                        o = bank(4 + e % 2, P * k, P * k + P)
                        t = slice(P * k, P * k + P)
                        pe.matmul(o, hh[:, e % 2, c, t], w2h[:, e, c, :], start=(c == 0 and k == 0), stop=False, skip_group_check=True)
                        pe.matmul(o, hh[:, e % 2, c, t], w2l[:, e, c, :], start=False, stop=False, skip_group_check=True)
                        ins = pe.matmul(o, hl[:, e % 2, c, t], w2h[:, e, c, :], start=False, stop=(c == NC - 1), skip_group_check=True)
                ins.then_inc(S["y_ready"], 1)

            def counts(n):
                w = 1 if n in (0, ROUNDS - 1) else 3
                pe.wait_ge(S["count_ready"], n + 1)
                pe.matmul(bank(7, 0, w), ones[:], sel[:, 0:w], start=True, stop=True).then_inc(S["count_all"], 1)

            def gated_bias(e):
                if e - 1 < G4:
                    if e >= 2:
                        pe.wait_ge(S["gt_kept"], e - 1)
                    pe.transpose(PS[0:32, 6, 0:P], gts[:, 4 * e - 4:4 * e, :].rearrange("p b e -> p (b e)"), identf[:]).then_inc(S["gt_turned"], 1)
                if e >= 2:
                    if e >= 3:
                        pe.wait_ge(S["gb_kept"], e - 2)
                    pe.matmul(bank(7), gtT[:, (e - 2) % 2, :], b2blk[:].rearrange("p k d -> p (k d)"), start=True, stop=True).then_inc(S["gb_done"], 1)

            hidden(0, 0)
            for e in range(1, E):
                hidden(0, e)
                outputs(0, e - 1)
            counts(ROUNDS - 1)
            hidden(1, 0)
            outputs(0, E - 1)
            pe.wait_ge(S["gates_ready"], 1)
            pe.wait_ge(S["b2_in"], 64)
            for e in range(1, E + 2):
                gated_bias(e)
                if e < E:
                    hidden(1, e)
                    outputs(1, e - 1)
            hidden(2, 0)
            outputs(1, E - 1)
            with pe.Fori(2, G4 - 1) as blk:
                for e in range(1, E):
                    hidden(blk, e)
                    outputs(blk, e - 1)
                hidden(blk + 1, 0)
                outputs(blk, E - 1)
            for e in range(1, E):
                hidden(G4 - 1, e)
                outputs(G4 - 1, e - 1)
            outputs(G4 - 1, E - 1)


_INS = ['x', 'ctx_1024', 'g_xattn', 'g_ffn', 'L0_xattn_ifgate_w', 'L0_xattn_ifgate_b', 'L0_xattn_outnorm_w', 'L0_ffn_W1',
        'L0_ffn_b1', 'L0_ffn_W2', 'L0_ffn_b2', 'L1_ffn_gate_weight', 'L1_ffn_w1', 'L1_ffn_b1', 'L1_ffn_w2', 'L1_ffn_b2']
_OUTS = [((32, 128, 128), 'float32')]


def kernel(**inputs):
    import numpy as _np
    import concourse.bacc as _bacc
    from concourse import mybir as _mybir
    from concourse.bass_utils import run_bass_kernel_spmd as _run

    nc = _bacc.Bacc("TRN2", target_bir_lowering=False, num_devices=1)
    arrays, args = {}, []
    for name in _INS:
        a = _np.ascontiguousarray(inputs[name])
        arrays[f"in_{name}_dram"] = a
        args.append(nc.dram_tensor(f"in_{name}_dram", a.shape, _mybir.dt.from_np(a.dtype), kind="ExternalInput").ap())
    for i, (shape, dtype) in enumerate(_OUTS):
        dt = _mybir.dt.from_np(_np.dtype(dtype))
        args.append(nc.dram_tensor(f"out_{i}_dram", shape, dt, kind="ExternalOutput").ap())
    program(nc, *args)
    r = _run(nc, [arrays], core_ids=[0])
    got = tuple(r.results[0][f"out_{i}_dram"] for i in range(len(_OUTS)))
    return got[0]
```

```python
from contextlib import ExitStack

import concourse.bass as bass
import concourse.mybir as mybir

F32 = mybir.dt.float32
BF16 = mybir.dt.bfloat16
I32 = mybir.dt.int32
U32 = mybir.dt.uint32
ALU = mybir.AluOpType
ACT = mybir.ActivationFunctionType
AX = mybir.AxisListType.X

P = 128
B = 32
D = 128
NH, DH = 8, 16
HID = 512
NC = HID // P
E = 8
G4 = B // 4
KTH = 4 * 128 * 6
MAGIC = 12582912.0
BIG = 1e30
LN_EPS, NORM_EPS, BACKEND_EPS = 1e-5, 1e-6, 5e-5
GATE_CAP = 15.0
VW = DH + 1
RC = 32
CHUNKS = [(0, 32), (32, 32), (64, 32), (96, 16), (112, 16)]
NRC = len(CHUNKS)
R9 = 5 * 16
MIN, DIAG, LEFT, SCAN, CUT = range(5)
PLACE_0 = 7
BACK = [sum(5 * rows // 4 for _, rows in CHUNKS[:c]) for c in range(NRC)]
LEFT_DONE = [BACK[c] + 3 * CHUNKS[c][1] // 4 for c in range(NRC - 1)] + [BACK[-1] + 3]
CUT_DONE = [BACK[c] + 5 * CHUNKS[c][1] // 4 for c in range(NRC - 1)] + [BACK[-1] + 6 + CHUNKS[-1][1] // 4]
SHIFT = [31] + [29 - 2 * n for n in range(15)] + [0]
ROUNDS = len(SHIFT)
NS = 2
RW = P + 1


def program(nc, x, ctx_, g_x, g_f, if_w, if_b, on_w, a_w1, a_b1, a_w2, a_b2, gate_w, m_w1, m_b1, m_w2, m_b2, out):
    with ExitStack() as stack:
        def sb(name, shape, dt=F32):
            return stack.enter_context(nc.sbuf_tensor(name, shape, dt))

        def sem(name):
            return stack.enter_context(nc.semaphore(name))

        def dram(name, shape, dt):
            return nc.dram_tensor(name, shape, dt)

        xs = sb("xs", [P, B, D])
        cs = sb("cs", [P, B, D])
        xn_w1 = sb("xn_w1", [P, B * D])
        kT_w2 = sb("kT_w2", [P, B * D])
        A = sb("A", [P, 16384])
        Bm = sb("Bm", [P, 14848])
        slab = sb("slab", [P, 2048])
        slab2 = sb("slab2", [P, 512])
        PS = stack.enter_context(nc.psum_tensor("PS", [P, 8, 512], F32))

        xn = xn_w1[:].rearrange("p (b d) -> p b d", b=B)
        kT = kT_w2

        qT = A[:, 0:4096]
        bmask = A[:, 8192:10240].bitcast(BF16).rearrange("p (k h t) -> p k h t", k=4, h=NH)
        av = A[:, 10240:12288].rearrange("p (w g t) -> p w g t", w=2, g=G4)
        av_res = A[:, 12288:14336].rearrange("p (w g t) -> p w g t", w=2, g=G4)
        av_cut = A[:, 14336:15360].bitcast(BF16).rearrange("p (w g t) -> p w g t", w=2, g=G4)
        av_part = A[:, 15360:16384].bitcast(BF16).rearrange("p (w g t) -> p w g t", w=2, g=G4)
        vh = Bm[:, 0:2176].bitcast(BF16).rearrange("p (b w) -> p b w", b=B)
        vl = Bm[:, 2176:4352].bitcast(BF16).rearrange("p (b w) -> p b w", b=B)
        oall = Bm[:, 4352:8704].rearrange("p (b w) -> p b w", b=B)
        decay = Bm[:, 8704:9728].rearrange("p (s c) -> p s c", s=2)
        sh = A[:, 12288:12800].bitcast(BF16).rearrange("p (s c) -> p s c", s=2)
        sl = A[:, 12800:13312].bitcast(BF16).rearrange("p (s c) -> p s c", s=2)
        smat = Bm[:, 9728:10752].rearrange("p (s c) -> p s c", s=2)
        mblk = Bm[:, 10752:14848].bitcast(BF16).rearrange("p (g h t) -> p g h t", g=G4, h=NH)
        osq = A[:, 4096:8192]
        hid = A[:, 0:16384].rearrange("p (c t) -> p c t", c=NC)
        hq = Bm[:, 0:8192].bitcast(BF16).rearrange("p (c t) -> p c t", c=NC)
        xq = Bm[:, 8192:10240].bitcast(BF16)
        xqT = Bm[:, 10240:12288].bitcast(BF16)
        xT2 = Bm[:, 0:1024].rearrange("p (s t) -> p s t", s=2)
        xTsq = Bm[:, 1024:2048].rearrange("p (s t) -> p s t", s=2)
        dsq = Bm[:, 2048:6144].rearrange("p (b j) -> p b j", b=B)
        dist = Bm[:, 6144:10240].rearrange("p (b j) -> p b j", b=B)
        dring = A[:, 0:8192].rearrange("p (s r j) -> p s r j", s=2, r=RC)
        kb = A[:, 8192:16384].bitcast(BF16).rearrange("p (i j) -> p i j", i=P)
        rring = Bm[:, 0:2 * (RC + 1) * RW].rearrange("p (s r j) -> p s r j", s=2, r=RC + 1)
        o0 = 2 * (RC + 1) * RW
        r9 = Bm[:, o0:o0 + 9 * RW].rearrange("p (r j) -> p r j", r=9)
        o0 += 9 * RW
        ch_m = Bm[:, o0:o0 + 1024].rearrange("p (r j) -> p r j", r=8)
        ch_g = Bm[:, o0 + 1024:o0 + 2048].rearrange("p (r j) -> p r j", r=8)
        ch_k = Bm[:, o0 + 2048:o0 + 3072].rearrange("p (r j) -> p r j", r=8)
        ch_s = Bm[:, o0 + 3072:o0 + 3072 + 8 * RW].rearrange("p (r j) -> p r j", r=8)
        o0 += 3072 + 8 * RW
        ch_d = Bm[:, o0:o0 + 512].bitcast(BF16).rearrange("p (r j) -> p r j", r=8)
        path = Bm[:, 0:4096].rearrange("p (b j) -> p b j", b=B)
        x4 = A[:, 0:4096].rearrange("p (b d) -> p b d", b=B)
        x4h = A[:, 4096:6144].bitcast(BF16)
        x4l = A[:, 6144:8192].bitcast(BF16)
        x4f = A[:, 8192:9216].rearrange("p (s t) -> p s t", s=2)
        hf = A[:, 9216:11264].rearrange("p (s t) -> p s t", s=4)
        hh = A[:, 11264:13312].bitcast(BF16).rearrange("p (s c t) -> p s c t", s=2, c=NC)
        hl = A[:, 13312:15360].bitcast(BF16).rearrange("p (s c t) -> p s c t", s=2, c=NC)
        w1h = xn_w1[:, 0:2048].bitcast(BF16).rearrange("p (e c t) -> p e c t", e=E, c=NC)
        w1l = xn_w1[:, 2048:4096].bitcast(BF16).rearrange("p (e c t) -> p e c t", e=E, c=NC)
        w2h = kT_w2[:, 0:2048].bitcast(BF16).rearrange("p (e c t) -> p e c t", e=E, c=NC)
        w2l = kT_w2[:, 2048:4096].bitcast(BF16).rearrange("p (e c t) -> p e c t", e=E, c=NC)

        identf = sb("identf", [P, P])
        identb = sb("identb", [P, P], BF16)
        tri = sb("tri", [P, P])
        neg = sb("neg", [P, P], BF16)
        iota2 = sb("iota2", [P, P])
        ones = sb("ones", [P, P])
        selb = slab2[:, 0:256].bitcast(BF16).rearrange("p (k t) -> p k t", k=4)
        pidx = sb("pidx", [P, 8], I32)
        hidx = sb("hidx", [P, 8], I32)
        hidf = sb("hidf", [P, 8])
        pm = sb("pm", [P, 16])
        hneg = sb("hneg", [P, 8])
        hpos = sb("hpos", [P, 8])
        cst = sb("cst", [P, 8])
        mhalf = sb("mhalf", [P, 32])
        bns = sb("bns", [P, B, 6])
        lnt = sb("lnt", [P, 8, B])
        ifw_n = Bm[0:16, 8704:9088]
        ifb_b = sb("ifb_b", [P, 16])
        onw_b = sb("onw_b", [P, D])
        tgr = sb("tgr", [P, 4])
        tg = sb("tg", [P, 4])
        ab1_n = Bm[0:NC, 9088:9216]
        ab2_b = sb("ab2_b", [P, D])
        gw_n = Bm[0:E, 9216:9344]
        mb1_n = Bm[0:E * NC, 9344:9472]
        b2blk = sb("b2blk", [32, 4, D])
        small_t = sb("small_t", [P, 92])
        wkv = sb("wkv", [P, 16])
        pre = slab[:, 0:512].rearrange("p (b w) -> p b w", b=B)
        nlf = slab[:, 512:768].rearrange("p (b h) -> p b h", b=B)
        a_tok = slab[:, 768:1024].rearrange("p (b h) -> p b h", b=B)
        ncs = slab[:, 1024:1280].rearrange("p (b h) -> p b h", b=B)
        expnm = sb("expnm", [P, B, NH])
        fin = slab[:, 1280:2048].rearrange("p (k m) -> p k m", k=3)
        kslot = slab2[:, 256:512].rearrange("p (s t) -> p s t", s=2)
        qslot = slab[:, 0:512].rearrange("p (s r t) -> p s r t", s=2, r=2)
        mm = sb("mm", [P, 24])
        gq = sb("gq", [2, 8])
        qs = sb("qs", [P, 40])
        w1n = xn_w1[:, 0:512]
        w2n = xn_w1[:, 512:1024]
        wtmp = xn_w1[:, 1024:2048]
        wqb = xn_w1[:, 3584:4096].bitcast(BF16)
        w1q = slab2[:, 0:256].bitcast(BF16)
        w2q = slab2[:, 256:512].bitcast(BF16).rearrange("p (c d) -> p c d", c=NC)
        aa = sb("aa", [P, B])
        ee = sb("ee", [B, P + 4])
        rowm = sb("rowm", [B, P])
        pathm = Bm[:, 4096:8192].rearrange("p (b j) -> p b j", b=B)
        hmm = sb("hmm", [P, 2, B])
        selw = A[:, 16000:16384].bitcast(BF16).rearrange("p (k n) -> p k n", k=3)
        eT = sb("eT", [P, 2, B])
        ec = sb("ec", [P, B])
        aa_tmp = Bm[:, 10752:14848].rearrange("p (b d) -> p b d", b=B)
        wraw = slab[:, 0:1024].rearrange("p (s c) -> p s c", s=2)
        wcp = slab[:, 1024:2048].rearrange("p (s c) -> p s c", s=2)
        lg = A[:, 15360:15616].rearrange("p (b e) -> p b e", b=B)
        gts = A[:, 15616:15872].rearrange("p (b e) -> p b e", b=B)
        gtT = A[0:32, 15872:16128].rearrange("p (s t) -> p s t", s=2)
        sel = sb("sel", [P, 16])
        seli = sb("seli", [P, 16], U32)
        key, ones32, step = (seli[:, k:k + 1] for k in range(3))
        cand, digit = seli[:, 4:7], seli[:, 8:11]
        ykept = Bm[:, 0:NS * 4096]
        gbias = Bm[:, NS * 4096:(NS + 1) * 4096]

        d_dram = dram("d_scratch", (B, P, P), F32).ap()

        S = {n: sem(n) for n in (
            "pool_step", "dve_step", "act_step",
            "consts_made", "small_in", "b2_in", "small_turned", "small_kept", "tg_in_ready", "tg_ready",
            "csq_done", "bn_done", "ln_sqrt", "ln_done", "shift_ready", "ln_half", "q_turned", "c_turned", "q_kept", "k_kept",
            "gates_summed", "gates_biased", "gates_capped", "nlf_ready", "cumsum_done", "a_ready", "a_turned",
            "m_ready", "m_turned", "m_tok_ready", "expnm_ready", "av_ready", "cut_done", "left_over", "part_ready", "mblk_ready", "vaug_ready",
            "kslot_ready", "qslot_ready", "ld_ready", "sc_ready", "exp_done", "prod_done", "s_high", "s_low", "av_done", "o_kept",
            "gain_ready", "norm_step", "onto_step", "osq_done", "osum_done", "osqrt_done", "x2_ready",
            "mm_ready", "mm_turned", "mm_global", "mm_spread", "scale_ready", "x_scaled", "x_cut", "xq_ready",
            "xq_turned", "xqT_kept", "aw_in", "w_scaled", "wq_ready", "wq_turned", "wq_kept",
            "ffn1_done", "gelu_done", "h_scaled", "h_cut", "hq_ready", "b2_added", "ffn2_done", "ffn2_added",
            "x3T_turned", "x3T_kept", "dsum_done", "dsq_ready", "dist_ready", "row_done", "rowm_done",
            "r9_in", "back_done", "k_made", "k_in",
            "track_done", "e_turned", "e_kept", "far_ready", "path_ready", "expanded", "expanded_added",
            "raw_turned", "raw_kept", "w_split",
            "x4_turned", "x4_kept", "x4_split", "logits_done", "count_ready", "count_all", "gates_ready", "late_added", "bias_added", "gb_kept",
            "gt_turned", "gt_kept", "gb_done", "h_ready", "h_gelu", "h_high", "h_low_even", "h_low_odd", "y_ready",
            "y_added", "stored")}
        x_in = [sem(f"x_in{c}") for c in range(4)]
        ctx_in = [sem(f"ctx_in{c}") for c in range(4)]
        d_out = [sem(f"d_out{c}") for c in range(2)]
        d_in = [sem(f"d_in{c}") for c in range(2)]
        k_last = [sem(f"k_last{q}") for q in range(4)]
        raw_in = [sem(f"raw_in{c}") for c in range(2)]

        def bank(n, a=0, b=512):
            return PS[:, n, a:b]

        def bankb(n):
            return PS[:, n, 0:256].bitcast(BF16)

        def g4(ap, g):
            return ap[:, 4 * g:4 * g + 4]

        def four(ap):
            return ap.rearrange("p (k t) -> p k t", k=4)

        def rep(ap, n):
            return ap.unsqueeze(1).to_broadcast([ap.shape[0], n, ap.shape[1]])

        def heads(m):
            return oall[:, bass.ds(m * 4, 4), :].rearrange("p b (h w) -> p (b h) w", h=NH)

        def last(ap, n):
            return ap.unsqueeze(2).to_broadcast([ap.shape[0], ap.shape[1], n])

        def raw_load(act, n):
            if n < E:
                dst, src = four(wraw[:, n % 2, :]), m_w1[n].rearrange("(c p) d -> p c d", c=NC)
            else:
                dst, src = wraw[:, n % 2, :], m_w2[n - E]
            act.dma_start(dst, src).then_inc(raw_in[n % 2], 16)

        def steps_out(sp, c, parts=range(3, -1, -1)):
            first, rows = CHUNKS[c]
            h = rows // 4
            sp.wait_ge(S["back_done"], CUT_DONE[c])
            for q in parts:
                arrived = S["k_in"] if c < NRC - 1 else k_last[q]
                sp.dma_start(kb[0:B, first + h * q:first + h * q + h], ch_d[32 * q:32 * q + 32, 0:h]).then_inc(arrived, 16)

        def back(dve, c, stage, q0, q1):
            h = CHUNKS[c][1] // 4
            q = slice(q0, q1)
            end = c == NRC - 1

            def after(stage):
                dve.wait_ge(S["back_done"], BACK[c] + (stage if end else stage * h + q0) + 1)
            if stage == MIN:
                if q0 == 0:
                    dve.wait_ge(S["r9_in"], R9 * (c + 1))
                    if c >= 1:
                        dve.wait_ge(S["k_made"], c)
                ins = dve.tensor_tensor(ch_m[:, q], r9[:, q0:q1, 0:P], r9[:, q0:q1, 1:RW], ALU.min)
            elif stage == DIAG:
                ins = dve.tensor_tensor(ch_g[:, q], r9[:, q0:q1, 0:P], r9[:, q0:q1, 1:RW], ALU.is_le)
            elif stage == LEFT:
                after(MIN)
                ins = dve.tensor_tensor(ch_m[:, q], r9[:, q0 + 1:q1 + 1, 0:P], ch_m[:, q], ALU.is_ge)
            elif stage == SCAN:
                if not end:
                    dve.wait_ge(S["k_made"], c + 1)
                ks = ch_k[:, q].rearrange("p r j -> p (r j)")
                ins = dve.tensor_tensor_scan(ch_s[:, q, 1:RW].rearrange("p r j -> p (r j)"), ks, ks, 0.0, ALU.max, ALU.max)
            else:
                if end:
                    dve.wait_ge(S["back_done"], CUT_DONE[c] - 1)
                else:
                    after(SCAN)
                if c >= 1:
                    dve.wait_ge(S["k_in"], 64 * c)
                ins = dve.tensor_tensor(ch_d[:, q], ch_s[:, q, 1:RW], ch_s[:, q, 0:P], ALU.subtract)
            ins.then_inc(S["back_done"], 1)

        def back_part(dve, c, n):
            h = CHUNKS[c][1] // 4
            each = 1 if CHUNKS[c + 1][1] == RC else 2
            n -= PLACE_0
            first, wait = 3 * h // each, 4 * h // (1 + each)
            for k in range(each):
                if 0 <= n < first:
                    m = each * n + k
                elif first + wait <= n:
                    m = each * (n - wait) + k
                else:
                    return
                if m < 5 * h:
                    back(dve, c, m // h, m % h, m % h + 1)

        block = stack.enter_context(nc.Block())

        @block.sync
        def _(sp):
            small = [(ifw_n, if_w), (ifb_b[:], if_b.partition_broadcast(P)),
                     (onw_b[:], on_w.partition_broadcast(P)),
                     (tgr[:, 0:2], g_x.partition_broadcast(P)), (tgr[:, 2:4], g_f.partition_broadcast(P)),
                     (ab1_n, a_b1.rearrange("(c p) -> c p", c=NC)), (ab2_b[:], a_b2.partition_broadcast(P)),
                     (gw_n, gate_w), (mb1_n, m_b1.rearrange("e (c p) -> (e c) p", c=NC))]
            for c in range(4):
                sp.dma_start(xs[:, 8 * c:8 * c + 8], x[8 * c:8 * c + 8].rearrange("b t d -> t b d")).then_inc(x_in[c], 16)
                sp.dma_start(cs[:, 8 * c:8 * c + 8], ctx_[8 * c:8 * c + 8].rearrange("b t d -> t b d")).then_inc(ctx_in[c], 16)
                if c == 0:
                    for dst, src in small:
                        sp.dma_start(dst, src).then_inc(S["small_in"], 16)
            sp.wait_ge(S["consts_made"], 1)
            for k in range(4):
                sp.dma_start(b2blk[8 * k:8 * k + 8, k, :], m_b2).then_inc(S["b2_in"], 16)
            sp.wait_ge(S["q_turned"], 2)
            sp.dma_start(w1n.rearrange("p (c d) -> p c d", c=NC), a_w1.rearrange("(c p) d -> p c d", c=NC)).then_inc(S["aw_in"], 16)
            sp.dma_start(w2n, a_w2).then_inc(S["aw_in"], 16)
            def distances(c, b0, b1):
                sp.dma_start(dring[b0:b1, c], d_dram[b0:b1, RC * c:RC * c + RC]).then_inc(d_in[c], 16)
            early = 4 * (G4 - 2)
            for g in range(G4):
                sp.wait_ge(S["dist_ready"], g + 1)
                sp.dma_start(d_dram[4 * g:4 * g + 4].rearrange("b i j -> i b j"), g4(dist, g)).then_inc(d_out[g // (G4 - 2)], 16)
            sp.wait_ge(d_out[0], 16 * (G4 - 2))
            distances(0, 0, early)
            sp.wait_ge(d_out[1], 32)
            distances(0, early, B)
            distances(1, 0, early)
            distances(1, early, B)
            for c, (first, rows) in enumerate(CHUNKS):
                if c >= 1:
                    sp.wait_ge(S["back_done"], LEFT_DONE[c - 1])
                h = rows // 4
                above = rring[0:B, (c - 1) % 2, CHUNKS[c - 1][1]] if c else rring[0:B, 0, 0]
                for q in range(4):
                    sp.wait_ge(S["row_done"], first + h * (q + 1))
                    if q == 0:
                        sp.dma_start(r9[0:B, 0], above).then_inc(S["r9_in"], 16)
                    lo = 0 if q else 1
                    sp.dma_start(r9[32 * q:32 * q + 32, lo:h + 1], rring[0:B, c % 2, h * q + lo:h * q + h + 1]).then_inc(S["r9_in"], 16)
                if c >= 1:
                    steps_out(sp, c - 1)
                if c < 2:
                    sp.dma_start(dring[0:B, c], d_dram[:, RC * (c + 2):RC * (c + 3)]).then_inc(d_in[c], 16)
            steps_out(sp, NRC - 1, (3, 1))
            for blk in range(2 * NS):
                sp.wait_ge(S["bias_added"], blk + 1)
                sp.dma_start(out[4 * blk:4 * blk + 4].rearrange("b t d -> t b d"), g4(xs, blk)).then_inc(S["stored"], 16)
            with sp.Fori(2 * NS, G4) as blk:
                sp.wait_ge(S["y_added"], blk * E + (E + 2))
                sp.dma_start(out[bass.ds(blk * 4, 4)].rearrange("b t d -> t b d"),
                             xs[:, bass.ds(blk * 4, 4)]).then_inc(S["stored"], 16)
            sp.wait_ge(S["stored"], 16 * G4)

        @block.gpsimd
        def _(pool):
            steps = [0]

            def link(ins):
                steps[0] += 1
                ins.then_inc(S["pool_step"], 1)
                pool.wait_ge(S["pool_step"], steps[0])

            pool.sem_inc(S["h_low_even"], 2)
            pool.memset(identf[:], 0.0)
            pool.memset(identb[:], 0.0)
            pool.memset(tri[:], 1.0)
            pool.memset(neg[:], 0.0)
            pool.memset(ones[:], 1.0)
            pool.iota(pidx[:, 0:1], [[0, 1]], base=0, channel_multiplier=1)
            pool.iota(hidx[:], [[1, 8]], base=0, channel_multiplier=0)
            pool.iota(iota2[:], [[2, P]], base=0, channel_multiplier=0, allow_small_or_imprecise_dtypes=True)
            pool.memset(mhalf[:], -0.5)
            link(pool.memset(b2blk[:], 0.0))
            line = [[1, P]]
            pool.affine_select(out=identf[:], in_=identf[:], compare_op=ALU.not_equal, fill=1.0, base=0, pattern=line, channel_multiplier=-1)
            pool.affine_select(out=identb[:], in_=identb[:], compare_op=ALU.not_equal, fill=1.0, base=0, pattern=line, channel_multiplier=-1)
            pool.affine_select(out=tri[:], in_=tri[:], compare_op=ALU.is_ge, fill=0.0, base=0, pattern=line, channel_multiplier=-1)
            pool.affine_select(out=neg[:], in_=neg[:], compare_op=ALU.is_ge, fill=-BIG, base=0, pattern=line, channel_multiplier=-1).then_inc(S["consts_made"], 1)
            for c in range(4):
                pool.wait_ge(ctx_in[c], 16)
            vh4 = vh.rearrange("p b (h w) -> p (b h) w", h=NH)
            vl4 = vl.rearrange("p b (h w) -> p (b h) w", h=NH)
            c4 = cs[:].rearrange("p b (h w) -> p (b h) w", h=NH)
            pool.memset(vh4[:, :, DH:VW], 1.0)
            pool.memset(vl4[:, :, DH:VW], 0.0)
            link(pool.tensor_scalar(vh4[:, :, 0:DH], c4, 1.0, 0.0, ALU.mult, ALU.add))
            pool.tensor_tensor(vl4[:, :, 0:DH], c4, vh4[:, :, 0:DH], ALU.subtract).then_inc(S["vaug_ready"], 1)
            pool.wait_ge(S["k_kept"], G4)
            pool.wait_ge(S["gain_ready"], 1)

            def slot_keys(g, k):
                pool.wait_ge(S["sc_ready"], g * 8 + (2 * k + 2))
                pool.tensor_copy(kslot[:, k % 2, :], kT[:, bass.ds(g * 512 + k * P, P)]).then_inc(S["kslot_ready"], 1)

            def squares(m):
                pool.wait_ge(S["o_kept"], m * 8 + 10)
                o3 = heads(m)[:, :, 0:DH]
                pool.tensor_tensor(osq[:, bass.ds(m * 512, 512)].rearrange("p (m w) -> p m w", w=DH), o3, o3, ALU.mult).then_inc(S["osq_done"], 1)

            def chain(ins, m, i):
                ins.then_inc(S["onto_step"], 1)
                pool.wait_ge(S["onto_step"], m * 4 + i)

            def inverse_roots(m, part):
                if part == 0:
                    pool.wait_ge(S["osum_done"], m + 1)
                f = fin[:, 1, bass.ds(m * 32 + 16 * part, 16)]
                chain(pool.tensor_tensor(f, f, mhalf[:, 0:16], ALU.pow), m, 1 + part)

            def normed(m):
                t = osq[:, bass.ds(m * 512, 512)]
                f = fin[:, 1, bass.ds(m * 32, 32)]
                chain(pool.tensor_tensor(t.rearrange("p (m w) -> p m w", w=DH), heads(m)[:, :, 0:DH], last(f, DH), ALU.mult), m, 3)

            def onto(m):
                t4 = four(osq[:, bass.ds(m * 512, 512)])
                chain(pool.tensor_tensor(t4, t4, rep(onw_b[:], 4), ALU.mult), m, 4)
                row = xs[:, bass.ds(m * 4, 4), :]
                pool.tensor_tensor(row, row, t4, ALU.add).then_inc(S["x2_ready"], 1)

            for g in range(G4):
                slot_keys(g, 0)
                if g >= 2:
                    inverse_roots(g - 2, 1)
                slot_keys(g, 1)
                if g >= 2:
                    normed(g - 2)
                    onto(g - 2)
                slot_keys(g, 2)
                if g >= 1:
                    squares(g - 1)
                slot_keys(g, 3)
                if g >= 1:
                    inverse_roots(g - 1, 0)
            inverse_roots(G4 - 2, 1)
            normed(G4 - 2)
            onto(G4 - 2)
            pool.wait_ge(S["scale_ready"], 2)
            for c in range(4):
                w = slice(1024 * c, 1024 * c + 1024)
                pool.wait_ge(S["x_cut"], c + 1)
                pool.tensor_scalar(xq[:, w], xn_w1[:, w], 1.0, -MAGIC, ALU.mult, ALU.add).then_inc(S["xq_ready"], 1)
            pool.wait_ge(S["ln_done"], G4 + 4)
            pool.wait_ge(S["ln_half"], 1)
            pool.tensor_tensor(xs[:], xs[:], rep(ab2_b[:], B), ALU.add).then_inc(S["b2_added"], 1)
            for nb in range(G4):
                w = slice(512 * nb, 512 * nb + 512)
                pool.wait_ge(S["h_cut"], nb + 1)
                pool.tensor_scalar(hq[:, :, w], hid[:, :, w], 1.0, -MAGIC, ALU.mult, ALU.add).then_inc(S["hq_ready"], 1)
            pool.wait_ge(S["dsum_done"], G4)
            def split_weights(n):
                wh, wl = (w1h, w1l) if n < E else (w2h, w2l)
                pool.wait_ge(S["raw_kept"], n + 1)
                src = four(wcp[:, n % 2, :])
                link(pool.tensor_scalar(wh[:, n % E], src, 1.0, 0.0, ALU.mult, ALU.add))
                pool.tensor_tensor(wl[:, n % E], src, wh[:, n % E], ALU.subtract).then_inc(S["w_split"], 1)

            for n in range(2 * E):
                split_weights(n)
            pool.memset(ch_s[:, :, 0:1], 0.0)
            for c in range(NRC - 1):
                h = CHUNKS[c][1] // 4
                pool.wait_ge(S["back_done"], LEFT_DONE[c])
                link(pool.tensor_tensor(ch_k[:, 0:h], rep(iota2[:], h), ch_g[:, 0:h], ALU.subtract))
                pool.tensor_tensor(ch_k[:, 0:h], ch_k[:, 0:h], ch_m[:, 0:h], ALU.mult).then_inc(S["k_made"], 1)
            for g in range(G4):
                pool.wait_ge(S["x4_kept"], g + 1)
                w = slice(512 * g, 512 * g + 512)
                pool.tensor_tensor(x4l[:, w], x4f[:, g % 2, :], x4h[:, w], ALU.subtract).then_inc(S["x4_split"], 1)
            def low(blk, e, c):
                pool.wait_ge(S["h_high"], blk * (E * NC) + (e * NC + c + 1))
                pool.tensor_tensor(hl[:, e % 2, c, :], hf[:, c, :], hh[:, e % 2, c, :], ALU.subtract)\
                    .then_inc(S["h_low_even" if c % 2 == 0 else "h_low_odd"], 1)

            with pool.Fori(0, NS) as blk:
                for e in range(E):
                    for c in range(NC):
                        low(blk, e, c)
            with pool.Fori(NS, G4) as blk:
                for e in range(E):
                    for c in range(0, NC, 2):
                        low(blk, e, c)

        @block.scalar
        def _(act):
            steps = [0]

            def link(ins):
                steps[0] += 1
                ins.then_inc(S["act_step"], 1)
                act.wait_ge(S["act_step"], steps[0])

            def ln(n, halves=(0, 1)):
                for h in halves:
                    act.wait_ge(S["bn_done"], 2 * n + h + 1)
                    act.activation(lnt[:, 5, 16 * h:16 * h + 16], lnt[:, 4, 16 * h:16 * h + 16], ACT.Sqrt, bias=cst[:, 0:1]).then_inc(S["ln_sqrt"], 1)

            act.sem_inc(S["s_high"], 2)
            act.sem_inc(S["exp_done"], 2)
            act.sem_inc(S["o_kept"], 2)
            act.sem_inc(S["h_gelu"], 4)
            act.wait_ge(S["tg_in_ready"], 1)
            act.activation(tg[:], tgr[:], ACT.Tanh).then_inc(S["tg_ready"], 1)
            for g in range(G4):
                act.wait_ge(S["c_turned"], g + 1)
                act.activation(kT[:, 512 * g:512 * g + 512], bank(2 + g % 2), ACT.Copy).then_inc(S["k_kept"], 1)
                if g in (3, 4):
                    ln(0, (g - 3,))
            for g in range(G4):
                act.wait_ge(S["q_turned"], g + 1)
                act.activation(qT[:, 512 * g:512 * g + 512], bank(g % 2), ACT.Copy).then_inc(S["q_kept"], 1)
                if g < 4:
                    act.activation(aa_tmp[:, 8 * g:8 * g + 8], cs[:, 8 * g:8 * g + 8], ACT.Square).then_inc(S["csq_done"], 1)
            act.wait_ge(S["gates_biased"], 1)
            act.activation(pre, pre, ACT.Tanh, scale=1.0 / GATE_CAP).then_inc(S["gates_capped"], 1)
            act.wait_ge(S["gates_capped"], 1)
            link(act.activation(nlf, pre[:, :, NH:2 * NH], ACT.Exp, scale=-GATE_CAP))
            act.activation(nlf, nlf, ACT.Ln, bias=cst[:, 3:4]).then_inc(S["nlf_ready"], 1)
            fl = lambda v, w: v[:, w].rearrange("p g t -> p (g t)")
            for r in range(2):
                for w in range(2):
                    if r == 0:
                        act.wait_ge(S["m_ready" if w else "av_ready"], G4 if w else 2)
                    else:
                        act.wait_ge(S["left_over"], w + 1)
                    act.activation(fl(av_cut, w), fl(av_res if r else av, w), ACT.Copy).then_inc(S["cut_done"], 1)
            act.wait_ge(S["left_over"], 3)
            act.activation(fl(av_part, 0), fl(av_res, 0), ACT.Identity, scale=pm[:, 4:5]).then_inc(S["part_ready"], 1)
            act.wait_ge(S["m_tok_ready"], 1)
            act.activation(expnm[:], expnm[:], ACT.Exp).then_inc(S["expnm_ready"], 1)
            act.wait_ge(S["scale_ready"], 1)
            act.activation(wtmp[:, 0:HID], w1n, ACT.Identity, scale=qs[:, 2:3], bias=cst[:, 2:3])
            act.activation(wtmp[:, HID:2 * HID], w2n, ACT.Identity, scale=qs[:, 3:4], bias=cst[:, 2:3]).then_inc(S["w_scaled"], 1)
            def high(g, m):
                act.wait_ge(S["prod_done"], g * 8 + (m + 3))
                act.wait_ge(S["av_done"], g * 8 + (m + 1))
                act.activation(sh[:, m % 2, :], smat[:, m % 2, :], ACT.Copy).then_inc(S["s_high"], 1)

            def keep(g, m):
                act.wait_ge(S["av_done"], g * 8 + (m + 3))
                o = 2 * VW * (m % 2)
                own = PS[:, 6 + m % 2, o:o + 4 * 7 * VW].rearrange("p (j w) -> p j w", j=4)[:, :, 0:VW]
                act.activation(oall[:, bass.ds(g * 4 + m // 2, 1), 4 * VW * (m % 2):4 * VW * (m % 2) + 4 * VW]
                               .rearrange("p b (j w) -> p (b j) w", j=4), own, ACT.Copy).then_inc(S["o_kept"], 1)

            def units(g, first=False):
                for m in range(8):
                    act.wait_ge(S["ld_ready"], g * 8 + (m + 1))
                    act.wait_ge(S["prod_done"], g * 8 + (m + 1))
                    act.activation(decay[:, m % 2, :], bank(m % 2), ACT.Exp).then_inc(S["exp_done"], 1)
                    if m or not first:
                        high(g, m - 1)
                    if m >= 3 or not first:
                        keep(g, m - 3)

            units(0, first=True)
            with act.Fori(1, G4) as g:
                units(g)
            high(G4, -1)
            for m in (-3, -2, -1):
                keep(G4, m)
            act.wait_ge(S["osum_done"], G4)
            f = fin[:, 1, 32 * (G4 - 1):32 * G4]
            act.activation(f, f, ACT.Sqrt).then_inc(S["osqrt_done"], 1)
            ln(1, (0,))
            act.wait_ge(S["shift_ready"], 1)
            for b in range(16):
                if b == 2:
                    ln(1, (1,))
                ins = act.activation(xn[:, b, :], xs[:, b, :], ACT.Identity, scale=lnt[:, 7, b:b + 1], bias=lnt[:, 1, b:b + 1])
            ins.then_inc(S["ln_half"], 1)
            act.wait_ge(S["ln_half"], 1)
            for n in range(2):
                act.wait_ge(S["wq_turned"], n + 1)
                dst = w1q if n == 0 else w2q.rearrange("p c d -> p (c d)")
                act.activation(dst, bankb(5 + n), ACT.Copy).then_inc(S["wq_kept"], 1)

            def scale_x(c):
                if c >= 2:
                    act.wait_ge(S["ln_done"], G4 + 2 * c - 2)
                v = xn[:, 8 * c:8 * c + 8]
                act.activation(v, v, ACT.Identity, scale=qs[:, 8:9], bias=cst[:, 2:3]).then_inc(S["x_scaled"], 1)
            act.wait_ge(S["scale_ready"], 2)
            scale_x(0)
            scale_x(1)
            for nb in range(G4):
                act.wait_ge(S["xq_turned"], nb + 1)
                act.activation(xqT[:, 512 * nb:512 * nb + 512], bankb(nb % 2), ACT.Copy).then_inc(S["xqT_kept"], 1)
                for c in range(NC):
                    act.wait_ge(S["ffn1_done"], NC * nb + c + 1)
                    act.activation(hid[:, c, 512 * nb:512 * nb + 512], bank(2 + c), ACT.Gelu, scale=qs[:, 12:13],
                                   bias=small_t[:, 80 + c:81 + c]).then_inc(S["gelu_done"], 1)
                if nb < 2:
                    scale_x(2 + nb)
            act.wait_ge(S["scale_ready"], 3)
            for nb in range(G4):
                v = hid[:, :, 512 * nb:512 * nb + 512]
                act.activation(v, v, ACT.Identity, scale=qs[:, 16:17], bias=cst[:, 2:3]).then_inc(S["h_scaled"], 1)
            raw_load(act, 0)
            raw_load(act, 1)
            ln(2, (0,))
            for g in range(G4 + 1):
                if g < G4:
                    if g == 1:
                        ln(2, (1,))
                    act.wait_ge(S["x3T_turned"], g + 1)
                    if g >= 2:
                        act.wait_ge(S["dsum_done"], g - 1)
                    act.activation(xT2[:, g % 2, :], bank(g % 2), ACT.Copy, scale=-2.0)
                    act.activation(xTsq[:, g % 2, :], bank(g % 2), ACT.Square).then_inc(S["x3T_kept"], 1)
                if g >= 1:
                    act.wait_ge(S["dsq_ready"], g)
                    act.activation(g4(dist, g - 1), g4(dsq, g - 1), ACT.Sqrt).then_inc(S["dist_ready"], 1)
            for n in range(2 * E):
                if n >= 2:
                    act.wait_ge(S["w_split"], n - 1)
                act.wait_ge(S["raw_turned"], n + 1)
                if n + 2 < 2 * E:
                    raw_load(act, n + 2)
                act.activation(wcp[:, n % 2, :], bank(4 + n % 2), ACT.Copy).then_inc(S["raw_kept"], 1)
            steps_out(act, NRC - 1, (2, 0))
            act.wait_ge(S["e_kept"], 1)
            for g in range(G4):
                for b in range(4 * g, 4 * g + 4):
                    ins = act.activation(pathm[:, b, :], iota2[:], ACT.Abs, bias=ec[:, b:b + 1])
                ins.then_inc(S["far_ready"], 1)
            ln(3, (0,))
            for g in range(G4):
                if g == 3:
                    ln(3, (1,))
                act.wait_ge(S["x4_turned"], g + 1)
                if g >= 2:
                    act.wait_ge(S["logits_done"], g - 1)
                    act.wait_ge(S["x4_split"], g - 1)
                act.activation(x4f[:, g % 2, :], bank(6 + g % 2), ACT.Copy)
                act.activation(x4h[:, 512 * g:512 * g + 512], bank(6 + g % 2), ACT.Copy).then_inc(S["x4_kept"], 1)
            def gelu(blk, e):
                for c in range(NC):
                    act.wait_ge(S["h_ready"], blk * (E * NC) + (e * NC + c + 1))
                    act.wait_ge(S["h_low_even" if c % 2 == 0 else "h_low_odd"], blk * (2 * E) + (2 * e + c // 2 + 1))
                    b1 = small_t[:, 48 + e * NC + c:49 + e * NC + c]
                    act.activation(hf[:, c, :], bank(c), ACT.Gelu_apprx_tanh, bias=b1).then_inc(S["h_gelu"], 1)

            def keep_y(blk, e):
                act.wait_ge(S["y_ready"], blk * E + (e + 3))
                act.activation(ykept[:, bass.ds(blk * (512 * E) + e * 512, 512)], bank(4 + e % 2), ACT.Copy).then_inc(S["y_added"], 1)

            gelu(0, 0)
            with act.Fori(0, NS) as blk:
                for e in range(1, E):
                    gelu(blk, e)
                    keep_y(blk, e - 1)
                gelu(blk + 1, 0)
                keep_y(blk, E - 1)
            for e in range(1, E + 2):
                if e < E:
                    gelu(NS, e)
                if e - 1 < G4:
                    act.wait_ge(S["gt_turned"], e)
                    act.activation(gtT[:, (e - 1) % 2, :], PS[0:32, 6, 0:P], ACT.Copy).then_inc(S["gt_kept"], 1)
                if e >= 2:
                    act.wait_ge(S["gb_done"], e - 1)
                    act.activation(gbias[:, 512 * (e - 2):512 * (e - 1)], bank(7), ACT.Copy).then_inc(S["gb_kept"], 1)
            with act.Fori(NS + 1, G4) as blk:
                for e in range(E):
                    gelu(blk, e)

        @block.vector
        def _(dve):
            steps = [0]

            def link(ins):
                steps[0] += 1
                ins.then_inc(S["dve_step"], 1)
                dve.wait_ge(S["dve_step"], steps[0])

            def ts(out, a, s1, s2, op0, op1=ALU.bypass):
                return dve.tensor_scalar(out, a, s1, s2, op0, op1)

            def ln_stats(n, h):
                w = slice(16 * h, 16 * h + 16)
                t = lambda k: lnt[:, k, w]
                dve.tensor_tensor(t(0), bns[:, w, 1], bns[:, w, 4], ALU.add)
                dve.tensor_tensor(t(1), bns[:, w, 1], bns[:, w, 4], ALU.subtract)
                link(dve.tensor_tensor(t(2), bns[:, w, 2], bns[:, w, 5], ALU.add))
                ts(t(3), t(0), 0.5, None, ALU.mult)
                link(dve.tensor_tensor(t(6), t(1), t(1), ALU.mult))
                link(ts(t(6), t(6), 0.25, None, ALU.mult))
                dve.scalar_tensor_tensor(out=t(4), in0=t(2), scalar=1.0 / D, in1=t(6), op0=ALU.mult, op1=ALU.add).then_inc(S["bn_done"], 1)

            def ln_scales(n, h):
                w = slice(16 * h, 16 * h + 16)
                dve.wait_ge(S["ln_sqrt"], 2 * n + h + 1)
                link(dve.reciprocal(lnt[:, 7, w], lnt[:, 5, w]))

            def ln_apply(h, src, dst, groups=range(4)):
                for b in range(16 * h + 4 * groups[0], 16 * h + 4 * groups[-1] + 4):
                    ins = ts(dst[:, b, :], src[:, b, :], lnt[:, 3, b:b + 1], lnt[:, 7, b:b + 1], ALU.subtract, ALU.mult)
                    if b % 4 == 3:
                        ins.then_inc(S["ln_done"], 1)

            def ln(n, src, dst, src_ready=None):
                for h in range(2):
                    for b in range(16 * h, 16 * h + 16):
                        if src_ready is not None:
                            src_ready(b)
                        ins = dve.bn_stats(bns[:, b, :], src[:, b, :])
                    link(ins)
                    ln_stats(n, h)
                for h in range(2):
                    ln_scales(n, h)
                    ln_apply(h, src, dst)

            def spread(n):
                dve.wait_ge(S["mm_turned"], n + 1)
                link(dve.tensor_reduce(gq[0:2, 0:1], PS[0:2, 7, 0:P], AX, ALU.max))
                ts(gq[0:2, 2:4], identf[0:2, 0:2], gq[0:2, 0:1], None, ALU.mult).then_inc(S["mm_global"], 1)
                dve.wait_ge(S["mm_spread"], n + 1)
                link(dve.tensor_copy(mm[:, 2:4], bank(7, P, P + 2)))

            def affine(o):
                q = lambda k: qs[:, o + k:o + k + 1]
                link(dve.tensor_tensor(q(0), mm[:, 2:3], mm[:, 3:4], ALU.add))
                link(ts(q(1), q(0), 1.0 / 255.0, 1e-8, ALU.mult, ALU.max))
                link(dve.reciprocal(q(0), q(1)))
                link(ts(q(2), q(0), mm[:, 3:4], MAGIC, ALU.mult, ALU.add))
                link(ts(q(2), q(2), MAGIC, -128.0, ALU.subtract, ALU.add))
                link(ts(q(2), q(2), -128.0, 127.0, ALU.max, ALU.min))
                ts(q(3), q(2), -1.0, MAGIC + 127.0, ALU.mult, ALU.add)
                link(ts(q(2), q(2), -1.0, MAGIC - 128.0, ALU.mult, ALU.add))

            dve.sem_inc(S["prod_done"], 2)
            dve.sem_inc(S["s_low"], 2)
            dve.sem_inc(S["y_added"], 2)
            dve.sem_inc(S["h_low_odd"], 2)
            dve.memset(cst[:, 0:1], LN_EPS)
            dve.memset(cst[:, 2:3], MAGIC)
            dve.memset(cst[:, 3:4], 1.0)
            dve.wait_ge(S["consts_made"], 1)
            ts(pidx[:, 1:2], pidx[:, 0:1], 3, 3, ALU.logical_shift_right, ALU.bitwise_and)
            ts(pidx[:, 2:3], pidx[:, 0:1], 4, 1, ALU.logical_shift_right, ALU.bitwise_and)
            ts(pidx[:, 3:4], pidx[:, 0:1], 7, None, ALU.bitwise_and)
            link(ts(pidx[:, 4:5], pidx[:, 0:1], 5, None, ALU.logical_shift_right))
            ts(pm[:, 0:1], pidx[:, 2:3], 0.0, None, ALU.is_equal)
            ts(pm[:, 1:2], pidx[:, 2:3], 1.0, None, ALU.is_equal)
            ts(pm[:, 2:3], pidx[:, 1:2], 1.0, -1.0, ALU.is_ge, ALU.mult)
            ts(pm[:, 3:4], pidx[:, 1:2], 2.0, -1.0, ALU.is_ge, ALU.mult)
            ts(pm[:, 4:5], pidx[:, 1:2], 3.0, None, ALU.is_lt)
            dve.tensor_copy(pm[:, 5:6], pidx[:, 3:4])
            for k in range(4):
                ts(pm[:, 6 + k:7 + k], pidx[:, 4:5], float(k), None, ALU.is_equal)
            link(dve.tensor_copy(hidf[:], hidx[:]))
            link(ts(hpos[:], hidf[:], pm[:, 5:6], None, ALU.is_equal))
            ts(hneg[:], hpos[:], -1.0, None, ALU.mult)
            for k in range(4):
                ts(selb[:, k, :], ones[:], pm[:, 6 + k:7 + k], None, ALU.mult)
                ins = ts(bmask[:, k], last(hpos[:], P), pm[:, 6 + k:7 + k], None, ALU.mult)
            link(ins)
            dve.wait_ge(S["small_in"], 16 * 9)
            dve.tensor_copy(tgr[:, 0:1], tgr[:, 0:1]).then_inc(S["tg_in_ready"], 1)

            def x_here(b):
                if b % 8 == 0:
                    dve.wait_ge(x_in[b // 8], 16)
            for h in range(2):
                for b in range(16 * h, 16 * h + 16):
                    x_here(b)
                    ins = dve.bn_stats(bns[:, b, :], xs[:, b, :])
                link(ins)
                ln_stats(0, h)
                if h == 0:
                    dve.wait_ge(S["small_turned"], 1)
                    link(dve.tensor_copy(small_t[:, 0:92], bank(6, 0, 92)))
                    dve.tensor_tensor(wkv[:], small_t[:, 16:32], small_t[:, 32:48], ALU.add).then_inc(S["small_kept"], 1)
            for h in range(2):
                ln_scales(0, h)
                ln_apply(h, xs, xn)
            dve.wait_ge(S["aw_in"], 32)
            dve.wait_ge(S["q_turned"], 4)
            dve.scalar_tensor_tensor(out=wtmp[:, 0:HID], in0=w1n, scalar=-1.0, in1=w1n, op0=ALU.mult, op1=ALU.max)
            link(dve.scalar_tensor_tensor(out=wtmp[:, HID:2 * HID], in0=w2n, scalar=-1.0, in1=w2n, op0=ALU.mult, op1=ALU.max))
            dve.tensor_reduce(mm[:, 0:2], wtmp.rearrange("p (w c) -> p w c", w=2), AX, ALU.max).then_inc(S["mm_ready"], 1)
            dve.wait_ge(S["csq_done"], 4)
            dve.tensor_reduce(aa[:], aa_tmp, AX, ALU.add)
            dve.wait_ge(S["gates_summed"], 1)
            link(dve.tensor_tensor(pre, bank(5).rearrange("p (b w) -> p b w", b=B), rep(ifb_b[:], B), ALU.add))
            dve.wait_ge(S["gates_summed"], 2)
            dve.tensor_tensor(pre, bank(4).rearrange("p (b w) -> p b w", b=B), pre, ALU.add).then_inc(S["gates_biased"], 1)
            spread(0)
            link(ts(qs[:, 0:2], mm[:, 2:4], 1.0 / 127.0, 1e-8, ALU.mult, ALU.max))
            dve.reciprocal(qs[:, 2:4], qs[:, 0:2]).then_inc(S["scale_ready"], 1)
            dve.wait_ge(S["cumsum_done"], 1)
            csum = bank(5, 0, B * NH).rearrange("p (b h) -> p b h", b=B)
            dve.tensor_copy(ncs, csum)
            link(dve.scalar_tensor_tensor(out=a_tok, in0=pre[:, :, 0:NH], scalar=GATE_CAP, in1=csum, op0=ALU.mult, op1=ALU.add))
            arep = A[:, 12288:13312].rearrange("p (b r h) -> p b r h", b=B, r=4)
            dve.tensor_copy(arep, a_tok.unsqueeze(2).to_broadcast([P, B, 4, NH])).then_inc(S["a_ready"], 1)
            for j in range(2):
                dve.wait_ge(S["a_turned"], j + 1)
                dve.tensor_copy(av[:, 0, 4 * j:4 * j + 4, :].rearrange("p g t -> p (g t)"), bank(j)).then_inc(S["av_ready"], 1)
            dve.wait_ge(S["av_ready"], 2)
            for g in range(G4):
                dve.tensor_tensor_scan(av[:, 1, g, :], av[:, 0, g, :], av[:, 0, g, :], -3e38, ALU.max, ALU.max).then_inc(S["m_ready"], 1)
            fl = lambda v, w: v[:, w].rearrange("p g t -> p (g t)")

            def left_over(w, r, src):
                dve.wait_ge(S["cut_done"], 2 * r + w + 1)
                dve.scalar_tensor_tensor(out=fl(av_res, w), in0=fl(av_cut, w), scalar=pm[:, 2 + r:3 + r], in1=fl(src, w),
                                         op0=ALU.mult, op1=ALU.add).then_inc(S["left_over"], 1)
            left_over(0, 0, av)
            dve.wait_ge(S["m_ready"], G4)
            left_over(1, 0, av)
            for j in range(2):
                dve.wait_ge(S["m_turned"], j + 1)
                mtok = bank(2 + j).rearrange("p (b r h) -> p b r h", b=16, r=4)[:, :, 0, :]
                ins = dve.tensor_tensor(expnm[:, 16 * j:16 * j + 16, :], ncs[:, 16 * j:16 * j + 16, :], mtok, ALU.subtract)
            ins.then_inc(S["m_tok_ready"], 1)
            left_over(0, 1, av_res)
            left_over(1, 1, av_res)
            dve.wait_ge(S["left_over"], 4)
            link(ts(fl(av_part, 1), fl(av_res, 1), pm[:, 4:5], None, ALU.mult))
            for h in range(NH):
                ins = ts(mblk[:, :, h, :], av_part[:, 1], hneg[:, h:h + 1], None, ALU.mult)
            ins.then_inc(S["mblk_ready"], 1)
            def weights_of(g, m, low=True):
                dve.wait_ge(S["exp_done"], g * 8 + (m + 3))
                dve.wait_ge(S["sc_ready"], g * 8 + (m + 5))
                dve.wait_ge(S["s_high"], g * 8 + (m + 1))
                dve.wait_ge(S["s_low"], g * 8 + (m + 1))
                half = m % 2
                dve.tensor_tensor(smat[:, half, :].rearrange("p (j c) -> p j c", j=2),
                                  decay[:, half, :].rearrange("p (j c) -> p j c", j=2),
                                  PS[:, 2 + 2 * half:4 + 2 * half, 0:256], ALU.mult).then_inc(S["prod_done"], 1)
                if low:
                    low_of(g, m - 1)

            def low_of(g, m):
                dve.wait_ge(S["s_high"], g * 8 + (m + 3))
                dve.wait_ge(S["av_done"], g * 8 + (m + 1))
                dve.tensor_tensor(sl[:, m % 2, :], smat[:, m % 2, :], sh[:, m % 2, :], ALU.subtract).then_inc(S["s_low"], 1)

            def slot_queries(g, k):
                dve.wait_ge(S["sc_ready"], g * 8 + (2 * k + 2))
                for r in range(2):
                    ins = ts(qslot[:, k % 2, r], qT[:, bass.ds(g * 512 + k * P, P)], pm[:, r:r + 1], None, ALU.mult)
                ins.then_inc(S["qslot_ready"], 1)

            def divisors(m):
                f = lambda k: fin[:, k, bass.ds(m * 32, 32)]
                dve.wait_ge(S["o_kept"], m * 8 + 10)
                s3 = heads(m)[:, :, DH:VW]
                chain(dve.scalar_tensor_tensor(out=f(0).unsqueeze(2), in0=s3, scalar=-1.0, in1=s3, op0=ALU.mult, op1=ALU.max), m, 1)
                chain(dve.scalar_tensor_tensor(out=f(0), in0=f(0), scalar=4 * BACKEND_EPS,
                                              in1=expnm[:].rearrange("p b h -> p (b h)")[:, bass.ds(m * 32, 32)],
                                              op0=ALU.add, op1=ALU.max), m, 2)
                dve.scalar_tensor_tensor(out=f(2), in0=f(0), scalar=NORM_EPS, in1=f(0), op0=ALU.mult, op1=ALU.mult)

            def mean_squares(m):
                f = lambda k: fin[:, k, bass.ds(m * 32, 32)]
                dve.wait_ge(S["osq_done"], m + 1)
                chain(dve.tensor_reduce(f(1), osq[:, bass.ds(m * 512, 512)].rearrange("p (m w) -> p m w", w=DH), AX, ALU.add), m, 3)
                dve.scalar_tensor_tensor(out=f(1), in0=f(1), scalar=1.0 / DH, in1=f(2), op0=ALU.mult, op1=ALU.add).then_inc(S["osum_done"], 1)

            def x_stats(m):
                dve.wait_ge(S["x2_ready"], m + 1)
                for k in range(4):
                    dve.bn_stats(bns[:].rearrange("p b s -> p (b s)")[:, bass.ds(m * 24 + 6 * k, 6)],
                                 xs[:].rearrange("p b d -> p (b d)")[:, bass.ds(m * 512 + P * k, P)])

            def x_range(m, w):
                op = ALU.max if w == 0 else ALU.min
                return dve.tensor_reduce(hmm[:, w, bass.ds(m * 4, 4)], xs[:, bass.ds(m * 4, 4), :], AX, op)

            def chain(ins, m, i):
                ins.then_inc(S["norm_step"], 1)
                dve.wait_ge(S["norm_step"], m * 3 + i)

            dve.wait_ge(S["tg_ready"], 1)
            ts(onw_b[:], onw_b[:], 1.0, tg[:, 0:1], ALU.add, ALU.mult)
            dve.wait_ge(S["expnm_ready"], 1)
            ts(expnm[:], expnm[:], 4.0, 4 * BACKEND_EPS, ALU.mult, ALU.add).then_inc(S["gain_ready"], 1)
            dve.wait_ge(S["gain_ready"], 1)
            def group(g, norm=True, stats=True, more=True):
                weights_of(g, 0, low=norm)
                slot_queries(g, 1)
                weights_of(g, 1)
                weights_of(g, 2)
                slot_queries(g, 2)
                weights_of(g, 3)
                if norm:
                    divisors(g - 1)
                else:
                    dve.wait_ge(S["w_scaled"], 1)
                    dve.wait_ge(S["q_turned"], G4)
                    link(ts(wtmp, wtmp, MAGIC - 127.0, MAGIC + 127.0, ALU.max, ALU.min))
                    ts(wqb, wtmp, MAGIC, None, ALU.subtract).then_inc(S["wq_ready"], 1)
                weights_of(g, 4)
                slot_queries(g, 3)
                if norm:
                    mean_squares(g - 1)
                weights_of(g, 5)
                if stats:
                    x_stats(g - 2)
                weights_of(g, 6)
                if more:
                    slot_queries(g + 1, 0)
                if stats:
                    x_range(g - 2, 0)
                weights_of(g, 7)
                if stats:
                    x_range(g - 2, 1)

            slot_queries(0, 0)
            group(0, norm=False, stats=False)
            group(1, stats=False)
            with dve.Fori(2, G4 - 1) as g:
                group(g)
            group(G4 - 1, more=False)
            low_of(G4, -1)
            m = G4 - 1
            divisors(m)
            o3 = heads(m)[:, :, 0:DH]
            t = osq[:, 512 * m:512 * m + 512]
            th = t.rearrange("p (m w) -> p m w", w=DH)
            f = fin[:, 1, 32 * m:32 * m + 32]
            dve.tensor_tensor(th, o3, o3, ALU.mult).then_inc(S["osq_done"], 1)
            mean_squares(m)
            x_stats(m - 1)
            x_range(m - 1, 0)
            x_range(m - 1, 1)
            dve.wait_ge(S["osqrt_done"], 1)
            link(dve.reciprocal(f, f))
            link(dve.tensor_tensor(th, o3, last(f, DH), ALU.mult))
            link(dve.tensor_tensor(four(t), four(t), rep(onw_b[:], 4), ALU.mult))
            dve.tensor_tensor(g4(xs, m), g4(xs, m), four(t), ALU.add).then_inc(S["x2_ready"], 1)
            ln_stats(1, 0)
            x_stats(m)
            x_range(m, 0)
            link(x_range(m, 1))
            ln_scales(1, 0)
            dve.scalar_tensor_tensor(out=lnt[:, 1, 0:16], in0=lnt[:, 3, 0:16], scalar=-1.0, in1=lnt[:, 7, 0:16],
                                     op0=ALU.mult, op1=ALU.mult).then_inc(S["shift_ready"], 1)
            ln_stats(1, 1)
            ln_scales(1, 1)
            link(dve.tensor_tensor(hmm[:], hmm[:], rep(lnt[:, 3, :], 2), ALU.subtract))
            link(dve.tensor_tensor(hmm[:], hmm[:], rep(lnt[:, 7, :], 2), ALU.mult))
            link(ts(hmm[:, 1, :], hmm[:, 1, :], -1.0, None, ALU.mult))
            dve.tensor_reduce(mm[:, 0:2], hmm[:], AX, ALU.max).then_inc(S["mm_ready"], 1)
            dve.wait_ge(S["wq_turned"], 2)
            ln_apply(1, xs, xn, range(0, 1))
            spread(1)
            affine_x = 20
            affine(affine_x)
            dve.tensor_copy(qs[:, 8:9], qs[:, affine_x:affine_x + 1])
            link(dve.tensor_tensor(qs[:, 12:13], qs[:, affine_x + 1:affine_x + 2], qs[:, 0:1], ALU.mult))
            dve.tensor_tensor(ab2_b[:], ab2_b[:], tg[:, 2:3].to_broadcast([P, D]), ALU.mult).then_inc(S["scale_ready"], 1)
            ln_apply(1, xs, xn, range(1, 2))

            def cut_x(c):
                v = xn_w1[:, 1024 * c:1024 * c + 1024]
                dve.wait_ge(S["x_scaled"], c + 1)
                ts(v, v, qs[:, affine_x + 2:affine_x + 3], qs[:, affine_x + 3:affine_x + 4], ALU.max, ALU.min).then_inc(S["x_cut"], 1)
            cut_x(0)
            ln_apply(1, xs, xn, range(2, 3))
            cut_x(1)
            ln_apply(1, xs, xn, range(3, 4))
            for nb in range(G4):
                if nb in (1, 2):
                    cut_x(1 + nb)
                dve.wait_ge(S["gelu_done"], NC * (nb + 1))
                v = hid[:, :, 512 * nb:512 * nb + 512]
                dve.tensor_reduce(hmm[:, 0, NC * nb:NC * nb + NC], v, AX, ALU.max)
                ins = dve.tensor_reduce(hmm[:, 1, NC * nb:NC * nb + NC], v, AX, ALU.min)
            link(ins)
            dve.tensor_reduce(mm[:, 0:1], hmm[:, 0, :], AX, ALU.max)
            link(dve.tensor_reduce(mm[:, 4:5], hmm[:, 1, :], AX, ALU.min))
            ts(mm[:, 1:2], mm[:, 4:5], -1.0, None, ALU.mult).then_inc(S["mm_ready"], 1)
            spread(2)
            affine_h = 24
            affine(affine_h)
            link(dve.tensor_tensor(qs[:, 13:14], qs[:, affine_h + 1:affine_h + 2], qs[:, 1:2], ALU.mult))
            link(dve.tensor_tensor(qs[:, 13:14], qs[:, 13:14], tg[:, 2:3], ALU.mult))
            dve.tensor_copy(qs[:, 16:17], qs[:, affine_h:affine_h + 1]).then_inc(S["scale_ready"], 1)

            def add2(nb):
                dve.wait_ge(S["ffn2_done"], nb + 1)
                dve.scalar_tensor_tensor(out=g4(xs, nb), in0=four(bank(nb % 2)), scalar=qs[:, 13:14], in1=g4(xs, nb),
                                         op0=ALU.mult, op1=ALU.add).then_inc(S["ffn2_added"], 1)

            def x3_stats(g):
                dve.wait_ge(S["ffn2_added"], g + 1)
                for b in range(4 * g, 4 * g + 4):
                    ins = dve.bn_stats(bns[:, b, :], xs[:, b, :])
                return ins
            dve.wait_ge(S["b2_added"], 1)
            for nb in range(G4):
                v = hid[:, :, 512 * nb:512 * nb + 512]
                dve.wait_ge(S["h_scaled"], nb + 1)
                ts(v, v, qs[:, affine_h + 2:affine_h + 3], qs[:, affine_h + 3:affine_h + 4], ALU.max, ALU.min).then_inc(S["h_cut"], 1)
                if nb >= 3:
                    add2(nb - 3)
                if nb >= 4:
                    ins = x3_stats(nb - 4)
            link(ins)
            ln_stats(2, 0)
            for nb in range(G4 - 3, G4):
                add2(nb)
                x3_stats(nb - 1)
                if nb == G4 - 3:
                    ln_scales(2, 0)
                    ln_apply(0, xs, xn, range(0, 1))
            link(x3_stats(G4 - 1))
            ln_stats(2, 1)
            ln_apply(0, xs, xn, range(1, 4))
            ln_scales(2, 1)
            ln_apply(1, xs, xn)
            for g in range(G4):
                dve.wait_ge(S["dsum_done"], g + 1)
                for k in range(4):
                    ins = ts(dsq[:, 4 * g + k, :], bank(2 + g % 2, P * k, P * k + P), aa[:, 4 * g + k:4 * g + k + 1], 0.0, ALU.add, ALU.max)
                ins.then_inc(S["dsq_ready"], 1)
            dve.wait_ge(d_out[0], 16 * (G4 - 2))
            dve.wait_ge(d_out[1], 32)
            dve.memset(rring[0:B, 0, 0, 1:RW], BIG)
            link(dve.memset(rring[0:B, :, :, 0:1], BIG))
            link(dve.memset(rring[0:B, 0, 0, 0:1], 0.0))
            dve.memset(ee[:], 2.0 * (P - 1))
            for c, (first, rows) in enumerate(CHUNKS):
                if c >= 2:
                    dve.wait_ge(S["r9_in"], R9 * (c - 1))
                for r in range(rows):
                    i = first + r
                    if i % RC == 0:
                        dve.wait_ge(d_in[i // RC % 2], 16 * (i // (2 * RC) + 2))
                    if c >= 1 and r == rows - 1:
                        dve.wait_ge(S["r9_in"], R9 * c)
                    if r:
                        above = rring[0:B, c % 2, r]
                    else:
                        above = rring[0:B, (c - 1) % 2, CHUNKS[c - 1][1]] if c else rring[0:B, 0, 0]
                    dve.tensor_tensor(rowm[:], above[:, 1:RW], above[:, 0:P], ALU.min).then_inc(S["rowm_done"], 1)
                    if c >= 1:
                        back_part(dve, c - 1, 2 * r)
                    dve.wait_ge(S["rowm_done"], i + 1)
                    dve.tensor_tensor_scan(rring[0:B, c % 2, r + 1, 1:RW], rowm[:], dring[0:B, i // RC % 2, i % RC], BIG, ALU.min, ALU.add)\
                        .then_inc(S["row_done"], 1)
                    if c >= 1:
                        back_part(dve, c - 1, 2 * r + 1)
                    dve.wait_ge(S["row_done"], i + 1)
                if c >= 1:
                    for n in range(2 * rows, 8 * RC):
                        back_part(dve, c - 1, n)
            c = NRC - 1
            h = CHUNKS[c][1] // 4
            for stage in (MIN, DIAG, LEFT):
                back(dve, c, stage, 0, h)
            dve.wait_ge(S["back_done"], LEFT_DONE[c])
            dve.tensor_tensor(ch_k[:, 0:h], rep(iota2[:], h), ch_g[:, 0:h], ALU.subtract).then_inc(S["back_done"], 1)
            dve.wait_ge(S["back_done"], LEFT_DONE[c] + 1)
            dve.tensor_tensor(ch_k[:, 0:h], ch_k[:, 0:h], ch_m[:, 0:h], ALU.mult).then_inc(S["back_done"], 1)
            dve.wait_ge(S["back_done"], LEFT_DONE[c] + 2)
            for q in range(h):
                back(dve, c, SCAN, q, q + 1)
            back(dve, c, CUT, 0, h)
            for i in reversed(range(P)):
                first, rows = CHUNKS[-1]
                if i >= first and (P - 1 - i) % (rows // 4) == 0:
                    dve.wait_ge(k_last[(i - first) // (rows // 4)], 16)
                elif i == first - 1:
                    dve.wait_ge(S["k_in"], 64 * (NRC - 1))
                dve.scalar_tensor_tensor(out=rowm[:], in0=iota2[0:B], scalar=ee[:, i + 1:i + 2], in1=kb[0:B, i, :],
                                         op0=ALU.is_le, op1=ALU.mult, accum_out=ee[:, i:i + 1]).then_inc(S["track_done"], 1)
                dve.wait_ge(S["track_done"], P - i)
            dve.wait_ge(S["e_turned"], 1)
            ends = bank(0, 0, 2 * B).rearrange("p (w b) -> p w b", w=2)
            link(dve.tensor_copy(eT[:, 0, :], ends[:, 0]))
            dve.tensor_tensor(ec[:], eT[:, 0, :], ends[:, 1], ALU.add)
            link(dve.tensor_tensor(eT[:, 1, :], ends[:, 1], eT[:, 0, :], ALU.subtract))
            link(ts(eT[:, 1, :], eT[:, 1, :], 0.5, None, ALU.mult))
            ts(ec[:], ec[:], -0.5, None, ALU.mult).then_inc(S["e_kept"], 1)
            def path_of(g):
                dve.wait_ge(S["far_ready"], g + 1)
                for b in range(4 * g, 4 * g + 4):
                    ins = ts(path[:, b, :], pathm[:, b, :], eT[:, 1, b:b + 1], None, ALU.is_le)
                ins.then_inc(S["path_ready"], 1)

            def add_expanded(g):
                dve.wait_ge(S["expanded"], g + 1)
                dve.scalar_tensor_tensor(out=g4(xs, g), in0=four(bank(1 + g % 2)), scalar=tg[:, 1:2], in1=g4(xs, g),
                                         op0=ALU.mult, op1=ALU.add).then_inc(S["expanded_added"], 1)

            def stats(g):
                dve.wait_ge(S["expanded_added"], g + 1)
                for b in range(4 * g, 4 * g + 4):
                    ins = dve.bn_stats(bns[:, b, :], xs[:, b, :])
                return ins

            for g in range(G4):
                path_of(g)
                if g >= 1:
                    add_expanded(g - 1)
                if g >= 2:
                    ins = stats(g - 2)
                if g == 5:
                    link(ins)
                    ln_stats(3, 0)
                if g == 6:
                    ln_scales(3, 0)
            ln_apply(0, xs, x4)
            add_expanded(7)
            stats(6)
            link(stats(7))
            ln_stats(3, 1)
            ln_scales(3, 1)
            ln_apply(1, xs, x4)
            dve.wait_ge(S["logits_done"], G4)
            lgf = lg.rearrange("p b e -> p (b e)")
            link(dve.tensor_copy(lgf, bank(3, 0, B * E)))
            dve.memset(key, 0)
            dve.memset(ones32, 0xFFFFFFFF)
            for k in range(3):
                dve.memset(digit[:, k:k + 1], k + 1)
            link(dve.memset(cand, 0))

            def count(k):
                return dve.tensor_scalar(selw[:, k, :], lgf, cand[:, k:k + 1].bitcast(F32), None, ALU.is_lt, ALU.add, accum_out=sel[:, k:k + 1])

            def round_start(n):
                w = 3 if 0 < n < ROUNDS - 1 else 1
                if n:
                    link(dve.scalar_tensor_tensor(out=cand[:, 0:w], in0=digit[:, 0:w], scalar=SHIFT[n], in1=key.to_broadcast([P, w]),
                                                  op0=ALU.logical_shift_left, op1=ALU.bitwise_xor))
                for k in range(w):
                    ins = count(k)
                ins.then_inc(S["count_ready"], 1)

            def round_end(n):
                dve.wait_ge(S["count_all"], n + 1)
                if n == 0:
                    link(ts(sel[:, 4:5], bank(7, 0, 1), KTH - 1.0, None, ALU.is_gt))
                    link(dve.copy_predicated(key, sel[:, 4:5].bitcast(U32), ones32))
                    return
                w = 1 if n == ROUNDS - 1 else 3
                link(dve.tensor_scalar(sel[:, 8:8 + w], bank(7, 0, w), KTH - 1.0, None, ALU.is_le, ALU.add, accum_out=sel[:, 4:5]))
                link(ts(step, sel[:, 4:5], float(1 << SHIFT[n]), None, ALU.mult))
                link(dve.tensor_tensor(key, key, step, ALU.bitwise_xor))

            def gates():
                link(dve.scalar_tensor_tensor(out=gts, in0=lg, scalar=key.bitcast(F32), in1=lg, op0=ALU.is_ge, op1=ALU.mult))
                ts(gts, gts, tg[:, 3:4], None, ALU.mult).then_inc(S["gates_ready"], 1)

            def parts(blk, e):
                search = isinstance(blk, int) and blk < NS
                for c in range(NC):
                    dve.wait_ge(S["h_gelu"], blk * (E * NC) + (e * NC + c + 5))
                    if c == 0:
                        dve.wait_ge(S["y_ready"], blk * E + (e + 1))
                    dve.tensor_copy(hh[:, e % 2, c, :], hf[:, c, :]).then_inc(S["h_high"], 1)
                    if e == 0 and not search and c == 1:
                        dve.wait_ge(S["h_gelu"], blk * (E * NC) + (NC + 4))
                    if not search and c % 2:
                        dve.wait_ge(S["h_high"], blk * (E * NC) + (e * NC + c + 1))
                        dve.tensor_tensor(hl[:, e % 2, c, :], hf[:, c, :], hh[:, e % 2, c, :], ALU.subtract).then_inc(S["h_low_odd"], 1)
                if search:
                    round_end(blk * E + e)
                    round_start(blk * E + e + 1)

            def gated_sum(blk, e):
                dve.wait_ge(S["y_ready"], blk * E + (e + 3))
                dve.wait_ge(S["y_added"], blk * E + (e + 2))
                for k in range(4):
                    row = xs[:].rearrange("p b d -> p (b d)")[:, bass.ds(blk * 512 + k * P, P)]
                    gate = gts.rearrange("p b e -> p (b e)")[:, bass.ds(blk * (4 * E) + (k * E + e), 1)]
                    ins = dve.scalar_tensor_tensor(out=row, in0=bank(4 + e % 2, P * k, P * k + P), scalar=gate, in1=row,
                                                   op0=ALU.mult, op1=ALU.add)
                ins.then_inc(S["y_added"], 1)

            def late_sum(blk, e):
                for k in range(4):
                    if e:
                        dve.wait_ge(S["late_added"], blk * (4 * E) + (4 * (e - 1) + k + 1 - 4 * E * NS))
                    row = xs[:].rearrange("p b d -> p (b d)")[:, bass.ds(blk * 512 + (k * P - 512 * NS), P)]
                    gate = gts.rearrange("p b e -> p (b e)")[:, bass.ds(blk * (4 * E) + (k * E + e - 4 * E * NS), 1)]
                    kept = ykept[:, bass.ds(blk * (512 * E) + (e * 512 + k * P - 512 * E * NS), P)]
                    dve.scalar_tensor_tensor(out=row, in0=kept, scalar=gate, in1=row,
                                             op0=ALU.mult, op1=ALU.add).then_inc(S["late_added"], 1)

            def bias_sum(blk):
                rows = slice(512 * blk, 512 * blk + 512) if isinstance(blk, int) else bass.ds(blk * 512, 512)
                row = xs[:].rearrange("p b d -> p (b d)")[:, rows]
                return dve.tensor_tensor(row, row, gbias[:, rows], ALU.add)

            round_start(0)
            for blk in range(NS):
                for e in range(E):
                    parts(blk, e)
            parts(NS, 0)
            round_end(ROUNDS - 1)
            gates()
            dve.wait_ge(S["gates_ready"], 1)
            with dve.Fori(NS, 2 * NS) as blk:
                for e in range(1, E):
                    late_sum(blk, e - 1)
                    parts(blk, e)
                    gated_sum(blk, e - 1)
                late_sum(blk, E - 1)
                parts(blk + 1, 0)
                gated_sum(blk, E - 1)
            dve.wait_ge(S["gb_kept"], G4)
            dve.wait_ge(S["late_added"], 4 * E * NS)
            dve.wait_ge(S["y_added"], 2 * NS * E + 2)
            for blk in range(2 * NS):
                bias_sum(blk).then_inc(S["bias_added"], 1)
            with dve.Fori(2 * NS, G4 - 1) as blk:
                bias_sum(blk).then_inc(S["bias_added"], 1)
                dve.wait_ge(S["bias_added"], blk + 1)
                for e in range(1, E):
                    parts(blk, e)
                    gated_sum(blk, e - 1)
                parts(blk + 1, 0)
                gated_sum(blk, E - 1)
            bias_sum(G4 - 1).then_inc(S["bias_added"], 1)
            dve.wait_ge(S["bias_added"], G4)
            for e in range(1, E):
                parts(G4 - 1, e)
                gated_sum(G4 - 1, e - 1)
            gated_sum(G4 - 1, E - 1)

        @block.tensor
        def _(pe):
            def keep_warm(n, products):
                for _ in range(products):
                    pe.matmul(bank(n), identb[:], rep(neg[:], 4), start=True, stop=True)

            def spread(n):
                pe.wait_ge(S["mm_ready"], n + 1)
                pe.transpose(PS[0:2, 7, 0:P], mm[:, 0:2], identf[:]).then_inc(S["mm_turned"], 1)
                pe.wait_ge(S["mm_global"], n + 1)
                pe.matmul(bank(7, P, P + 2), ones[0:2, :], gq[0:2, 2:4], start=True, stop=True).then_inc(S["mm_spread"], 1)

            pe.sem_inc(S["sc_ready"], 4)
            pe.sem_inc(S["av_done"], 2)
            pe.sem_inc(S["y_ready"], 2)
            pe.wait_ge(S["consts_made"], 1)
            pe.wait_ge(S["small_in"], 16 * 9)
            for k in range(3):
                pe.transpose(bank(6, 16 * k, 16 * k + 16), ifw_n[:, P * k:P * k + P], identf[0:16, 0:16])
            pe.transpose(bank(6, 48, 80), mb1_n, identf[0:32, 0:32])
            pe.transpose(bank(6, 80, 84), ab1_n, identf[0:4, 0:4])
            pe.transpose(bank(6, 84, 92), gw_n, identf[0:8, 0:8]).then_inc(S["small_turned"], 1)
            def gate_sums(o, tokens, w, g):
                for b in range(4 * g, 4 * g + 4):
                    ins = pe.matmul(bank(o, 16 * b, 16 * b + 16), tokens[:, P * b:P * b + P], w, start=True, stop=True)
                return ins

            for g in range(G4 + 1):
                if g < G4:
                    if g % 2 == 0:
                        pe.wait_ge(ctx_in[g // 2], 16)
                    if g >= 2:
                        pe.wait_ge(S["k_kept"], g - 1)
                    for k in range(4):
                        ins = pe.transpose(bank(2 + g % 2, P * k, P * k + P), cs[:, 4 * g + k, :], identf[:])
                    ins.then_inc(S["c_turned"], 1)
                if g >= 1:
                    if g == 1:
                        pe.wait_ge(S["small_kept"], 1)
                    pe.wait_ge(S["k_kept"], g)
                    ins = gate_sums(5, kT, wkv[:], g - 1)
            ins.then_inc(S["gates_summed"], 1)
            for g in range(G4 + 1):
                if g < G4:
                    pe.wait_ge(S["ln_done"], g + 1)
                    if g >= 2:
                        pe.wait_ge(S["q_kept"], g - 1)
                    for k in range(4):
                        ins = pe.transpose(bank(g % 2, P * k, P * k + P), xn[:, 4 * g + k, :], identf[:])
                    ins.then_inc(S["q_turned"], 1)
                if g >= 1:
                    pe.wait_ge(S["q_kept"], g)
                    ins = gate_sums(4, qT, small_t[:, 0:16], g - 1)
            ins.then_inc(S["gates_summed"], 1)
            spread(0)
            pe.wait_ge(S["nlf_ready"], 1)
            pe.matmul(bank(5, 0, B * NH), tri[:], nlf.rearrange("p b h -> p (b h)"), start=True, stop=True).then_inc(S["cumsum_done"], 1)
            pe.wait_ge(S["a_ready"], 1)
            for j in range(2):
                for g in range(4):
                    ins = pe.transpose(bank(j, P * g, P * g + P), A[:, 12288 + P * (4 * j + g):12288 + P * (4 * j + g + 1)], identf[:])
                ins.then_inc(S["a_turned"], 1)
            for j in range(2):
                pe.wait_ge(S["m_ready"], 4 * (j + 1))
                for g in range(4):
                    ins = pe.transpose(bank(2 + j, P * g, P * g + P), av[:, 1, 4 * j + g, :], identf[:])
                ins.then_inc(S["m_turned"], 1)
            pe.wait_ge(S["scale_ready"], 1)
            keep_warm(7, 16)
            pe.wait_ge(S["m_tok_ready"], 1)
            pe.wait_ge(S["mblk_ready"], 1)
            pe.wait_ge(S["part_ready"], 1)
            pe.wait_ge(S["vaug_ready"], 1)
            def weigh(g, m):
                pe.wait_ge(S["s_low"], g * 8 + (m + 3))
                pe.wait_ge(S["o_kept"], g * 8 + (m + 1))
                half = m % 2
                v6h, v6l = (v[:, bass.ds(g * 4 + m // 2, 1), 2 * VW * half:2 * VW * half + 6 * VW].rearrange("p b w -> p (b w)")
                            for v in (vh, vl))
                for j in range(4):
                    o = bank(6 + half, 6 * VW * j, 6 * VW * (j + 1))
                    w = slice(P * j, P * j + P)
                    pe.matmul(o, sh[:, half, w], v6h, start=True, stop=False)
                    pe.matmul(o, sh[:, half, w], v6l, start=False, stop=False)
                    ins = pe.matmul(o, sl[:, half, w], v6h, start=False, stop=True)
                ins.then_inc(S["av_done"], 1)

            def units(g, first=False):
                for m in range(8):
                    k, half = m // 2, m % 2
                    pe.wait_ge(S["exp_done"], g * 8 + (m + 1))
                    mb = mblk.rearrange("p g h t -> p (g h t)")[:, bass.ds(g * 1024 + 512 * half, 512)]
                    pe.matmul(bank(half), selb[:, k, :], mb, start=True, stop=False)
                    pe.matmul(bank(half), av_part[:, 0].rearrange("p g t -> p (g t)")[:, bass.ds(g * P, P)],
                              bmask[:, k, 4 * half:4 * half + 4, :].rearrange("p h t -> p (h t)"), start=False, stop=False)
                    pe.matmul(bank(half), identb[:], rep(neg[:], 4), start=False, stop=True).then_inc(S["ld_ready"], 1)
                    pe.wait_ge(S["prod_done"], g * 8 + (m + 1))
                    if half == 0:
                        pe.wait_ge(S["kslot_ready"], g * 4 + (k + 1))
                        pe.wait_ge(S["qslot_ready"], g * 4 + (k + 1))
                    for jj in range(2):
                        r = slice(64 * half + 32 * jj, 64 * half + 32 * jj + 32)
                        ins = pe.matmul(PS[:, 2 + 2 * half + jj, 0:256], kslot[r, k % 2, :], qslot[r, k % 2],
                                        start=True, stop=True)
                    ins.then_inc(S["sc_ready"], 1)
                    if m >= 2 or not first:
                        weigh(g, m - 2)

            units(0, first=True)
            with pe.Fori(1, G4) as g:
                units(g)
            weigh(G4, -2)
            weigh(G4, -1)
            pe.wait_ge(S["wq_ready"], 1)
            pe.wait_ge(S["o_kept"], 2 * B + 2)
            for n in range(2):
                for c in range(NC):
                    w = slice(HID * n + P * c, HID * n + P * c + P)
                    ins = pe.transpose(bankb(5 + n)[:, P * c:P * c + P], wqb[:, w], identb[:])
                ins.then_inc(S["wq_turned"], 1)
            spread(1)
            for nb in range(G4):
                pe.wait_ge(S["xq_ready"], nb // 2 + 1)
                if nb >= 2:
                    pe.wait_ge(S["xqT_kept"], nb - 1)
                for k in range(4):
                    b = 4 * nb + k
                    ins = pe.transpose(bankb(nb % 2)[:, P * k:P * k + P], xq[:, P * b:P * b + P], identb[:])
                ins.then_inc(S["xq_turned"], 1)
                pe.wait_ge(S["xqT_kept"], nb + 1)
                pe.wait_ge(S["wq_kept"], 2)
                for c in range(NC):
                    if nb >= 1:
                        pe.wait_ge(S["gelu_done"], NC * (nb - 1) + c + 1)
                    pe.matmul(bank(2 + c), w1q[:, P * c:P * c + P], xqT[:, 512 * nb:512 * nb + 512], start=True, stop=True).then_inc(S["ffn1_done"], 1)
            spread(2)
            for nb in range(G4):
                pe.wait_ge(S["hq_ready"], nb + 1)
                if nb >= 2:
                    pe.wait_ge(S["ffn2_added"], nb - 1)
                for k in range(4):
                    for c in range(NC):
                        t0 = 512 * nb + P * k
                        ins = pe.matmul(bank(nb % 2, P * k, P * k + P), hq[:, c, t0:t0 + P], w2q[:, c, :], start=(c == 0), stop=(c == NC - 1))
                ins.then_inc(S["ffn2_done"], 1)
            def turn_x3(g):
                if g < 2:
                    pe.wait_ge(S["ffn2_added"], G4 - 1 + g)
                pe.wait_ge(S["ln_done"], 2 * G4 - 4 + g + 1)
                if g >= 2:
                    pe.wait_ge(S["x3T_kept"], g - 1)
                for k in range(4):
                    ins = pe.transpose(bank(g % 2, P * k, P * k + P), xn[:, 4 * g + k, :], identf[:])
                ins.then_inc(S["x3T_turned"], 1)

            def squared_distances(g):
                pe.wait_ge(S["x3T_kept"], g + 1)
                if g >= 2:
                    pe.wait_ge(S["dsq_ready"], g - 1)
                pe.matmul(bank(2 + g % 2), ones[:], xTsq[:, g % 2, :], start=True, stop=False)
                for k in range(4):
                    b = 4 * g + k
                    ins = pe.matmul(bank(2 + g % 2, P * k, P * k + P), kT[:, P * b:P * b + P], xT2[:, g % 2, P * k:P * k + P],
                                    start=False, stop=(k == 3))
                ins.then_inc(S["dsum_done"], 1)

            turn_x3(0)
            for g in range(1, G4 + 1):
                if g < G4:
                    turn_x3(g)
                squared_distances(g - 1)
            for n in range(2 * E):
                pe.wait_ge(raw_in[n % 2], 16 * (n // 2 + 1))
                if n >= 2:
                    pe.wait_ge(S["raw_kept"], n - 1)
                for c in range(NC):
                    ins = pe.transpose(bank(4 + n % 2, P * c, P * c + P), wraw[:, n % 2, P * c:P * c + P], identf[:])
                ins.then_inc(S["raw_turned"], 1)
            pe.wait_ge(S["track_done"], P)
            pe.transpose(bank(0, 0, B), ee[:, 0:P], identf[0:B, 0:B])
            pe.transpose(bank(0, B, 2 * B), ee[:, 1:P + 1], identf[0:B, 0:B]).then_inc(S["e_turned"], 1)
            for g in range(G4):
                pe.wait_ge(S["path_ready"], g + 1)
                if g >= 2:
                    pe.wait_ge(S["expanded_added"], g - 1)
                for k in range(4):
                    b = 4 * g + k
                    ins = pe.matmul(bank(1 + g % 2, P * k, P * k + P), path[:, b, :], cs[:, b, :], start=True, stop=True)
                ins.then_inc(S["expanded"], 1)
            for g in range(G4 + 1):
                if g < G4:
                    pe.wait_ge(S["ln_done"], 3 * G4 - 4 + g + 1)
                    if g >= 2:
                        pe.wait_ge(S["x4_kept"], g - 1)
                    for k in range(4):
                        ins = pe.transpose(bank(6 + g % 2, P * k, P * k + P), x4[:, 4 * g + k, :], identf[:])
                    ins.then_inc(S["x4_turned"], 1)
                if g >= 1:
                    pe.wait_ge(S["x4_kept"], g)
                    for k in range(4):
                        b = 4 * (g - 1) + k
                        ins = pe.matmul(bank(3, E * b, E * b + E), x4f[:, (g - 1) % 2, P * k:P * k + P], small_t[:, 84:92], start=True, stop=True)
                    ins.then_inc(S["logits_done"], 1)
            pe.wait_ge(S["x4_split"], G4)
            pe.wait_ge(S["w_split"], 2 * E)

            def hidden(blk, e):
                xw = slice(512 * blk, 512 * blk + 512) if isinstance(blk, int) else bass.ds(blk * 512, 512)
                for c in range(NC):
                    pe.wait_ge(S["h_gelu"], blk * (E * NC) + (e * NC + c + 1))
                    pe.matmul(bank(c), w1h[:, e, c, :], x4h[:, xw], start=True, stop=False)
                    pe.matmul(bank(c), w1h[:, e, c, :], x4l[:, xw], start=False, stop=False)
                    pe.matmul(bank(c), w1l[:, e, c, :], x4h[:, xw], start=False, stop=True).then_inc(S["h_ready"], 1)
                    if isinstance(blk, int) and blk * E + e < ROUNDS and c == (1 if blk or e else 2):
                        counts(blk * E + e)

            def outputs(blk, e):
                pe.wait_ge(S["y_added"], blk * E + (e + 1))
                for c in range(NC):
                    pe.wait_ge(S["h_low_even" if c % 2 == 0 else "h_low_odd"], blk * (2 * E) + (2 * e + c // 2 + 3))
                    for k in range(4):
                        o = bank(4 + e % 2, P * k, P * k + P)
                        t = slice(P * k, P * k + P)
                        pe.matmul(o, hh[:, e % 2, c, t], w2h[:, e, c, :], start=(c == 0 and k == 0), stop=False, skip_group_check=True)
                        pe.matmul(o, hh[:, e % 2, c, t], w2l[:, e, c, :], start=False, stop=False, skip_group_check=True)
                        ins = pe.matmul(o, hl[:, e % 2, c, t], w2h[:, e, c, :], start=False, stop=(c == NC - 1), skip_group_check=True)
                ins.then_inc(S["y_ready"], 1)

            def counts(n):
                w = 1 if n in (0, ROUNDS - 1) else 3
                pe.wait_ge(S["count_ready"], n + 1)
                pe.matmul(bank(7, 0, w), ones[:], sel[:, 0:w], start=True, stop=True).then_inc(S["count_all"], 1)

            def gated_bias(e):
                if e - 1 < G4:
                    if e >= 2:
                        pe.wait_ge(S["gt_kept"], e - 1)
                    pe.transpose(PS[0:32, 6, 0:P], gts[:, 4 * e - 4:4 * e, :].rearrange("p b e -> p (b e)"), identf[:]).then_inc(S["gt_turned"], 1)
                if e >= 2:
                    if e >= 3:
                        pe.wait_ge(S["gb_kept"], e - 2)
                    pe.matmul(bank(7), gtT[:, (e - 2) % 2, :], b2blk[:].rearrange("p k d -> p (k d)"), start=True, stop=True).then_inc(S["gb_done"], 1)

            hidden(0, 0)
            for blk in range(NS):
                for e in range(1, E):
                    hidden(blk, e)
                    outputs(blk, e - 1)
                hidden(blk + 1, 0)
                outputs(blk, E - 1)
            for e in range(1, E + 2):
                if e < E:
                    hidden(NS, e)
                if e == 1:
                    pe.wait_ge(S["gates_ready"], 1)
                    pe.wait_ge(S["b2_in"], 64)
                gated_bias(e)
                if e < E:
                    outputs(NS, e - 1)
            hidden(NS + 1, 0)
            outputs(NS, E - 1)
            with pe.Fori(NS + 1, G4 - 1) as blk:
                for e in range(1, E):
                    hidden(blk, e)
                    outputs(blk, e - 1)
                hidden(blk + 1, 0)
                outputs(blk, E - 1)
            for e in range(1, E):
                hidden(G4 - 1, e)
                outputs(G4 - 1, e - 1)
            outputs(G4 - 1, E - 1)


_INS = ['x', 'ctx_1024', 'g_xattn', 'g_ffn', 'L0_xattn_ifgate_w', 'L0_xattn_ifgate_b', 'L0_xattn_outnorm_w', 'L0_ffn_W1',
        'L0_ffn_b1', 'L0_ffn_W2', 'L0_ffn_b2', 'L1_ffn_gate_weight', 'L1_ffn_w1', 'L1_ffn_b1', 'L1_ffn_w2', 'L1_ffn_b2']
_OUTS = [((32, 128, 128), 'float32')]


def kernel(**inputs):
    import numpy as _np
    import concourse.bacc as _bacc
    from concourse import mybir as _mybir
    from concourse.bass_utils import run_bass_kernel_spmd as _run

    nc = _bacc.Bacc("TRN2", target_bir_lowering=False, num_devices=1)
    arrays, args = {}, []
    for name in _INS:
        a = _np.ascontiguousarray(inputs[name])
        arrays[f"in_{name}_dram"] = a
        args.append(nc.dram_tensor(f"in_{name}_dram", a.shape, _mybir.dt.from_np(a.dtype), kind="ExternalInput").ap())
    for i, (shape, dtype) in enumerate(_OUTS):
        dt = _mybir.dt.from_np(_np.dtype(dtype))
        args.append(nc.dram_tensor(f"out_{i}_dram", shape, dt, kind="ExternalOutput").ap())
    program(nc, *args)
    r = _run(nc, [arrays], core_ids=[0])
    got = tuple(r.results[0][f"out_{i}_dram"] for i in range(len(_OUTS)))
    return got[0]
```
